# Optimizing a Trainium2 kernel written in Bass

```python
import numpy as np
import jax
import jax.numpy as jnp

def _softmax(x, axis=-1):
    return jax.nn.softmax(x, axis=axis)

def _gelu(x):
    return jax.nn.gelu(x, approximate=True)

def _silu(x):
    return jax.nn.silu(x)

def _sigmoid(x):
    return jax.nn.sigmoid(x)

def _layernorm(x, axis=-1, eps=1e-05):
    m = jnp.mean(x, axis=axis, keepdims=True)
    v = jnp.var(x, axis=axis, keepdims=True)
    return (x - m) / jnp.sqrt(v + eps)

def _scatter_add(tgt, idx, src, axis=0):
    return tgt.at[idx].add(src)

def _segment_sum(src, seg, n):
    return jax.ops.segment_sum(src, seg, n)
kernel_name = 'mk_decoder_postln_d1_seqx_r8_82f4a5'

def setup_inputs(seed: int=0):
    np.random.seed(seed)
    _w = jnp.asarray

    def _rec_inputs():
        import jax
        import jax.numpy as jnp
        _rk = jax.random.key(seed)
        x = -0.0003929 + 0.9999 * jax.random.normal(jax.random.fold_in(_rk, 1), (16, 64, 512), jnp.float32)
        _lenS = 64 - jax.random.randint(jax.random.fold_in(_rk, 7), (16,), 0, max(1, 64 // 4) + 1, jnp.int32)
        _lenS2 = 64 - jax.random.randint(jax.random.fold_in(_rk, 8), (16,), 0, max(1, 64 // 4) + 1, jnp.int32)
        _ctx_4096P = jax.random.normal(jax.random.fold_in(_rk, 11), (16, 16, 512), jnp.float32)
        _ctx_4096c = jax.random.dirichlet(jax.random.fold_in(_rk, 511), 0.3 * jnp.ones((16,), jnp.float32), (16, 64))
        _ctx_4096t = jnp.einsum('bsk,bkd->bsd', _ctx_4096c, _ctx_4096P)
        _ctx_4096t = _ctx_4096t * jax.lax.rsqrt(jnp.mean(jnp.square(_ctx_4096t)) + 1e-12) * 0.953939
        ctx_4096 = 2.81802e-05 + 1.00001 * (_ctx_4096t + 0.3 * jax.random.normal(jax.random.fold_in(_rk, 611), (16, 64, 512), jnp.float32))
        pos_BxS2 = jnp.broadcast_to(jnp.arange(64, dtype=jnp.int32), (16, 64))
        _validS = jnp.arange(64)[None, :] < _lenS[:, None]
        _validS2 = jnp.arange(64)[None, :] < _lenS2[:, None]
        _causal = jnp.tril(jnp.ones((64, 64), dtype=bool))
        mask_BxSxS2_ik0 = jnp.where(jnp.broadcast_to(_validS2[:, None, :], (16, 64, 64)), 0, 1).astype(jnp.int32)
        return (x, ctx_4096, pos_BxS2, mask_BxSxS2_ik0)
    x, ctx_4096, pos_BxS2, mask_BxSxS2_ik0 = _rec_inputs()

    def _L0_attn_setup():
        import jax, jax.numpy as jnp
        import numpy as np
        import math
        DIM = 512
        N_HEADS = 32
        N_KV_HEADS = 8
        HEAD_DIM = DIM // N_HEADS
        N_REP = N_HEADS // N_KV_HEADS
        ROPE_BASE = 10000.0

        def apply_rotary_emb(x):
            b, s, h, d = x.shape
            inv_freq = 1.0 / ROPE_BASE ** (jnp.arange(0, d, 2, dtype=jnp.float32) / d)
            pos = jnp.arange(s, dtype=jnp.float32)
            ang = pos[:, None] * inv_freq[None, :]
            cos = jnp.cos(ang)[None, :, None, :]
            sin = jnp.sin(ang)[None, :, None, :]
            xr = x.reshape(b, s, h, d // 2, 2)
            x0, x1 = (xr[..., 0], xr[..., 1])
            out = jnp.stack([x0 * cos - x1 * sin, x0 * sin + x1 * cos], axis=-1)
            return out.reshape(b, s, h, d)
        key = jax.random.key(seed)
        ks = jax.random.split(key, 5)
        sc = 1.0 / math.sqrt(DIM)
        return {'x': jax.random.normal(ks[0], (2, 256, DIM), dtype=jnp.float32), 'Wq': jax.random.normal(ks[1], (DIM, N_HEADS * HEAD_DIM), dtype=jnp.float32) * sc, 'Wk': jax.random.normal(ks[2], (DIM, N_KV_HEADS * HEAD_DIM), dtype=jnp.float32) * sc, 'Wv': jax.random.normal(ks[3], (DIM, N_KV_HEADS * HEAD_DIM), dtype=jnp.float32) * sc, 'Wo': jax.random.normal(ks[4], (N_HEADS * HEAD_DIM, DIM), dtype=jnp.float32) * sc}
    _L0_attn_all = _L0_attn_setup()
    _L0_attn_in = {k: v for k, v in _L0_attn_all.items() if k in ('Wq', 'Wk', 'Wv', 'Wo')}
    del _L0_attn_all

    def _L0_xattn_setup():
        import jax, jax.numpy as jnp
        import numpy as np
        B, S, E = (2, 256, 512)
        H, KVH, D = (32, 8, 128)
        GROUPS = H // KVH
        MAX_POS = 512
        ROPE_THETA = 10000.0

        def _rope_tables(max_pos, dim, theta):
            inv_freq = 1.0 / theta ** (jnp.arange(0, dim, 2, dtype=jnp.float32) / dim)
            t = jnp.arange(max_pos, dtype=jnp.float32)
            freqs = jnp.einsum('i,j->ij', t, inv_freq)
            emb = jnp.concatenate([freqs, freqs], axis=-1)
            return (jnp.cos(emb), jnp.sin(emb))

        def _rotate_half(x):
            x1, x2 = (x[..., :x.shape[-1] // 2], x[..., x.shape[-1] // 2:])
            return jnp.concatenate([-x2, x1], axis=-1)
        key = jax.random.key(seed)
        ks = jax.random.split(key, 8)
        scale_w = 1.0 / np.sqrt(E)
        query = jax.random.normal(ks[0], (B, S, E), dtype=jnp.float32)
        k_in = jax.random.normal(ks[1], (B, S, E), dtype=jnp.float32)
        v_in = jax.random.normal(ks[2], (B, S, E), dtype=jnp.float32)
        position_ids = jnp.broadcast_to(jnp.arange(S, dtype=jnp.int64), (B, S))
        src_mask = jnp.tril(jnp.ones((S, S), dtype=jnp.int32))
        src_mask = jnp.broadcast_to(src_mask, (B, S, S))
        Wq = jax.random.normal(ks[3], (E, H * D), dtype=jnp.float32) * scale_w
        Wk = jax.random.normal(ks[4], (E, KVH * D), dtype=jnp.float32) * scale_w
        Wv = jax.random.normal(ks[5], (E, KVH * D), dtype=jnp.float32) * scale_w
        Wo = jax.random.normal(ks[6], (H * D, E), dtype=jnp.float32) * scale_w
        return {'query': query, 'key': k_in, 'value': v_in, 'position_ids': position_ids, 'src_mask': src_mask, 'Wq': Wq, 'Wk': Wk, 'Wv': Wv, 'Wo': Wo}
    _L0_xattn_all = _L0_xattn_setup()
    _L0_xattn_in = {k: v for k, v in _L0_xattn_all.items() if k in ('Wq', 'Wk', 'Wv', 'Wo')}
    del _L0_xattn_all

    def _L0_ffn_setup():
        import jax, jax.numpy as jnp
        import numpy as np
        IN_F = 512
        OUT_F = 512
        N_CLUSTERS = 64
        THRESHOLD = 0.01
        TEMPERATURE = 0.1
        BATCH, SEQ = (4, 256)
        key = jax.random.key(seed)
        k1, k2, k3, k4, k5 = jax.random.split(key, 5)
        s = 1.0 / np.sqrt(IN_F)
        return {'input': jax.random.normal(k1, (BATCH, SEQ, IN_F), dtype=jnp.float32), 'weight': jax.random.normal(k2, (OUT_F, IN_F), dtype=jnp.float32) * s, 'bias': jax.random.uniform(k3, (OUT_F,), dtype=jnp.float32, minval=-s, maxval=s), 'centroids': jax.random.normal(k4, (N_CLUSTERS, IN_F), dtype=jnp.float32) * s, 'assignments': jax.random.randint(k5, (OUT_F,), 0, N_CLUSTERS, dtype=jnp.int32)}
    _L0_ffn_all = _L0_ffn_setup()
    _L0_ffn_in = {k: v for k, v in _L0_ffn_all.items() if k in ('weight', 'bias', 'centroids', 'assignments')}
    del _L0_ffn_all
    return {'x': x, 'ctx_4096': ctx_4096, 'pos_BxS2': pos_BxS2, 'mask_BxSxS2_ik0': mask_BxSxS2_ik0, 'L0_attn_Wq': _L0_attn_in['Wq'], 'L0_attn_Wk': _L0_attn_in['Wk'], 'L0_attn_Wv': _L0_attn_in['Wv'], 'L0_attn_Wo': _L0_attn_in['Wo'], 'L0_xattn_Wq': _L0_xattn_in['Wq'], 'L0_xattn_Wk': _L0_xattn_in['Wk'], 'L0_xattn_Wv': _L0_xattn_in['Wv'], 'L0_xattn_Wo': _L0_xattn_in['Wo'], 'L0_ffn_weight': _L0_ffn_in['weight'], 'L0_ffn_bias': _L0_ffn_in['bias'], 'L0_ffn_centroids': _L0_ffn_in['centroids'], 'L0_ffn_assignments': _L0_ffn_in['assignments']}

def reference(x, ctx_4096, pos_BxS2, mask_BxSxS2_ik0, L0_attn_Wq, L0_attn_Wk, L0_attn_Wv, L0_attn_Wo, L0_xattn_Wq, L0_xattn_Wk, L0_xattn_Wv, L0_xattn_Wo, L0_ffn_weight, L0_ffn_bias, L0_ffn_centroids, L0_ffn_assignments):
    import jax
    import jax.numpy as jnp

    def _L0_attn_ref(x, Wq, Wk, Wv, Wo):
        import jax, jax.numpy as jnp
        import numpy as np
        import math
        DIM = 512
        N_HEADS = 32
        N_KV_HEADS = 8
        HEAD_DIM = DIM // N_HEADS
        N_REP = N_HEADS // N_KV_HEADS
        ROPE_BASE = 10000.0

        def apply_rotary_emb(x):
            b, s, h, d = x.shape
            inv_freq = 1.0 / ROPE_BASE ** (jnp.arange(0, d, 2, dtype=jnp.float32) / d)
            pos = jnp.arange(s, dtype=jnp.float32)
            ang = pos[:, None] * inv_freq[None, :]
            cos = jnp.cos(ang)[None, :, None, :]
            sin = jnp.sin(ang)[None, :, None, :]
            xr = x.reshape(b, s, h, d // 2, 2)
            x0, x1 = (xr[..., 0], xr[..., 1])
            out = jnp.stack([x0 * cos - x1 * sin, x0 * sin + x1 * cos], axis=-1)
            return out.reshape(b, s, h, d)
        b, s, _ = x.shape
        xq = (x @ Wq).reshape(b, s, N_HEADS, HEAD_DIM)
        xk = (x @ Wk).reshape(b, s, N_KV_HEADS, HEAD_DIM)
        xv = (x @ Wv).reshape(b, s, N_KV_HEADS, HEAD_DIM)
        xq = apply_rotary_emb(xq)
        xk = apply_rotary_emb(xk)
        xk = jnp.repeat(xk, N_REP, axis=2)
        xv = jnp.repeat(xv, N_REP, axis=2)
        scores = jnp.einsum('bqhd,bkhd->bhqk', xq, xk) / math.sqrt(HEAD_DIM)
        causal = jnp.tril(jnp.ones((s, s), dtype=bool))
        scores = jnp.where(causal[None, None], scores, -jnp.inf)
        probs = jax.nn.softmax(scores.astype(jnp.float32), axis=-1).astype(xq.dtype)
        out = jnp.einsum('bhqk,bkhd->bqhd', probs, xv).reshape(b, s, N_HEADS * HEAD_DIM)
        return out @ Wo

    def _L0_xattn_ref(query, key, value, position_ids, src_mask, Wq, Wk, Wv, Wo):
        import jax, jax.numpy as jnp
        import numpy as np
        B, S, E = (2, 256, 512)
        H, KVH, D = (32, 8, 128)
        GROUPS = H // KVH
        MAX_POS = 512
        ROPE_THETA = 10000.0

        def _rope_tables(max_pos, dim, theta):
            inv_freq = 1.0 / theta ** (jnp.arange(0, dim, 2, dtype=jnp.float32) / dim)
            t = jnp.arange(max_pos, dtype=jnp.float32)
            freqs = jnp.einsum('i,j->ij', t, inv_freq)
            emb = jnp.concatenate([freqs, freqs], axis=-1)
            return (jnp.cos(emb), jnp.sin(emb))

        def _rotate_half(x):
            x1, x2 = (x[..., :x.shape[-1] // 2], x[..., x.shape[-1] // 2:])
            return jnp.concatenate([-x2, x1], axis=-1)
        nb, q_len, _ = query.shape
        q = (query @ Wq).reshape(nb, q_len, H, D).transpose(0, 2, 1, 3)
        k = (key @ Wk).reshape(nb, q_len, KVH, D).transpose(0, 2, 1, 3)
        v = (value @ Wv).reshape(nb, q_len, KVH, D).transpose(0, 2, 1, 3)
        cos_t, sin_t = _rope_tables(MAX_POS, D, ROPE_THETA)
        cos = cos_t[position_ids][:, None]
        sin = sin_t[position_ids][:, None]
        q = q * cos + _rotate_half(q) * sin
        k = k * cos + _rotate_half(k) * sin
        k = jnp.repeat(k, GROUPS, axis=1)
        v = jnp.repeat(v, GROUPS, axis=1)
        scores = jnp.einsum('bhqd,bhkd->bhqk', q, k) / jnp.sqrt(jnp.float32(D))
        mask = src_mask[:, None]
        scores = jnp.where(mask == 0, jnp.float32(-1000000000.0), scores)
        attn = jax.nn.softmax(scores, axis=-1)
        x = jnp.einsum('bhqk,bhkd->bhqd', attn, v)
        x = x.transpose(0, 2, 1, 3).reshape(nb, q_len, H * D)
        return x @ Wo

    def _L0_ffn_ref(input, weight, bias, centroids, assignments):
        import jax, jax.numpy as jnp
        import numpy as np
        IN_F = 512
        OUT_F = 512
        N_CLUSTERS = 64
        THRESHOLD = 0.01
        TEMPERATURE = 0.1
        BATCH, SEQ = (4, 256)
        shape = input.shape
        x = input.reshape(-1, shape[-1])
        dots = jax.nn.softmax(x @ centroids.T / TEMPERATURE, axis=-1)
        hits = dots > THRESHOLD
        query_sel = jnp.any(hits, axis=1)
        cluster_sel = jnp.any(hits, axis=0)
        row_sel = cluster_sel[assignments]
        dense = x @ weight.T + bias
        out = jnp.where(query_sel[:, None] & row_sel[None, :], dense, jnp.zeros((), dense.dtype))
        return out.reshape(*shape[:-1], -1)
    x = _layernorm(x + _L0_attn_ref(x, L0_attn_Wq, L0_attn_Wk, L0_attn_Wv, L0_attn_Wo), axis=-1)
    x = _layernorm(x + _L0_xattn_ref(x, ctx_4096, ctx_4096, pos_BxS2, mask_BxSxS2_ik0, L0_xattn_Wq, L0_xattn_Wk, L0_xattn_Wv, L0_xattn_Wo), axis=-1)
    x = _layernorm(x + _L0_ffn_ref(x, L0_ffn_weight, L0_ffn_bias, L0_ffn_centroids, L0_ffn_assignments), axis=-1)
    return x

_drawn_inputs = setup_inputs


def setup_inputs(seed=0):
    import zlib

    import numpy as np

    out = dict(_drawn_inputs(seed))
    spreads = {}
    factors = {'L0_ffn_bias': 3.222}
    for name, (base, spread) in spreads.items():
        noise = np.random.default_rng([zlib.crc32(name.encode()), seed]).standard_normal(out[name].shape)
        drawn = base * np.exp(spread * noise) if base else spread * noise
        out[name] = jnp.asarray(drawn.astype(out[name].dtype))
    for name, factor in factors.items():
        out[name] = (out[name] * factor).astype(out[name].dtype)
    return out
```

```python
from contextlib import ExitStack

import concourse.bass as bass
from concourse import mybir

F32 = mybir.dt.float32
F32R = mybir.dt.float32r
I32 = mybir.dt.int32
ALU = mybir.AluOpType
ACT = mybir.ActivationFunctionType
AX = mybir.AxisListType

P = 128
B, S, E = 16, 64, 512
T = B * S // P
EC = E // P
H1, G1, D1 = 32, 8, 16
KV1 = G1 * D1
SCALE1 = 1.0 / D1 ** 0.5
NEG1 = -1e38
H2, G2, D2 = 32, 8, 128
HG = H2 // G2
SCALE2 = 1.0 / D2 ** 0.5
NEG2 = -1e9 * D2 ** 0.5
UN = 4
U = G2 * UN
NC = 64
THRESHOLD, INV_TEMPERATURE = 0.01, 10.0
EPS = 1e-5


def bcast(ap, axis, n):
    v = ap.unsqueeze(axis)
    shape = list(v.shape)
    shape[axis] = n
    return v.broadcast_to(shape)


def decoder_layer(nc, x, ctx_in, pos, mask, w1q, w1k, w1v, w1o, w2q, w2k, w2v, w2o,
                  fw, fbias, fcent, fassign, c_ident, c_causal, c_rope1, c_rope2, out):
    stack = ExitStack()
    with stack:
        def sb(name, n, dt=F32, p=P):
            return stack.enter_context(nc.sbuf_tensor(name, [p, n], dt))

        def sem(name):
            return stack.enter_context(nc.semaphore(name))

        arena_r = sb("arena_r", 8192 + 25088, F32R)
        arena_f = sb("arena_f", 5120 + 4096 + 1024 + 6144)
        ident = sb("ident", P)
        causal = sb("causal", S, I32)
        mask_i = sb("mask_i", B * S, I32)
        pos_i = sb("pos_i", T, I32)
        rope1 = sb("rope1", 24)
        small = sb("small", 256)

        class Carver:
            def __init__(self, arena, at):
                self.arena, self.at = arena, at

            def take(self, n):
                v = self.arena[:, self.at:self.at + n]
                self.at += n
                return v

        def parts(carver, n):
            return [carver.take(n), carver.take(n)]

        def cut(ap, **kw):
            names = list(kw)
            return ap.rearrange(f"p ({' '.join(names)}) -> p {' '.join(names)}", **kw)

        r = Carver(arena_r, 0)
        xT = [cut(v, c=EC, n=B * S) for v in parts(r, EC * B * S)]
        r1, r2, r3 = (Carver(arena_r, r.at) for _ in range(3))
        f = Carver(arena_f, 0)
        raw = f.take(5120)
        res = cut(f.take(T * E), t=T, n=E)
        cs = cut(f.take(T * P), t=T, n=P)
        f1, f2, f3 = (Carver(arena_f, f.at) for _ in range(3))

        w1 = [cut(v, c=EC, n=E + 2 * KV1) for v in parts(r1, EC * (E + 2 * KV1))]
        w1out = [cut(v, c=HG, n=E) for v in parts(r1, HG * E)]
        xt = [cut(v, c=EC, n=P) for v in parts(r1, EC * P)]
        stack_q = cut(r1.take(H1 * 64), h=H1, r=64)
        stack_k = cut(r1.take(G1 * 128), g=G1, r=128)
        qT1 = cut(r1.take(16 * P), b=2, j=16, q=S)
        kT1 = cut(r1.take(G1 * P), g=G1, n=P)
        vpad = parts(r1, G1 * (P + D1))
        pT1 = [cut(v, g=G1, a=2, n=P) for v in parts(r1, G1 * 2 * P)]
        at1 = [cut(v, a=4, b=2, q=S) for v in parts(r1, 4 * P)]
        x_st = f1.take(E)
        t1q, t2q = f1.take(E), f1.take(E)
        t1k, t2k = f1.take(KV1), f1.take(KV1)
        sc1 = [f1.take(512), f1.take(512)]
        p1 = [f1.take(512) for _ in range(4)]
        x1n = f1.take(E)
        v_raw = f1.take(KV1)
        w1_raw = cut(raw[:, 0:EC * (E + 2 * KV1)], c=EC, n=E + 2 * KV1)
        w1out_raw = cut(raw[:, EC * (E + 2 * KV1):5120], c=HG, n=E)

        cT = [cut(v, c=EC, n=B * S) for v in parts(r2, EC * B * S)]
        w2q_s = [cut(v, c=EC, n=HG * D2) for v in parts(r2, EC * HG * D2)]
        w2kv_s = [cut(v, c=EC, n=2 * D2) for v in parts(r2, EC * 2 * D2)]
        w2o_s = [cut(v, h=HG, n=E) for v in parts(r2, HG * E)]
        qT2 = [cut(v, b=4, h=HG, q=S) for v in parts(r2, HG * 2 * P)]
        kT2 = parts(r2, 2 * P)
        v2 = [[cut(v, i=2, n=D2) for v in parts(r2, 2 * D2)] for _ in range(2)]
        pT2 = [cut(v, i=2, n=2 * P) for v in parts(r2, 4 * P)]
        at2 = [cut(v, h=HG, n=2 * P) for v in parts(r2, HG * 2 * P)]
        ctx_raw = cut(f2.take(T * E), t=T, n=E)
        sc2 = [f2.take(512) for _ in range(UN)]
        f2b = Carver(arena_f, f1.at - 5504)
        u1q = [f2b.take(512), f2b.take(512)]
        u2q = [f2b.take(512), f2b.take(512)]
        u1k, u2k = f2b.take(256), f2b.take(256)
        p2 = f2b.take(512)
        w2q_raw = cut(raw[:, 0:2048], c=EC, n=512)
        w2kv_raw = cut(raw[:, 2048:3072], c=EC, n=256)
        w2o_raw = cut(raw[:, 3072:5120], h=HG, n=E)

        fwT = [cut(v, c=EC, n=E) for v in parts(r3, EC * E)]
        fcT = [cut(v, c=EC, n=NC) for v in parts(r3, EC * NC)]
        x3T = [[cut(v, c=EC, n=P) for v in parts(r3, EC * P)] for _ in range(2)]
        dense = cut(f3.take(T * E), t=T, n=E)
        x3n = [f3.take(E), f3.take(E)]
        y_out = [f3.take(E), f3.take(E)]
        fw_raw = cut(raw[:, 0:2048], c=EC, n=E)
        fc_raw = raw[0:NC, 2048:2560]
        bias_b = raw[:, 2560:3072]
        onehot = raw[0:NC, 3072:3584]
        row_sel = raw[:, 3584:4096]
        assign_f = raw[0:NC, 4096:4608]
        dots = raw[:, 4608:5120]
        assign_i = mask_i[0:NC, 0:E]
        hits = mask_i[:, E:2 * E].bitcast(F32)

        mx1 = [small[:, 8 * u:8 * u + 8] for u in range(4)]
        sm1 = [small[:, 32 + 8 * u:40 + 8 * u] for u in range(4)]
        mx2, sm2 = small[:, 64:72], small[:, 72:80]
        st6, mv, rstd, half = small[:, 80:86], small[:, 86:88], small[:, 88:89], small[:, 89:90]
        mv8, rstd8, half8, var8 = small[:, 96:112], small[:, 112:120], small[:, 120:128], small[:, 128:136]
        qsel = small[:, 136:144]
        any_hit = small[:, 144:208]
        cid = small[0:NC, 208:209]
        st6b = small[:, 216:222]

        banks = [stack.enter_context(nc.psum_tensor(f"bank{i}", [P, 512], F32)) for i in range(8)]
        cluster_hit = sb("cluster_hit", P, F32)
        ones = sb("ones", P)

        d_w1, d_w1o, d_x, d_const, d_res = sem("d_w1"), sem("d_w1o"), sem("d_x"), sem("d_const"), sem("d_res")
        d_pos, d_cs = sem("d_pos"), sem("d_cs")
        d_mask, d_ctx = sem("d_mask"), sem("d_ctx")
        d_w2q, d_w2kv, d_w2o = sem("d_w2q"), sem("d_w2kv"), sem("d_w2o")
        d_fw, d_fc, d_out = sem("d_fw"), sem("d_fc"), [sem("d_out0"), sem("d_out1")]
        s_w1h, s_w1l, s_init, s_dinit = sem("s_w1h"), sem("s_w1l"), sem("s_init"), sem("s_dinit")
        s_gate = sem("s_gate")
        s_xT, s_xh, s_xl = sem("s_xT"), sem("s_xh"), sem("s_xl")
        s_q, s_kv = sem("s_q"), sem("s_kv")
        s_rq, s_rk, s_qs, s_ks = sem("s_rq"), sem("s_rk"), sem("s_qs"), sem("s_ks")
        s_qh, s_ql, s_kh, s_kl = sem("s_qh"), sem("s_ql"), sem("s_kh"), sem("s_kl")
        s_vr, s_vh, s_vl = sem("s_vr"), sem("s_vh"), sem("s_vl")
        s_qk, s_qke = sem("s_qk"), sem("s_qke")
        s_s, s_cp, s_mx, s_sub = sem("s_s"), sem("s_cp"), sem("s_mx"), sem("s_sub")
        s_ex, s_sum, s_rc, s_pn = sem("s_ex"), sem("s_sum"), sem("s_rc"), sem("s_pn")
        s_pt, s_ph, s_pl = sem("s_pt"), sem("s_ph"), sem("s_pl")
        s_pv, s_ah, s_al, s_wo = sem("s_pv"), sem("s_ah"), sem("s_al"), sem("s_wo")
        s_res, s_ln, s_lp, s_x1n = sem("s_res"), sem("s_ln"), sem("s_lp"), sem("s_x1n")
        s_x1c, s_x1T, s_x1h, s_x1l = sem("s_x1c"), sem("s_x1T"), sem("s_x1h"), sem("s_x1l")
        c_init, c_xT, c_xh, c_xl = sem("c_init"), sem("c_xT"), sem("c_xh"), sem("c_xl")
        c_wqh, c_wql, c_wkh, c_wkl = sem("c_wqh"), sem("c_wql"), sem("c_wkh"), sem("c_wkl")
        c_woh, c_wol = sem("c_woh"), sem("c_wol")
        c_q, c_kv, c_rq, c_rk, c_qs, c_ks = (sem(n) for n in ("c_q", "c_kv", "c_rq", "c_rk", "c_qs", "c_ks"))
        c_vh, c_vl, c_tr, c_trh, c_trl = (sem(n) for n in ("c_vh", "c_vl", "c_tr", "c_trh", "c_trl"))
        c_s, c_cp, c_mx, c_sub, c_ex = (sem(n) for n in ("c_s", "c_cp", "c_mx", "c_sub", "c_ex"))
        c_sum, c_rc, c_pn, c_pt, c_ph, c_pl = (sem(n) for n in ("c_sum", "c_rc", "c_pn", "c_pt", "c_ph", "c_pl"))
        c_pv, c_ah, c_al, c_wo, c_acc = (sem(n) for n in ("c_pv", "c_ah", "c_al", "c_wo", "c_acc"))
        f_wT, f_wh, f_wl, f_st, f_var, f_pow, f_xn, f_xc = (
            sem(n) for n in ("f_wT", "f_wh", "f_wl", "f_st", "f_var", "f_pow", "f_xn", "f_xc"))
        f_xT, f_xh, f_xl, f_dots, f_dense, f_dn = (
            sem(n) for n in ("f_xT", "f_xh", "f_xl", "f_dots", "f_dense", "f_dn"))
        f_v, f_p, f_cnt, f_rs, f_ex, f_y, f_g = (sem(n) for n in ("f_v", "f_p", "f_cnt", "f_rs", "f_ex", "f_y", "f_g"))

        PASSES = ((0, 0), (0, 1), (1, 0))

        def f32(ap):
            return ap.bitcast(F32)

        block = stack.enter_context(nc.Block())

        @block.sync
        def _(sp):
            def load_x(t):
                sp.dma_start(x_st, x[bass.ds(t * P, P), :]).then_inc(d_x, 16)

            sp.dma_start(x_st, x[0:P, :]).then_inc(d_x, 16)
            sp.dma_start(ident[:], c_ident).then_inc(d_const, 16)
            sp.dma_start(causal[:], c_causal).then_inc(d_const, 16)
            sp.dma_start(rope1[:], c_rope1).then_inc(d_const, 16)
            for w, at, n in ((w1q, 0, E), (w1k, E, KV1), (w1v, E + KV1, KV1)):
                sp.dma_start(w1_raw[:, :, at:at + n], w.rearrange("(c p) n -> p c n", p=P)).then_inc(d_w1, 16)
            w1o_v = w1o.rearrange("(g h d) n -> g d h n", g=G1, h=HG)
            for g in range(G1):
                sp.dma_start(w1out_raw[D1 * g:D1 * g + D1, :, :], w1o_v[g]).then_inc(d_w1o, 16)
            sp.dma_start(res, x.rearrange("(t p) n -> p t n", p=P)).then_inc(d_res, 16)
            sp.dma_start(pos_i[:], pos).then_inc(d_pos, 16)
            for i in range(2):
                sp.dma_start(mask_i[S * i:S * i + S, :].rearrange("q (b k) -> q b k", b=B),
                             mask.rearrange("b q k -> q b k")).then_inc(d_mask, 16)

            def next_x(t):
                sp.wait_ge(s_xT, t)
                load_x(t)
            with sp.Fori(1, T) as t:
                next_x(t)

            sp.wait_ge(s_x1l, T)
            sp.wait_ge(s_x1c, T)
            sp.dma_start(ctx_raw, ctx_in.rearrange("(t p) n -> p t n", p=P)).then_inc(d_ctx, 16)

            wq_v = w2q.rearrange("(c p) n -> p c n", p=P)
            wk_v = w2k.rearrange("(c p) n -> p c n", p=P)
            wv_v = w2v.rearrange("(c p) n -> p c n", p=P)

            def load_q(g):
                sp.dma_start(w2q_raw, wq_v[:, :, bass.ds(g * HG * D2, HG * D2)]).then_inc(d_w2q, 16)

            def load_kv(g):
                sp.dma_start(w2kv_raw[:, :, 0:D2], wk_v[:, :, bass.ds(g * D2, D2)]).then_inc(d_w2kv, 16)
                sp.dma_start(w2kv_raw[:, :, D2:2 * D2], wv_v[:, :, bass.ds(g * D2, D2)]).then_inc(d_w2kv, 16)

            def load_o(g):
                sp.dma_start(w2o_raw, w2o[bass.ds(g * HG * D2, HG * D2), :].rearrange("(h p) n -> p h n", p=P)
                             ).then_inc(d_w2o, 16)
            load_q(0)
            load_kv(0)
            load_o(0)
            with sp.Fori(0, G2 - 1) as g:
                sp.wait_ge(c_wql, g + 1)
                load_q(g + 1)
                sp.wait_ge(c_wkl, g + 1)
                load_kv(g + 1)
                sp.wait_ge(c_wol, g + 1)
                load_o(g + 1)

            sp.wait_ge(c_wol, G2)
            sp.dma_start(fw_raw, fw.rearrange("(c p) n -> p c n", p=P)).then_inc(d_fw, 16)
            sp.dma_start(fc_raw, fcent).then_inc(d_fc, 16)
            sp.dma_start(bias_b, fbias.rearrange("(o n) -> o n", o=1).broadcast_to([P, E])).then_inc(d_fc, 16)
            sp.wait_ge(c_cp, U)
            sp.dma_start(assign_i, fassign.rearrange("(o n) -> o n", o=1).broadcast_to([NC, E])).then_inc(d_fc, 16)

            out_v = out.rearrange("(t p) n -> t p n", p=P)
            for t in range(T):
                sp.wait_ge(f_y, t + 1)
                sp.dma_start(out_v[t], y_out[t % 2]).then_inc(d_out[t % 2], 16)
            for i in range(2):
                sp.wait_ge(d_out[i], 16 * (T // 2))

        @block.tensor
        def _(pe):
            def product(bank, lhs, rhs, chunks, inc=None):
                for c in range(chunks):
                    for n, (a, b) in enumerate(PASSES):
                        mm = pe.matmul(bank, lhs(a, c), rhs(b, c), start=(c == 0 and n == 0),
                                       stop=(c == chunks - 1 and n == 2))
                return mm

            TX, BQ, BKV, TR, SB, BO = banks[0], banks[1], banks[2], banks[3:5], banks[5:7], banks[7]

            def a_stage(t):
                for c in range(EC):
                    mm = pe.transpose(TX[:, c * P:(c + 1) * P], x_st[:, c * P:(c + 1) * P], ident[:])
                mm.then_inc(s_xT, 1)

            def b_stage(t):
                product(BQ[:], lambda a, c: xt[a][:, c, :], lambda b, c: w1[b][:, c, 0:E], EC).then_inc(s_q, 1)
                product(BKV[:, 0:2 * KV1], lambda a, c: xt[a][:, c, :],
                        lambda b, c: w1[b][:, c, E:E + 2 * KV1], EC).then_inc(s_kv, 1)

            def pt_stage(v, u):
                if u < 2:
                    pe.wait_ge(s_qke, 6 * v + 5 + u)
                else:
                    pe.wait_ge(s_pl, 4 * v + u - 1)
                pe.wait_ge(s_pn, 4 * v + u + 1)
                for i in range(4):
                    mm = pe.transpose(TR[u % 2][:, i * P:(i + 1) * P], p1[u][:, i * P:(i + 1) * P], ident[:])
                mm.then_inc(s_pt, 1)

            def pv_stage(v, half_, first, last):
                for g in range(4 * half_, 4 * half_ + 4):
                    for n, (a, b) in enumerate(PASSES):
                        for i in range(2):
                            rows = slice(S * i, S * i + S)
                            mm = pe.matmul((BO, BKV)[i][:, 0:2 * P], vpad[a][rows, g * P:(g + 1) * P],
                                           pT1[b][rows, g, :, :].rearrange("p a n -> p (a n)"),
                                           start=(g == 0 and n == 0), stop=(g == G1 - 1 and n == 2))
                if last:
                    mm.then_inc(s_pv, 1)

            def qk_stage(t, first):
                pe.wait_ge(s_ql, t + 1)
                pe.wait_ge(s_kl, t + 1)
                for j, (kind, n) in enumerate((("q", 0), ("q", 1), ("k", 0), ("q", 2), ("q", 3), ("k", 1))):
                    if j >= 2:
                        pe.wait_ge(s_qke, 6 * t + j - 1)
                    elif not first:
                        pe.wait_ge(s_pl, 4 * t - 1 + j)
                    for i in range(4):
                        m = 4 * n + i
                        src = f32(stack_q[:, 2 * m:2 * m + 2, :].rearrange("p h r -> p (h r)")) \
                            if kind == "q" else f32(stack_k[:, m, :])
                        mm = pe.transpose(TR[j % 2][:, i * P:(i + 1) * P], src, ident[:])
                    mm.then_inc(s_qk, 1)

            def wo_stage(v, first):
                pe.wait_ge(s_al, v + 1)
                if not first:
                    pe.wait_ge(s_x1l, v)
                product(TX[:], lambda a, c: at1[a][:, c, :, :].rearrange("p b q -> p (b q)"),
                        lambda b, c: w1out[b][:, 2 * (c % 2) + c // 2, :], 4).then_inc(s_wo, 1)

            def s_stage(t, first):
                for u in range(4):
                    if u % 2 == 0:
                        pe.wait_ge(s_qke, 6 * t + 3 + 3 * (u // 2))
                    if u >= 2 or not first:
                        pe.wait_ge(s_cp, 4 * t + u - 1)
                    rows = slice(S * (u % 2), S * (u % 2) + S)
                    for i in range(4):
                        g = 4 * (u // 2) + i
                        for b in range(2):
                            mm = pe.matmul(SB[u % 2][:, (2 * i + b) * S:(2 * i + b + 1) * S],
                                           qT1[rows, b, 2 * g:2 * g + 2, :].rearrange("p j q -> p (j q)"),
                                           kT1[rows, g, b * S:(b + 1) * S], start=True, stop=True)
                    mm.then_inc(s_s, 1)

            def x1_stage(v, last):
                pe.wait_ge(s_x1n, v + 1)
                pe.wait_ge(s_xl, T if last else v + 3)
                for c in range(EC):
                    mm = pe.transpose(TX[:, c * P:(c + 1) * P], x1n[:, c * P:(c + 1) * P], ident[:])
                mm.then_inc(s_x1T, 1)

            def tile_steps(t, first=False, last=False, second=False):
                v = t - 1
                pe.wait_ge(s_xl, t + 1)
                if not first:
                    pe.wait_ge(s_rq, t)
                    if not second:
                        pe.wait_ge(s_al, v)
                b_stage(t)
                if not first:
                    pt_stage(v, 0)
                    pt_stage(v, 1)
                    pe.wait_ge(s_vl, v + 1)
                    pe.wait_ge(s_rk, t + 1)
                    pe.wait_ge(s_vr, t + 1)
                    pe.wait_ge(s_pl, 4 * v + 2)
                    pv_stage(v, 0, first, False)
                    pt_stage(v, 2)
                    pt_stage(v, 3)
                    pe.wait_ge(s_pl, 4 * v + 4)
                    pv_stage(v, 1, first, True)
                qk_stage(t, first)
                if not first:
                    wo_stage(v, second)
                s_stage(t, first)
                if not last:
                    pe.wait_ge(d_x, 16 * (t + 2))
                    if not first:
                        pe.wait_ge(s_res, t)
                    else:
                        pe.wait_ge(s_xl, 1)
                    a_stage(t + 1)
                if not first:
                    x1_stage(v, last)

            pe.wait_ge(d_const, 48)
            pe.wait_ge(d_x, 16)
            a_stage(0)
            pe.wait_ge(s_w1l, 2)
            pe.wait_ge(s_init, 3)
            tile_steps(0, first=True)
            tile_steps(1, second=True)
            with pe.Fori(2, T - 1) as t:
                tile_steps(t)
            tile_steps(T - 1, last=True)
            v = T - 1
            pt_stage(v, 0)
            pt_stage(v, 1)
            pe.wait_ge(s_vl, T)
            pe.wait_ge(s_al, v)
            pe.wait_ge(s_pl, 4 * v + 2)
            pv_stage(v, 0, False, False)
            pt_stage(v, 2)
            pt_stage(v, 3)
            pe.wait_ge(s_pl, 4 * v + 4)
            pv_stage(v, 1, False, True)
            wo_stage(v, False)
            x1_stage(v, True)

            pe.wait_ge(s_x1l, T)
            pe.wait_ge(d_ctx, 16)
            CT = banks[0:4]
            for t in range(T):
                if t >= 4:
                    pe.wait_ge(c_xl, t - 3)
                for c in range(EC):
                    mm = pe.transpose(CT[t % 4][:, c * P:(c + 1) * P], ctx_raw[:, t, c * P:(c + 1) * P], ident[:])
                mm.then_inc(c_xT, 1)
            pe.wait_ge(c_xl, T)

            BQ2, BKV2, TR2, BS2, BO2 = banks[0:2], banks[2], banks[3:5], banks[5], banks[6:8]

            def q_proj(u, c, i, g, first):
                if not first:
                    pe.wait_ge(c_rq, 2 * u + i - 1)
                tok = slice((2 * c + i) * P, (2 * c + i + 1) * P)
                product(BQ2[i][:], lambda a, e: xT[a][:, e, tok], lambda b, e: w2q_s[b][:, e, :], EC
                        ).then_inc(c_q, 1)

            def kv_proj(u, c, first):
                if not first:
                    pe.wait_ge(c_rk, u)
                    pe.wait_ge(c_vl, u)
                for i in range(2):
                    tok = slice((2 * c + i) * P, (2 * c + i + 1) * P)
                    mm = product(BKV2[:, 256 * i:256 * i + 256], lambda a, e: cT[a][:, e, tok],
                                 lambda b, e: w2kv_s[b][:, e, :], EC)
                mm.then_inc(c_kv, 1)

            def p_turn(v):
                pe.wait_ge(c_trl, 3 * v + 2)
                pe.wait_ge(c_pn, v + 1)
                for i in range(2):
                    for h in range(2):
                        mm = pe.transpose(TR2[0][:, (2 * i + h) * P:(2 * i + h + 1) * P],
                                          p2[:, (2 * h + i) * P:(2 * h + i + 1) * P], ident[:])
                mm.then_inc(c_pt, 1)

            def pv(v, c, first):
                pe.wait_ge(c_pl, v + 1)
                pe.wait_ge(c_vl, v + 1)
                if not first:
                    pe.wait_ge(c_acc, 2 * v)
                for i in range(2):
                    for n, (a, b) in enumerate(PASSES):
                        for s in range(2):
                            rows = slice(S * s, S * s + S)
                            mm = pe.matmul(BO2[s][:, 256 * i:256 * i + 256], v2[c % 2][a][rows, i, :],
                                           pT2[b][rows, i, :], start=(n == 0), stop=(n == 2))
                mm.then_inc(c_pv, 1)

            def q_turn(u, i, first):
                if i == 0:
                    if not first:
                        pe.wait_ge(c_trl, 3 * u)
                elif not first:
                    pe.wait_ge(c_pl, u)
                pe.wait_ge(c_qs, 2 * u + i + 1)
                for h in range(HG):
                    mm = pe.transpose(TR2[1 - i][:, h * P:(h + 1) * P], u1q[i][:, h * P:(h + 1) * P], ident[:])
                mm.then_inc(c_tr, 1)

            def k_turn(u):
                pe.wait_ge(c_trl, 3 * u + 1)
                pe.wait_ge(c_ks, u + 1)
                for i in range(2):
                    mm = pe.transpose(TR2[1][:, i * P:(i + 1) * P], u1k[:, i * P:(i + 1) * P], ident[:])
                mm.then_inc(c_tr, 1)

            def out_proj(v, i):
                product(BO2[i][:], lambda a, h: at2[a][:, h, i * P:(i + 1) * P], lambda b, h: w2o_s[b][:, h, :], HG
                        ).then_inc(c_wo, 1)

            def scores(u, first):
                pe.wait_ge(c_trl, 3 * u + 3)
                if not first:
                    pe.wait_ge(c_cp, u)
                for h in range(2):
                    for b in range(4):
                        at = (4 * h + b) * S
                        for n, (a, k) in enumerate(PASSES):
                            mm = pe.matmul(BS2[:, at:at + S], qT2[a][:, b, 2 * h:2 * h + 2, :].rearrange("p h q -> p (h q)"),
                                           kT2[k][:, b * S:(b + 1) * S], start=(n == 0), stop=(n == 2))
                mm.then_inc(c_s, 1)

            def slot(u, g, c, has_x=True, has_y=True, first_y=False):
                v = u - 1
                gv = g if c > 0 else g - 1
                if has_x:
                    pe.wait_ge(c_wql, g + 1)
                    q_proj(u, c, 0, g, not has_y)
                    q_proj(u, c, 1, g, not has_y)
                if has_y:
                    p_turn(v)
                if has_x:
                    pe.wait_ge(c_wkl, g + 1)
                    kv_proj(u, c, not has_y)
                if has_y:
                    pv(v, (c - 1) % UN, first_y)
                if has_x:
                    q_turn(u, 0, not has_y)
                    q_turn(u, 1, not has_y)
                if has_y:
                    pe.wait_ge(c_al, 2 * v + 2)
                    pe.wait_ge(c_wol, gv + 1)
                    out_proj(v, 0)
                if has_x:
                    k_turn(u)
                if has_y:
                    out_proj(v, 1)
                if has_x:
                    scores(u, not has_y)

            slot(0, 0, 0, has_y=False)
            slot(1, 0, 1, first_y=True)
            for c in range(2, UN):
                slot(c, 0, c)
            slot(UN, 1, 0)
            with pe.Fori(1, G2 - 1) as g:
                for c in range(1, UN + 1):
                    slot(UN * g + c, g + c // UN, c % UN)
            for c in range(1, UN):
                slot(U - UN + c, G2 - 1, c)
            slot(U, G2, 0, has_x=False)

            pe.wait_ge(d_fw, 16)
            pe.wait_ge(d_fc, 16 * 3)
            for c in range(EC):
                for j in range(EC):
                    mm = pe.transpose(banks[c][:, j * P:(j + 1) * P], fw_raw[:, j, c * P:(c + 1) * P], ident[:])
                mm.then_inc(f_wT, 1)
            for c in range(EC):
                mm = pe.transpose(banks[4][:, c * NC:(c + 1) * NC], fc_raw[:, c * P:(c + 1) * P], ident[0:NC, 0:NC])
            mm.then_inc(f_wT, 1)
            pe.wait_ge(f_wl, EC + 1)
            pe.wait_ge(c_acc, 2 * U)

            def ffn_tile(t, par, first):
                bt, bd = banks[par], banks[2 + par]
                pe.wait_ge(f_xn, t + 1)
                if not first:
                    pe.wait_ge(f_xl, t - 1)
                for c in range(EC):
                    mm = pe.transpose(bt[:, c * P:(c + 1) * P], x3n[par][:, c * P:(c + 1) * P], ident[:])
                mm.then_inc(f_xT, 1)
                pe.wait_ge(f_xl, t + 1)
                if not first:
                    pe.wait_ge(f_dn, t - 1)
                product(bd[:], lambda a, c: x3T[par][a][:, c, :], lambda b, c: fwT[b][:, c, :], EC
                        ).then_inc(f_dense, 1)
                product(banks[5][:, bass.ds(t * NC, NC)], lambda a, c: x3T[par][a][:, c, :],
                        lambda b, c: fcT[b][:, c, :], EC).then_inc(f_dots, 1)

            ffn_tile(0, 0, True)
            ffn_tile(1, 1, True)
            with pe.Fori(1, T // 2) as i:
                ffn_tile(2 * i, 0, False)
                ffn_tile(2 * i + 1, 1, False)
            pe.wait_ge(f_v, 7)
            pe.matmul(banks[6][0:NC, 0:P], any_hit, ones[:], start=True, stop=True).then_inc(f_cnt, 1)
            pe.wait_ge(f_rs, 1)
            pe.matmul(banks[7][:], cluster_hit[0:NC, :], onehot, start=True, stop=True).then_inc(f_cnt, 1)

        @block.scalar
        def _(act):
            def copy(dst, src, done):
                act.activation(dst, src, ACT.Copy).then_inc(done, 1)

            act.wait_ge(s_xT, 1)
            copy(xt[0], banks[0][:].rearrange("p (c n) -> p c n", c=EC), s_xh)
            act.wait_ge(d_w1, 48)
            copy(w1[0], w1_raw, s_w1h)
            act.wait_ge(d_w1o, 16 * G1)
            copy(w1out[0], w1out_raw, s_w1h)

            def p_high(v, u, first):
                act.wait_ge(s_pt, 4 * v + u + 1)
                if u == 0 and not first:
                    act.wait_ge(s_pv, v)
                copy(pT1[0][:, 4 * (u // 2):4 * (u // 2) + 4, u % 2, :],
                     banks[3 + u % 2][:].rearrange("p (g n) -> p g n", g=4), s_ph)

            def at_high(v, first):
                act.wait_ge(s_pv, v + 1)
                if not first:
                    act.wait_ge(s_wo, v)
                for i, bank in enumerate((banks[7], banks[2])):
                    copy(at1[0][:, :, i, :], bank[:, 0:2 * P].rearrange("p (a q) -> p a q", a=4), s_ah)

            def tile_steps(t, first=False, last=False, tail=False, second=False):
                v = t - 1
                if not tail:
                    act.wait_ge(s_kv, t + 1)
                    if not first:
                        act.wait_ge(s_vl, t)
                    copy(v_raw, banks[2][:, KV1:2 * KV1], s_vr)
                if not first:
                    p_high(v, 0, second)
                    p_high(v, 1, second)
                if not tail:
                    act.wait_ge(s_qs, t + 1)
                    if not first:
                        act.wait_ge(s_qk, 6 * t)
                    copy(stack_q.rearrange("p h (a b d) -> p h a b d", a=2, b=2)[:, :, 0],
                         bcast(t1q.rearrange("p (h d) -> p h d", h=H1), 2, 2), s_qh)
                    act.wait_ge(s_ks, t + 1)
                    copy(stack_k.rearrange("p g (a b d) -> p g a b d", a=4, b=2)[:, :, :, 0],
                         bcast(t1k.rearrange("p (g d) -> p g d", g=G1), 2, 4), s_kh)
                if not first:
                    p_high(v, 2, second)
                    p_high(v, 3, second)
                    at_high(v, second)
                if not tail:
                    copy(vpad[0].rearrange("p (g n) -> p g n", g=G1)[:, :, 0:D1],
                         v_raw.rearrange("p (g d) -> p g d", g=G1), s_vh)
                    n_q = n_k = 0
                    if not first:
                        act.wait_ge(s_s, 4 * t)
                    for j, kind in enumerate("qqkqqk"):
                        act.wait_ge(s_qk, 6 * t + j + 1)
                        src = banks[3 + j % 2][:].rearrange("p (g n) -> p g n", g=4)
                        if kind == "q":
                            copy(qT1[:, :, 4 * n_q:4 * n_q + 4, :].rearrange("p b j q -> p j b q"),
                                 src.rearrange("p g (b q) -> p g b q", b=2), s_qke)
                            n_q += 1
                        else:
                            copy(kT1[:, 4 * n_k:4 * n_k + 4, :], src, s_qke)
                            n_k += 1
                if not first:
                    act.wait_ge(s_x1n, v + 1)
                    copy(res[:, bass.ds(v, 1), :].rearrange("p t n -> p (t n)"), x1n, s_x1c)

                def expo(u):
                    act.wait_ge(s_sub, 4 * t + u + 1)
                    act.activation(p1[u], p1[u], ACT.Exp, scale=SCALE1).then_inc(s_ex, 1)

                if not tail:
                    expo(0)
                    expo(1)
                    if not last:
                        act.wait_ge(s_xT, t + 2)
                        copy(xt[0], banks[0][:].rearrange("p (c n) -> p c n", c=EC), s_xh)
                    expo(2)
                if not first:
                    act.wait_ge(s_x1T, v + 1)
                    copy(xT[0][:, :, bass.ds(v * P, P)], banks[0][:].rearrange("p (c n) -> p c n", c=EC), s_x1h)
                if not tail:
                    expo(3)

            act.wait_ge(s_init, 3)
            act.wait_ge(d_res, 16)
            tile_steps(0, first=True)
            tile_steps(1, second=True)
            with act.Fori(2, T - 1) as t:
                tile_steps(t)
            tile_steps(T - 1, last=True)
            tile_steps(T, tail=True)

            act.wait_ge(s_x1l, T)
            for t in range(T):
                act.wait_ge(c_xT, t + 1)
                copy(cT[0][:, :, t * P:(t + 1) * P], banks[t % 4][:].rearrange("p (c n) -> p c n", c=EC), c_xh)

            def w_qkv(g):
                act.wait_ge(d_w2q, 16 * (g + 1))
                copy(w2q_s[0], w2q_raw, c_wqh)
                act.wait_ge(d_w2kv, 32 * (g + 1))
                copy(w2kv_s[0], w2kv_raw, c_wkh)

            def w_out(g):
                act.wait_ge(d_w2o, 16 * (g + 1))
                copy(w2o_s[0], w2o_raw, c_woh)

            def turn_high(u, n):
                act.wait_ge(c_tr, 3 * u + n + 1)
                if n < 2:
                    copy(qT2[0][:, 2 * n:2 * n + 2].rearrange("p b h q -> p h b q"),
                         cut(banks[4 - n][:], h=HG, b=2, q=S), c_trh)
                else:
                    copy(kT2[0], banks[4][:, 0:2 * P], c_trh)

            def slot(u, g, c, has_x=True, has_y=True):
                v = u - 1
                if has_y:
                    act.wait_ge(c_sub, v + 1)
                    act.activation(p2, p2, ACT.Exp, scale=SCALE2).then_inc(c_ex, 1)
                    act.wait_ge(c_pt, v + 1)
                    if not (g == 0 and c == 1) if isinstance(g, int) else True:
                        act.wait_ge(c_pv, v)
                    copy(pT2[0], banks[3][:].rearrange("p (i n) -> p i n", i=2), c_ph)
                if has_x:
                    act.wait_ge(c_kv, u + 1)
                    if has_y:
                        act.wait_ge(c_pv, v)
                    copy(v2[c % 2][0], banks[2][:].rearrange("p (i n) -> p i n", i=2)[:, :, D2:2 * D2], c_vh)
                    if c == UN - 1 and not (isinstance(g, int) and g == G2 - 1):
                        w_qkv(g + 1)
                    if has_y:
                        act.wait_ge(c_s, u)
                    turn_high(u, 0)
                if has_y:
                    act.wait_ge(c_pv, v + 1)
                    if not (g == 0 and c == 1) if isinstance(g, int) else True:
                        act.wait_ge(c_wo, 2 * v)
                    for s in range(2):
                        copy(at2[0].rearrange("p h (i s q) -> p s i h q", i=2, s=2)[:, s],
                             banks[6 + s][:].rearrange("p (i h q) -> p i h q", i=2, h=HG), c_ah)
                if has_x:
                    turn_high(u, 1)
                    turn_high(u, 2)
                if has_y and has_x and c == 0:
                    act.wait_ge(c_wo, 2 * v + 2)
                    w_out(g)

            w_qkv(0)
            w_out(0)
            slot(0, 0, 0, has_y=False)
            for c in range(1, UN):
                slot(c, 0, c)
            slot(UN, 1, 0)
            with act.Fori(1, G2 - 1) as g:
                for c in range(1, UN + 1):
                    slot(UN * g + c, g + c // UN, c % UN)
            for c in range(1, UN):
                slot(U - UN + c, G2 - 1, c)
            slot(U, G2, 0, has_x=False)

            for c in range(EC):
                act.wait_ge(f_wT, c + 1)
                copy(fwT[0][:, c, :], banks[c][:], f_wh)
            act.wait_ge(f_wT, EC + 1)
            copy(fcT[0], banks[4][:, 0:EC * NC].rearrange("p (c n) -> p c n", c=EC), f_wh)

            def ffn_tile(t, par, first):
                act.wait_ge(f_xT, t + 1)
                if not first:
                    act.wait_ge(f_dots, t - 1)
                copy(x3T[par][0], banks[par][:].rearrange("p (c n) -> p c n", c=EC), f_xh)
                copy(res[:, bass.ds(t, 1), :].rearrange("p t n -> p (t n)"), x3n[par], f_xc)

            ffn_tile(0, 0, True)
            ffn_tile(1, 1, True)
            with act.Fori(1, T // 2) as i:
                ffn_tile(2 * i, 0, False)
                ffn_tile(2 * i + 1, 1, False)
            act.wait_ge(f_v, 2)
            act.activation(dots, dots, ACT.Exp, scale=INV_TEMPERATURE).then_inc(f_ex, 1)

        @block.gpsimd
        def _(pool):
            pool.memset(f32(vpad[0]), 0.0).then_inc(s_init, 1)
            pool.memset(f32(vpad[1]), 0.0).then_inc(s_init, 1)
            pool.memset(half[:], -0.5).then_inc(s_init, 1)
            pool.memset(half8, -0.5).then_inc(s_dinit, 1)
            pool.memset(ones[:], 1.0).then_inc(s_dinit, 1)
            for i in range(2):
                pool.memset(sc1[i], NEG1).then_inc(s_dinit, 1)
            pool.wait_ge(d_pos, 16)
            for t in range(T):
                pool.indirect_dma_start(cs[:, t, :], None, c_rope2,
                                        bass.IndirectOffsetOnAxis(ap=pos_i[:, t:t + 1], axis=0)).then_inc(d_cs, 16)

            def rope_sum(t):
                pool.wait_ge(s_rq, t + 1)
                pool.tensor_tensor(t1q, t1q, t2q, ALU.add).then_inc(s_qs, 1)
                pool.wait_ge(s_rk, t + 1)
                pool.tensor_tensor(t1k, t1k, t2k, ALU.add).then_inc(s_ks, 1)

            def sub(t, u, first):
                pool.wait_ge(s_mx, 4 * t + u + 1)
                if not first:
                    pool.wait_ge(s_pt, 4 * t + u - 3)
                pool.tensor_tensor(cut(p1[u], b=8, k=S), cut(sc1[u % 2], b=8, k=S), bcast(mx1[u], 2, S),
                                   ALU.subtract).then_inc(s_sub, 1)

            def norm(t, u):
                pool.wait_ge(s_rc, 4 * t + u + 1)
                pool.tensor_tensor(cut(p1[u], b=8, k=S), cut(p1[u], b=8, k=S), bcast(sm1[u], 2, S),
                                   ALU.mult).then_inc(s_pn, 1)

            def ln(v):
                pool.wait_ge(s_ln, 3 * v + 3)
                pool.tensor_tensor(rstd, mv[:, 1:2], half, ALU.pow).then_inc(s_lp, 1)

            def tile_steps(t, first=False, tail=False):
                if not tail:
                    rope_sum(t)
                if not first:
                    ln(t - 1)
                if not tail:
                    sub(t, 0, first)
                    sub(t, 1, first)
                    norm(t, 0)
                    sub(t, 2, first)
                    norm(t, 1)
                    sub(t, 3, first)
                    norm(t, 2)
                    norm(t, 3)

            pool.wait_ge(s_init, 3)
            tile_steps(0, first=True)
            with pool.Fori(1, T) as t:
                tile_steps(t)
            tile_steps(T, tail=True)

            pool.wait_ge(s_x1l, T)
            for i in range(UN):
                pool.memset(sc2[i], NEG2).then_inc(c_init, 1)

            def sum_q(u, i):
                pool.wait_ge(c_rq, 2 * u + i + 1)
                pool.tensor_tensor(u1q[i], u1q[i], u2q[i], ALU.add).then_inc(c_qs, 1)

            def slot(u, g, c, has_x=True, has_y=True, first_y=False):
                v = u - 1
                if has_y:
                    pool.wait_ge(c_mx, v + 1)
                    if not first_y:
                        pool.wait_ge(c_pt, v)
                    pool.tensor_tensor(cut(p2, b=8, k=S), cut(sc2[(c - 1) % UN], b=8, k=S), bcast(mx2, 2, S),
                                       ALU.subtract).then_inc(c_sub, 1)
                if has_x:
                    sum_q(u, 0)
                if has_y:
                    pool.wait_ge(c_rc, v + 1)
                    pool.tensor_tensor(cut(p2, b=8, k=S), cut(p2, b=8, k=S), bcast(sm2, 2, S),
                                       ALU.mult).then_inc(c_pn, 1)
                if has_x:
                    sum_q(u, 1)
                    pool.wait_ge(c_rk, u + 1)
                    pool.tensor_tensor(u1k, u1k, u2k, ALU.add).then_inc(c_ks, 1)

            slot(0, 0, 0, has_y=False)
            slot(1, 0, 1, first_y=True)
            for c in range(2, UN):
                slot(c, 0, c)
            slot(UN, 1, 0)
            with pool.Fori(1, G2 - 1) as g:
                for c in range(1, UN + 1):
                    slot(UN * g + c, g + c // UN, c % UN)
            for c in range(1, UN):
                slot(U - UN + c, G2 - 1, c)
            slot(U, G2, 0, has_x=False)

            pool.iota(pos_i[0:NC, 0:1], pattern=[[0, 1]], base=0,
                      channel_multiplier=1).then_inc(f_g, 1)
            pool.wait_ge(f_var, 1)
            pool.tensor_tensor(rstd8, var8, half8, ALU.pow).then_inc(f_pow, 1)
            pool.wait_ge(f_var, 2)
            pool.tensor_tensor(rstd8, var8, half8, ALU.pow).then_inc(f_pow, 1)

        @block.vector
        def _(dve):
            def low(dst, src, high, done):
                dve.tensor_tensor(dst, src, f32(high), ALU.subtract).then_inc(done, 1)

            def hold():
                dve.sem_inc(s_gate, 1)

            def x_low(t):
                dve.wait_ge(s_xh, t + 1)
                low(xt[1], banks[0][:].rearrange("p (c n) -> p c n", c=EC), xt[0], s_xl)

            def rope_q(t, first):
                q = banks[1][:].rearrange("p (h d) -> p h d", h=H1)
                t1, t2 = (v.rearrange("p (h d) -> p h d", h=H1) for v in (t1q, t2q))
                dve.wait_ge(s_q, t + 1)
                if not first:
                    dve.wait_ge(s_ql, t)
                dve.tensor_tensor(t1, q, bcast(rope1[:, 0:D1], 1, H1), ALU.mult)
                sin = bcast(rope1[:, D1:D1 + 8], 1, H1)
                dve.scalar_tensor_tensor(t2[:, :, 0:D1:2], q[:, :, 1:D1:2], -1.0, sin, ALU.mult, ALU.mult)
                dve.tensor_tensor(t2[:, :, 1:D1:2], q[:, :, 0:D1:2], sin, ALU.mult).then_inc(s_rq, 1)

            def rope_k(t, first):
                k = banks[2][:, 0:KV1].rearrange("p (h d) -> p h d", h=G1)
                t1, t2 = (v.rearrange("p (h d) -> p h d", h=G1) for v in (t1k, t2k))
                dve.wait_ge(s_kv, t + 1)
                dve.wait_ge(s_vr, t + 1)
                if not first:
                    dve.wait_ge(s_kl, t)
                dve.tensor_tensor(t1, k, bcast(rope1[:, 0:D1], 1, G1), ALU.mult)
                sin = bcast(rope1[:, D1:D1 + 8], 1, G1)
                dve.scalar_tensor_tensor(t2[:, :, 0:D1:2], k[:, :, 1:D1:2], -1.0, sin, ALU.mult, ALU.mult)
                dve.tensor_tensor(t2[:, :, 1:D1:2], k[:, :, 0:D1:2], sin, ALU.mult).then_inc(s_rk, 1)

            def p_low(v, u):
                dve.wait_ge(s_ph, 4 * v + u + 1)
                gs = slice(4 * (u // 2), 4 * (u // 2) + 4)
                low(pT1[1][:, gs, u % 2, :], banks[3 + u % 2][:].rearrange("p (g n) -> p g n", g=4),
                    pT1[0][:, gs, u % 2, :], s_pl)

            def stack_low(t):
                dve.wait_ge(s_qh, t + 1)
                sq = stack_q.rearrange("p h (a b d) -> p h a b d", a=2, b=2)
                low(sq[:, :, 1], bcast(t1q.rearrange("p (h d) -> p h d", h=H1), 2, 2), sq[:, :, 0], s_ql)
                dve.wait_ge(s_kh, t + 1)
                sk = stack_k.rearrange("p g (a b d) -> p g a b d", a=4, b=2)
                low(sk[:, :, :, 1], bcast(t1k.rearrange("p (g d) -> p g d", g=G1), 2, 4), sk[:, :, :, 0], s_kl)

            def at_low(v):
                for i, bank in enumerate((banks[7], banks[2])):
                    dve.wait_ge(s_ah, 2 * v + i + 1)
                    ins = dve.tensor_tensor(at1[1][:, :, i, :], bank[:, 0:2 * P].rearrange("p (a q) -> p a q", a=4),
                                            f32(at1[0][:, :, i, :]), ALU.subtract)
                ins.then_inc(s_al, 1)

            def v_low(t):
                dve.wait_ge(s_vh, t + 1)
                vp = [v.rearrange("p (g n) -> p g n", g=G1)[:, :, 0:D1] for v in vpad]
                low(vp[1], v_raw.rearrange("p (g d) -> p g d", g=G1), vp[0], s_vl)

            def ln(v, first):
                y = res[:, bass.ds(v, 1), :].rearrange("p t n -> p (t n)")
                dve.wait_ge(s_wo, v + 1)
                dve.tensor_tensor(y, banks[0][:], y, ALU.add).then_inc(s_res, 1)
                dve.wait_ge(s_res, v + 1)
                hold()
                dve.bn_stats(st6, y).then_inc(s_ln, 1)
                dve.wait_ge(s_ln, 3 * v + 1)
                hold()
                dve.bn_aggr(mv, st6).then_inc(s_ln, 1)
                dve.wait_ge(s_ln, 3 * v + 2)
                dve.tensor_scalar(mv[:, 1:2], mv[:, 1:2], EPS, None, ALU.add).then_inc(s_ln, 1)
                dve.wait_ge(s_lp, v + 1)
                if not first:
                    dve.wait_ge(s_x1T, v)
                    dve.wait_ge(s_x1c, v)
                dve.tensor_scalar(x1n, y, mv[:, 0:1], rstd, ALU.subtract, ALU.mult).then_inc(s_x1n, 1)

            def masked_max(t, u, first):
                dve.wait_ge(s_s, 4 * t + u + 1)
                if u >= 2 or not first:
                    dve.wait_ge(s_sub, 4 * t + u - 1)
                sc = cut(sc1[u % 2], b=8, k=S)
                hold()
                dve.copy_predicated(sc, bcast(causal[:], 1, 8), cut(banks[5 + u % 2][:], b=8, k=S)).then_inc(s_cp, 1)
                dve.wait_ge(s_cp, 4 * t + u + 1)
                dve.tensor_reduce(mx1[u], sc, AX.X, ALU.max).then_inc(s_mx, 1)

            def total(t, u):
                dve.wait_ge(s_ex, 4 * t + u + 1)
                dve.tensor_reduce(sm1[u], cut(p1[u], b=8, k=S), AX.X, ALU.add).then_inc(s_sum, 1)
                dve.wait_ge(s_sum, 4 * t + u + 1)
                dve.reciprocal(sm1[u], sm1[u]).then_inc(s_rc, 1)

            def tile_steps(t, first=False, last=False, tail=False, second=False):
                v = t - 1
                if not tail:
                    rope_q(t, first)
                    rope_k(t, first)
                if not first:
                    p_low(v, 0)
                    p_low(v, 1)
                if not tail:
                    stack_low(t)
                if not first:
                    p_low(v, 2)
                    p_low(v, 3)
                    at_low(v)
                if not tail:
                    v_low(t)
                if not first:
                    ln(v, second)
                if not tail:
                    masked_max(t, 0, first)
                    masked_max(t, 1, first)
                    total(t, 0)
                    masked_max(t, 2, first)
                    total(t, 1)
                    if not last:
                        x_low(t + 1)
                    masked_max(t, 3, first)
                    total(t, 2)
                if not first:
                    dve.wait_ge(s_x1h, v + 1)
                    low(xT[1][:, :, bass.ds(v * P, P)], banks[0][:].rearrange("p (c n) -> p c n", c=EC),
                        xT[0][:, :, bass.ds(v * P, P)], s_x1l)
                if not tail:
                    total(t, 3)

            x_low(0)
            dve.wait_ge(s_w1h, 1)
            low(w1[1], w1_raw, w1[0], s_w1l)
            dve.wait_ge(s_w1h, 2)
            low(w1out[1], w1out_raw, w1out[0], s_w1l)
            dve.wait_ge(d_const, 48)
            dve.wait_ge(s_dinit, 4)
            dve.wait_ge(s_init, 3)
            dve.wait_ge(d_res, 16)
            tile_steps(0, first=True)
            tile_steps(1, second=True)
            with dve.Fori(2, T - 1) as t:
                tile_steps(t)
            tile_steps(T - 1, last=True)
            tile_steps(T, tail=True)

            for t in range(T):
                dve.wait_ge(c_xh, t + 1)
                low(cT[1][:, :, t * P:(t + 1) * P], banks[t % 4][:].rearrange("p (c n) -> p c n", c=EC),
                    cT[0][:, :, t * P:(t + 1) * P], c_xl)

            def w_qkv(g):
                dve.wait_ge(c_wqh, g + 1)
                low(w2q_s[1], w2q_raw, w2q_s[0], c_wql)
                dve.wait_ge(c_wkh, g + 1)
                low(w2kv_s[1], w2kv_raw, w2kv_s[0], c_wkl)

            def w_out(g):
                dve.wait_ge(c_woh, g + 1)
                low(w2o_s[1], w2o_raw, w2o_s[0], c_wol)

            def rope2_q(u, c, i, first):
                dve.wait_ge(c_q, 2 * u + i + 1)
                if not first:
                    dve.wait_ge(c_tr, 3 * u + i - 2)
                q = banks[i][:].rearrange("p (h f d) -> p h f d", h=HG, f=2)
                t1, t2 = (w[i].rearrange("p (h f d) -> p h f d", h=HG, f=2) for w in (u1q, u2q))
                cos = bcast(bcast(cs[:, 2 * c + i, 0:64], 1, 2), 1, HG)
                sin = bcast(cs[:, 2 * c + i, 64:128], 1, HG)
                dve.tensor_tensor(t1, q, cos, ALU.mult)
                dve.scalar_tensor_tensor(t2[:, :, 0, :], q[:, :, 1, :], -1.0, sin, ALU.mult, ALU.mult)
                dve.tensor_tensor(t2[:, :, 1, :], q[:, :, 0, :], sin, ALU.mult).then_inc(c_rq, 1)

            def rope2_k(u, c, first):
                dve.wait_ge(c_kv, u + 1)
                dve.wait_ge(c_vh, u + 1)
                if not first:
                    dve.wait_ge(c_tr, 3 * u)
                k = banks[2][:].rearrange("p (i n) -> p i n", i=2)[:, :, 0:D2].rearrange("p i (f d) -> p i f d", f=2)
                t1, t2 = (w.rearrange("p (i f d) -> p i f d", i=2, f=2) for w in (u1k, u2k))
                cos = bcast(cs[:, 2 * c:2 * c + 2, 0:64], 2, 2)
                sin = cs[:, 2 * c:2 * c + 2, 64:128]
                dve.tensor_tensor(t1, k, cos, ALU.mult)
                dve.scalar_tensor_tensor(t2[:, :, 0, :], k[:, :, 1, :], -1.0, sin, ALU.mult, ALU.mult)
                dve.tensor_tensor(t2[:, :, 1, :], k[:, :, 0, :], sin, ALU.mult).then_inc(c_rk, 1)

            def turn_low(u, n):
                dve.wait_ge(c_trh, 3 * u + n + 1)
                if n < 2:
                    high, lo_ = (w[:, 2 * n:2 * n + 2].rearrange("p b h q -> p h b q") for w in qT2)
                    low(lo_, cut(banks[4 - n][:], h=HG, b=2, q=S), high, c_trl)
                else:
                    low(kT2[1], banks[4][:, 0:2 * P], kT2[0], c_trl)

            def slot(u, g, c, has_x=True, has_y=True):
                v = u - 1
                cv = (c - 1) % UN
                if has_y:
                    sc = sc2[cv].rearrange("p (h n) -> p h n", h=2)
                    dve.wait_ge(c_s, v + 1)
                    hold()
                    dve.copy_predicated(sc, bcast(mask_i[:, cv * 4 * S:(cv + 1) * 4 * S], 1, 2),
                                        banks[5][:].rearrange("p (h n) -> p h n", h=2)).then_inc(c_cp, 1)
                    dve.wait_ge(c_cp, v + 1)
                    dve.tensor_reduce(mx2, cut(sc2[cv], b=8, k=S), AX.X, ALU.max).then_inc(c_mx, 1)
                if has_x:
                    rope2_q(u, c, 0, not has_y)
                if has_y:
                    dve.wait_ge(c_ex, v + 1)
                    dve.tensor_reduce(sm2, cut(p2, b=8, k=S), AX.X, ALU.add).then_inc(c_sum, 1)
                    dve.wait_ge(c_sum, v + 1)
                    dve.reciprocal(sm2, sm2).then_inc(c_rc, 1)
                if has_x:
                    rope2_q(u, c, 1, not has_y)
                if has_y:
                    dve.wait_ge(c_ph, v + 1)
                    low(pT2[1], banks[3][:].rearrange("p (i n) -> p i n", i=2), pT2[0], c_pl)
                if has_x:
                    rope2_k(u, c, not has_y)
                    low(v2[c % 2][1], banks[2][:].rearrange("p (i n) -> p i n", i=2)[:, :, D2:2 * D2],
                        v2[c % 2][0], c_vl)
                    if c == UN - 1 and not (isinstance(g, int) and g == G2 - 1):
                        w_qkv(g + 1)
                    turn_low(u, 0)
                if has_y:
                    for s in range(2):
                        dve.wait_ge(c_ah, 2 * v + s + 1)
                        at = [w.rearrange("p h (i s q) -> p s i h q", i=2, s=2)[:, s] for w in at2]
                        low(at[1], banks[6 + s][:].rearrange("p (i h q) -> p i h q", i=2, h=HG), at[0], c_al)
                if has_x:
                    turn_low(u, 1)

                def accumulate(i):
                    dve.wait_ge(c_wo, 2 * v + i + 1)
                    y = res[:, 2 * cv + i, :]
                    dve.tensor_tensor(y, banks[6 + i][:], y, ALU.add).then_inc(c_acc, 1)

                if has_y:
                    accumulate(0)
                if has_x:
                    turn_low(u, 2)
                if has_y:
                    accumulate(1)
                if has_y and has_x and c == 0:
                    w_out(g)

            dve.wait_ge(d_cs, 16 * T)
            dve.wait_ge(d_mask, 32)
            dve.wait_ge(c_init, UN)
            w_qkv(0)
            w_out(0)
            slot(0, 0, 0, has_y=False)
            for c in range(1, UN):
                slot(c, 0, c)
            slot(UN, 1, 0)
            with dve.Fori(1, G2 - 1) as g:
                for c in range(1, UN + 1):
                    slot(UN * g + c, g + c // UN, c % UN)
            for c in range(1, UN):
                slot(U - UN + c, G2 - 1, c)
            slot(U, G2, 0, has_x=False)

            def low_weights():
                for c in range(EC):
                    dve.wait_ge(f_wh, c + 1)
                    low(fwT[1][:, c, :], banks[c][:], fwT[0][:, c, :], f_wl)
                dve.wait_ge(f_wh, EC + 1)
                low(fcT[1], banks[4][:, 0:EC * NC].rearrange("p (c n) -> p c n", c=EC), fcT[0], f_wl)

            def stats(y, t, n):
                dve.bn_stats(st6b, y).then_inc(f_st, 1)
                dve.wait_ge(f_st, 2 * n + 1)
                dve.bn_aggr(mv8[:, 2 * t:2 * t + 2], st6b).then_inc(f_st, 1)
                dve.wait_ge(f_st, 2 * n + 2)

            def variances():
                dve.tensor_scalar(var8, mv8.rearrange("p (t k) -> p k t", k=2)[:, 1, :], EPS, None,
                                  ALU.add).then_inc(f_var, 1)

            dve.wait_ge(c_acc, 2 * U)
            for t in range(T):
                stats(res[:, t, :], t, t)
            variances()
            low_weights()
            dve.wait_ge(f_pow, 1)

            def norm_tile(t):
                if t >= 2:
                    dve.wait_ge(f_xc, t - 1)
                    dve.wait_ge(f_xT, t - 1)
                dve.tensor_scalar(x3n[t % 2], res[:, t, :], mv8[:, 2 * t:2 * t + 1], rstd8[:, t:t + 1],
                                  ALU.subtract, ALU.mult).then_inc(f_xn, 1)

            norm_tile(0)
            norm_tile(1)
            dve.wait_ge(d_fc, 48)
            for t in range(T):
                dve.wait_ge(f_xh, t + 1)
                if t >= 2:
                    dve.wait_ge(f_dots, t - 1)
                low(x3T[t % 2][1], banks[t % 2][:].rearrange("p (c n) -> p c n", c=EC), x3T[t % 2][0], f_xl)
                if t + 2 < T:
                    norm_tile(t + 2)
                dve.wait_ge(f_dense, t + 1)
                dve.tensor_tensor(dense[:, t, :], banks[2 + t % 2][:], bias_b, ALU.add).then_inc(f_dn, 1)

            n = 0

            def step(ins):
                nonlocal n
                n += 1
                ins.then_inc(f_v, 1)
                dve.wait_ge(f_v, n)

            d3 = cut(dots, t=T, k=NC)
            dve.wait_ge(f_dots, T)
            step(dve.tensor_reduce(qsel, cut(banks[5][:], t=T, k=NC), AX.X, ALU.max))
            step(dve.tensor_tensor(d3, cut(banks[5][:], t=T, k=NC), bcast(qsel, 2, NC), ALU.subtract))
            dve.wait_ge(f_ex, 1)
            step(dve.tensor_reduce(var8, d3, AX.X, ALU.add))
            step(dve.reciprocal(var8, var8))
            step(dve.tensor_tensor(d3, d3, bcast(var8, 2, NC), ALU.mult))
            step(dve.tensor_scalar(hits, dots, THRESHOLD, None, ALU.is_gt))
            step(dve.tensor_reduce(any_hit, hits.rearrange("p (t k) -> p k t", t=T), AX.X, ALU.max))
            step(dve.tensor_reduce(qsel, cut(hits, t=T, k=NC), AX.X, ALU.max))
            step(dve.tensor_copy(assign_f, assign_i))
            dve.wait_ge(f_g, 1)
            step(dve.tensor_copy(cid, pos_i[0:NC, 0:1]))
            step(dve.tensor_scalar(onehot, assign_f, cid, None, ALU.is_equal))
            dve.wait_ge(f_cnt, 1)
            dve.tensor_scalar(cluster_hit[0:NC, :], banks[6][0:NC, 0:P], 0.5, None, ALU.is_gt).then_inc(f_rs, 1)
            dve.wait_ge(f_cnt, 2)
            step(dve.tensor_copy(row_sel, banks[7][:]))
            dve.wait_ge(f_xc, T)
            for t in range(T):
                step(dve.tensor_tensor(dense[:, t, :], dense[:, t, :], row_sel, ALU.mult))
                step(dve.scalar_tensor_tensor(res[:, t, :], dense[:, t, :], qsel[:, t:t + 1], res[:, t, :],
                                              ALU.mult, ALU.add))
                stats(res[:, t, :], t, T + t)
            variances()
            dve.wait_ge(f_pow, 2)
            for t in range(T):
                if t >= 2:
                    dve.wait_ge(d_out[t % 2], 16 * (t // 2))
                dve.tensor_scalar(y_out[t % 2], res[:, t, :], mv8[:, 2 * t:2 * t + 1], rstd8[:, t:t + 1],
                                  ALU.subtract, ALU.mult).then_inc(f_y, 1)


_INS = ["x", "ctx_4096", "pos_BxS2", "mask_BxSxS2_ik0", "L0_attn_Wq", "L0_attn_Wk", "L0_attn_Wv", "L0_attn_Wo",
        "L0_xattn_Wq", "L0_xattn_Wk", "L0_xattn_Wv", "L0_xattn_Wo",
        "L0_ffn_weight", "L0_ffn_bias", "L0_ffn_centroids", "L0_ffn_assignments"]


def _constants():
    import numpy as np

    q, k = np.arange(P)[:, None] % S, np.arange(S)[None, :]
    inv1 = np.float32(1.0) / np.float32(10000.0) ** (np.arange(0, D1, 2, dtype=np.float32) / np.float32(D1))
    ang1 = (np.arange(P) % S).astype(np.float32)[:, None] * inv1[None, :]
    inv2 = np.float32(1.0) / np.float32(10000.0) ** (np.arange(0, D2, 2, dtype=np.float32) / np.float32(D2))
    ang2 = np.arange(512, dtype=np.float32)[:, None] * inv2[None, :]
    return {
        "c_ident": np.eye(P, dtype=np.float32),
        "c_causal": (q >= k).astype(np.int32),
        "c_rope1": np.concatenate([np.repeat(np.cos(ang1), 2, 1), np.sin(ang1)], 1).astype(np.float32),
        "c_rope2": np.concatenate([np.cos(ang2), np.sin(ang2)], 1).astype(np.float32),
    }


def kernel(**inputs):
    import numpy as _np
    import concourse.bacc as _bacc
    from concourse import mybir as _mybir
    from concourse.bass_utils import run_bass_kernel_spmd as _run

    nc = _bacc.Bacc("TRN2", target_bir_lowering=False, num_devices=1)
    arrays, args = {}, []
    flat = {"x": (B * S, E), "ctx_4096": (B * S, E)}
    for name in _INS:
        a = _np.ascontiguousarray(inputs[name])
        if name in flat:
            a = a.reshape(flat[name])
        if name == "pos_BxS2":
            a = _np.ascontiguousarray(a.reshape(T, P).T)
        arrays[f"in_{name}"] = a
    for name, a in _constants().items():
        arrays[f"in_{name}"] = a
    for name, a in arrays.items():
        args.append(nc.dram_tensor(name, a.shape, _mybir.dt.from_np(a.dtype), kind="ExternalInput").ap())
    out = nc.dram_tensor("out_0", (B * S, E), F32, kind="ExternalOutput").ap()
    decoder_layer(nc, *args, out)
    r = _run(nc, [arrays], core_ids=[0])
    return r.results[0]["out_0"].reshape(B, S, E)
```

```python
from contextlib import ExitStack

import concourse.bass as bass
from concourse import mybir

F32 = mybir.dt.float32
F32R = mybir.dt.float32r
I32 = mybir.dt.int32
ALU = mybir.AluOpType
ACT = mybir.ActivationFunctionType
AX = mybir.AxisListType

P = 128
B, S, E = 16, 64, 512
T = B * S // P
EC = E // P
H1, G1, D1 = 32, 8, 16
KV1 = G1 * D1
SCALE1 = 1.0 / D1 ** 0.5
NEG1 = -1e38
H2, G2, D2 = 32, 8, 128
HG = H2 // G2
SCALE2 = 1.0 / D2 ** 0.5
NEG2 = -1e9 * D2 ** 0.5
UN = 4
U = G2 * UN
NC = 64
THRESHOLD, INV_TEMPERATURE = 0.01, 10.0
EPS = 1e-5


def bcast(ap, axis, n):
    v = ap.unsqueeze(axis)
    shape = list(v.shape)
    shape[axis] = n
    return v.broadcast_to(shape)


def decoder_layer(nc, x, ctx_in, pos, mask, w1q, w1k, w1v, w1o, w2q, w2k, w2v, w2o,
                  fw, fbias, fcent, fassign, c_ident, c_causal, c_rope1, c_rope2, out):
    stack = ExitStack()
    with stack:
        def sb(name, n, dt=F32, p=P):
            return stack.enter_context(nc.sbuf_tensor(name, [p, n], dt))

        def sem(name):
            return stack.enter_context(nc.semaphore(name))

        arena_r = sb("arena_r", 8192 + 25088, F32R)
        arena_f = sb("arena_f", 5120 + 4096 + 1024 + 6144)
        ident = sb("ident", P)
        causal = sb("causal", S, I32)
        mask_i = sb("mask_i", B * S, I32)
        pos_i = sb("pos_i", T, I32)
        rope1 = sb("rope1", 24)
        small = sb("small", 256)

        class Carver:
            def __init__(self, arena, at):
                self.arena, self.at = arena, at

            def take(self, n):
                v = self.arena[:, self.at:self.at + n]
                self.at += n
                return v

        def parts(carver, n):
            return [carver.take(n), carver.take(n)]

        def cut(ap, **kw):
            names = list(kw)
            return ap.rearrange(f"p ({' '.join(names)}) -> p {' '.join(names)}", **kw)

        r = Carver(arena_r, 0)
        xT = [cut(v, c=EC, n=B * S) for v in parts(r, EC * B * S)]
        r1, r2, r3 = (Carver(arena_r, r.at) for _ in range(3))
        f = Carver(arena_f, 0)
        raw = f.take(5120)
        res = cut(f.take(T * E), t=T, n=E)
        cs = cut(f.take(T * P), t=T, n=P)
        f1, f2, f3 = (Carver(arena_f, f.at) for _ in range(3))

        w1 = [cut(v, c=EC, n=E + 2 * KV1) for v in parts(r1, EC * (E + 2 * KV1))]
        w1out = [cut(v, c=HG, n=E) for v in parts(r1, HG * E)]
        xt = [cut(v, c=EC, n=P) for v in parts(r1, EC * P)]
        stack_q = cut(r1.take(H1 * 64), h=H1, r=64)
        stack_k = cut(r1.take(G1 * 128), g=G1, r=128)
        qT1 = cut(r1.take(16 * P), b=2, j=16, q=S)
        kT1 = cut(r1.take(G1 * P), g=G1, n=P)
        vpad = parts(r1, G1 * (P + D1))
        pT1 = [cut(v, g=G1, a=2, n=P) for v in parts(r1, G1 * 2 * P)]
        at1 = [cut(v, a=4, b=2, q=S) for v in parts(r1, 4 * P)]
        x_st = f1.take(E)
        t1q, t2q = f1.take(E), f1.take(E)
        t1k, t2k = f1.take(KV1), f1.take(KV1)
        sc1 = [f1.take(512), f1.take(512)]
        p1 = [f1.take(512) for _ in range(4)]
        x1n = f1.take(E)
        v_raw = f1.take(KV1)
        w1_raw = cut(raw[:, 0:EC * (E + 2 * KV1)], c=EC, n=E + 2 * KV1)
        w1out_raw = cut(raw[:, EC * (E + 2 * KV1):5120], c=HG, n=E)

        cT = [cut(v, c=EC, n=B * S) for v in parts(r2, EC * B * S)]
        r3.at = r2.at
        w2q_s = [cut(v, c=EC, n=HG * D2) for v in parts(r2, EC * HG * D2)]
        w2kv_s = [cut(v, c=EC, n=2 * D2) for v in parts(r2, EC * 2 * D2)]
        w2o_s = [cut(v, h=HG, n=E) for v in parts(r2, HG * E)]
        qT2 = [cut(v, b=4, h=HG, q=S) for v in parts(r2, HG * 2 * P)]
        kT2 = parts(r2, 2 * P)
        v2 = [[cut(v, i=2, n=D2) for v in parts(r2, 2 * D2)] for _ in range(2)]
        pT2 = [cut(v, i=2, n=2 * P) for v in parts(r2, 4 * P)]
        at2 = [cut(v, h=HG, n=2 * P) for v in parts(r2, HG * 2 * P)]
        ctx_raw = cut(f2.take(T * E), t=T, n=E)
        sc2 = [f2.take(512) for _ in range(UN)]
        f2b = Carver(arena_f, f1.at - 5504)
        u1q = [f2b.take(512), f2b.take(512)]
        u2q = [f2b.take(512), f2b.take(512)]
        u1k, u2k = f2b.take(256), f2b.take(256)
        p2 = f2b.take(512)
        w2q_raw = cut(raw[:, 0:2048], c=EC, n=512)
        w2kv_raw = cut(raw[:, 2048:3072], c=EC, n=256)
        w2o_raw = cut(raw[:, 3072:5120], h=HG, n=E)

        fwT = [cut(v, c=EC, n=E) for v in parts(r3, EC * E)]
        fcT = [cut(v, c=EC, n=NC) for v in parts(r3, EC * NC)]
        masked = [f3.take(E), f3.take(E)]
        y_out = [f3.take(E), f3.take(E)]
        fw_raw = cut(raw[:, 0:2048], c=EC, n=E)
        fc_raw = raw[0:NC, 2048:2560]
        bias_b = raw[:, 2560:3072]
        onehot = raw[0:NC, 3072:3584]
        row_sel = raw[:, 3584:4096]
        assign_f = raw[0:NC, 4096:4608]
        dots = raw[:, 4608:5120]
        assign_i = mask_i[0:NC, 0:E]
        hits = mask_i[:, E:2 * E].bitcast(F32)

        mx1 = [small[:, 8 * u:8 * u + 8] for u in range(4)]
        sm1 = [small[:, 32 + 8 * u:40 + 8 * u] for u in range(4)]
        mx2, sm2 = small[:, 64:72], small[:, 72:80]
        st6, mv, rstd, half = small[:, 80:86], small[:, 86:88], small[:, 88:89], small[:, 89:90]
        mv8, rstd8, half8, var8 = small[:, 96:112], small[:, 112:120], small[:, 120:128], small[:, 128:136]
        qsel = small[:, 136:144]
        any_hit = small[:, 144:208]
        cid = small[0:NC, 208:209]
        tot8 = small[:, 224:232]
        st6b = small[:, 216:222]

        banks = [stack.enter_context(nc.psum_tensor(f"bank{i}", [P, 512], F32)) for i in range(8)]
        cluster_hit = sb("cluster_hit", P, F32)
        ones = sb("ones", P)

        d_w1, d_w1o, d_x, d_const, d_res = sem("d_w1"), sem("d_w1o"), sem("d_x"), sem("d_const"), sem("d_res")
        d_pos, d_cs = sem("d_pos"), sem("d_cs")
        d_mask, d_ctx = sem("d_mask"), sem("d_ctx")
        d_w2q, d_w2kv, d_w2o = sem("d_w2q"), sem("d_w2kv"), sem("d_w2o")
        d_fw, d_fc, d_out = sem("d_fw"), sem("d_fc"), [sem("d_out0"), sem("d_out1")]
        s_w1h, s_w1l, s_init, s_dinit = sem("s_w1h"), sem("s_w1l"), sem("s_init"), sem("s_dinit")
        s_gate = sem("s_gate")
        s_xT, s_xh, s_xl = sem("s_xT"), sem("s_xh"), sem("s_xl")
        s_q, s_kv = sem("s_q"), sem("s_kv")
        s_rq, s_rk, s_qs, s_ks = sem("s_rq"), sem("s_rk"), sem("s_qs"), sem("s_ks")
        s_qh, s_ql, s_kh, s_kl = sem("s_qh"), sem("s_ql"), sem("s_kh"), sem("s_kl")
        s_vr, s_vh, s_vl = sem("s_vr"), sem("s_vh"), sem("s_vl")
        s_qk, s_qke = sem("s_qk"), sem("s_qke")
        s_s, s_cp, s_mx, s_sub = sem("s_s"), sem("s_cp"), sem("s_mx"), sem("s_sub")
        s_ex, s_sum, s_rc, s_pn = sem("s_ex"), sem("s_sum"), sem("s_rc"), sem("s_pn")
        s_pt, s_ph, s_pl = sem("s_pt"), sem("s_ph"), sem("s_pl")
        s_pv, s_ah, s_al, s_wo = sem("s_pv"), sem("s_ah"), sem("s_al"), sem("s_wo")
        s_res, s_ln, s_lp, s_x1n = sem("s_res"), sem("s_ln"), sem("s_lp"), sem("s_x1n")
        s_x1c, s_x1T, s_x1h, s_x1l = sem("s_x1c"), sem("s_x1T"), sem("s_x1h"), sem("s_x1l")
        c_init, c_xT, c_xh, c_xl = sem("c_init"), sem("c_xT"), sem("c_xh"), sem("c_xl")
        c_wqh, c_wql, c_wkh, c_wkl = sem("c_wqh"), sem("c_wql"), sem("c_wkh"), sem("c_wkl")
        c_woh, c_wol = sem("c_woh"), sem("c_wol")
        c_q, c_kv, c_rq, c_rk, c_qs, c_ks = (sem(n) for n in ("c_q", "c_kv", "c_rq", "c_rk", "c_qs", "c_ks"))
        c_vh, c_vl, c_tr, c_trh, c_trl = (sem(n) for n in ("c_vh", "c_vl", "c_tr", "c_trh", "c_trl"))
        c_s, c_cp, c_mx, c_sub, c_ex = (sem(n) for n in ("c_s", "c_cp", "c_mx", "c_sub", "c_ex"))
        c_sum, c_rc, c_pn, c_pt, c_ph, c_pl = (sem(n) for n in ("c_sum", "c_rc", "c_pn", "c_pt", "c_ph", "c_pl"))
        c_pv, c_ah, c_al, c_wo, c_acc = (sem(n) for n in ("c_pv", "c_ah", "c_al", "c_wo", "c_acc"))
        f_wT, f_wh, f_wl, f_st, f_var, f_pow, f_xn, f_hit = (
            sem(n) for n in ("f_wT", "f_wh", "f_wl", "f_st", "f_var", "f_pow", "f_xn", "f_hit"))
        f_sel, f_m, f_r = sem("f_sel"), sem("f_m"), sem("f_r")
        f_xT, f_xh, f_xl, f_dots, f_dense, f_dn = (
            sem(n) for n in ("f_xT", "f_xh", "f_xl", "f_dots", "f_dense", "f_dn"))
        f_v, f_p, f_cnt, f_rs, f_ex, f_y, f_g = (sem(n) for n in ("f_v", "f_p", "f_cnt", "f_rs", "f_ex", "f_y", "f_g"))

        PASSES = ((0, 0), (0, 1), (1, 0))

        def stages(u):
            return (u >= 1, u >= 2) if isinstance(u, int) else (True, True)

        def f32(ap):
            return ap.bitcast(F32)

        block = stack.enter_context(nc.Block())

        @block.sync
        def _(sp):
            def load_x(t):
                sp.dma_start(x_st, x[bass.ds(t * P, P), :]).then_inc(d_x, 16)

            sp.dma_start(x_st, x[0:P, :]).then_inc(d_x, 16)
            sp.dma_start(ident[:], c_ident).then_inc(d_const, 16)
            sp.dma_start(causal[:], c_causal).then_inc(d_const, 16)
            sp.dma_start(rope1[:], c_rope1).then_inc(d_const, 16)
            for w, at, n in ((w1q, 0, E), (w1k, E, KV1), (w1v, E + KV1, KV1)):
                sp.dma_start(w1_raw[:, :, at:at + n], w.rearrange("(c p) n -> p c n", p=P)).then_inc(d_w1, 16)
            w1o_v = w1o.rearrange("(g h d) n -> g d h n", g=G1, h=HG)
            for g in range(G1):
                sp.dma_start(w1out_raw[D1 * g:D1 * g + D1, :, :], w1o_v[g]).then_inc(d_w1o, 16)
            sp.dma_start(res, x.rearrange("(t p) n -> p t n", p=P)).then_inc(d_res, 16)
            sp.dma_start(pos_i[:], pos).then_inc(d_pos, 16)
            for i in range(2):
                sp.dma_start(mask_i[S * i:S * i + S, :].rearrange("q (b k) -> q b k", b=B),
                             mask.rearrange("b q k -> q b k")).then_inc(d_mask, 16)

            def next_x(t):
                sp.wait_ge(s_xT, t)
                load_x(t)
            with sp.Fori(1, T) as t:
                next_x(t)

            sp.wait_ge(s_x1l, T)
            sp.wait_ge(s_x1c, T)
            sp.dma_start(ctx_raw, ctx_in.rearrange("(t p) n -> p t n", p=P)).then_inc(d_ctx, 16)

            wq_v = w2q.rearrange("(c p) n -> p c n", p=P)
            wk_v = w2k.rearrange("(c p) n -> p c n", p=P)
            wv_v = w2v.rearrange("(c p) n -> p c n", p=P)

            def load_q(g):
                sp.dma_start(w2q_raw, wq_v[:, :, bass.ds(g * HG * D2, HG * D2)]).then_inc(d_w2q, 16)

            def load_kv(g):
                sp.dma_start(w2kv_raw[:, :, 0:D2], wk_v[:, :, bass.ds(g * D2, D2)]).then_inc(d_w2kv, 16)
                sp.dma_start(w2kv_raw[:, :, D2:2 * D2], wv_v[:, :, bass.ds(g * D2, D2)]).then_inc(d_w2kv, 16)

            def load_o(g):
                sp.dma_start(w2o_raw, w2o[bass.ds(g * HG * D2, HG * D2), :].rearrange("(h p) n -> p h n", p=P)
                             ).then_inc(d_w2o, 16)
            load_q(0)
            load_kv(0)
            load_o(0)
            with sp.Fori(0, G2 - 1) as g:
                sp.wait_ge(c_wql, 4 * g + 4)
                load_q(g + 1)
                sp.wait_ge(c_wkl, 2 * g + 2)
                load_kv(g + 1)
                sp.wait_ge(c_wol, 4 * g + 4)
                load_o(g + 1)

            sp.wait_ge(c_wql, 4 * G2)
            sp.dma_start(fw_raw, fw.rearrange("(c p) n -> p c n", p=P)).then_inc(d_fw, 16)
            sp.wait_ge(c_wkl, 2 * G2)
            sp.dma_start(fc_raw, fcent).then_inc(d_fc, 16)
            sp.dma_start(bias_b, fbias.rearrange("(o n) -> o n", o=1).broadcast_to([P, E])).then_inc(d_fc, 16)
            sp.wait_ge(c_cp, U - 2)
            sp.dma_start(assign_i, fassign.rearrange("(o n) -> o n", o=1).broadcast_to([NC, E])).then_inc(d_fc, 16)

            out_v = out.rearrange("(t p) n -> t p n", p=P)
            for t in range(T):
                sp.wait_ge(f_y, t + 1)
                sp.dma_start(out_v[t], y_out[t % 2]).then_inc(d_out[t % 2], 16)
            for i in range(2):
                sp.wait_ge(d_out[i], 16 * (T // 2))

        @block.tensor
        def _(pe):
            def product(bank, lhs, rhs, chunks, inc=None):
                for c in range(chunks):
                    for n, (a, b) in enumerate(PASSES):
                        mm = pe.matmul(bank, lhs(a, c), rhs(b, c), start=(c == 0 and n == 0),
                                       stop=(c == chunks - 1 and n == 2))
                return mm

            TX, BQ, BKV, TR, SB, BO = banks[0], banks[1], banks[2], banks[3:5], banks[5:7], banks[7]

            def a_stage(t):
                for c in range(EC):
                    mm = pe.transpose(TX[:, c * P:(c + 1) * P], x_st[:, c * P:(c + 1) * P], ident[:])
                mm.then_inc(s_xT, 1)

            def b_stage(t):
                product(BQ[:], lambda a, c: xt[a][:, c, :], lambda b, c: w1[b][:, c, 0:E], EC).then_inc(s_q, 1)
                product(BKV[:, 0:2 * KV1], lambda a, c: xt[a][:, c, :],
                        lambda b, c: w1[b][:, c, E:E + 2 * KV1], EC).then_inc(s_kv, 1)

            def pt_stage(v, u):
                if u < 2:
                    pe.wait_ge(s_qke, 6 * v + 5 + u)
                else:
                    pe.wait_ge(s_pl, 4 * v + u - 1)
                pe.wait_ge(s_pn, 4 * v + u + 1)
                for i in range(4):
                    mm = pe.transpose(TR[u % 2][:, i * P:(i + 1) * P], p1[u][:, i * P:(i + 1) * P], ident[:])
                mm.then_inc(s_pt, 1)

            def pv_stage(v, half_, first, last):
                for g in range(4 * half_, 4 * half_ + 4):
                    for n, (a, b) in enumerate(PASSES):
                        for i in range(2):
                            rows = slice(S * i, S * i + S)
                            mm = pe.matmul((BO, BKV)[i][:, 0:2 * P], vpad[a][rows, g * P:(g + 1) * P],
                                           pT1[b][rows, g, :, :].rearrange("p a n -> p (a n)"),
                                           start=(g == 0 and n == 0), stop=(g == G1 - 1 and n == 2))
                if last:
                    mm.then_inc(s_pv, 1)

            def qk_stage(t, first):
                pe.wait_ge(s_ql, t + 1)
                pe.wait_ge(s_kl, t + 1)
                for j, (kind, n) in enumerate((("q", 0), ("q", 1), ("k", 0), ("q", 2), ("q", 3), ("k", 1))):
                    if j >= 2:
                        pe.wait_ge(s_qke, 6 * t + j - 1)
                    elif not first:
                        pe.wait_ge(s_pl, 4 * t - 1 + j)
                    for i in range(4):
                        m = 4 * n + i
                        src = f32(stack_q[:, 2 * m:2 * m + 2, :].rearrange("p h r -> p (h r)")) \
                            if kind == "q" else f32(stack_k[:, m, :])
                        mm = pe.transpose(TR[j % 2][:, i * P:(i + 1) * P], src, ident[:])
                    mm.then_inc(s_qk, 1)

            def wo_stage(v, first):
                pe.wait_ge(s_al, v + 1)
                if not first:
                    pe.wait_ge(s_x1l, v)
                product(TX[:], lambda a, c: at1[a][:, c, :, :].rearrange("p b q -> p (b q)"),
                        lambda b, c: w1out[b][:, 2 * (c % 2) + c // 2, :], 4).then_inc(s_wo, 1)

            def s_stage(t, first):
                for u in range(4):
                    if u % 2 == 0:
                        pe.wait_ge(s_qke, 6 * t + 3 + 3 * (u // 2))
                    if u >= 2 or not first:
                        pe.wait_ge(s_cp, 4 * t + u - 1)
                    rows = slice(S * (u % 2), S * (u % 2) + S)
                    for i in range(4):
                        g = 4 * (u // 2) + i
                        for b in range(2):
                            mm = pe.matmul(SB[u % 2][:, (2 * i + b) * S:(2 * i + b + 1) * S],
                                           qT1[rows, b, 2 * g:2 * g + 2, :].rearrange("p j q -> p (j q)"),
                                           kT1[rows, g, b * S:(b + 1) * S], start=True, stop=True)
                    mm.then_inc(s_s, 1)

            def x1_stage(v, last):
                pe.wait_ge(s_x1n, v + 1)
                pe.wait_ge(s_xl, T if last else v + 3)
                for c in range(EC):
                    mm = pe.transpose(TX[:, c * P:(c + 1) * P], x1n[:, c * P:(c + 1) * P], ident[:])
                mm.then_inc(s_x1T, 1)

            def tile_steps(t, first=False, last=False, second=False):
                v = t - 1
                pe.wait_ge(s_xl, t + 1)
                if not first:
                    pe.wait_ge(s_rq, t)
                    if not second:
                        pe.wait_ge(s_al, v)
                b_stage(t)
                if not first:
                    pt_stage(v, 0)
                    pt_stage(v, 1)
                    pe.wait_ge(s_vl, v + 1)
                    pe.wait_ge(s_rk, t + 1)
                    pe.wait_ge(s_vr, t + 1)
                    pe.wait_ge(s_pl, 4 * v + 2)
                    pv_stage(v, 0, first, False)
                    pt_stage(v, 2)
                    pt_stage(v, 3)
                    pe.wait_ge(s_pl, 4 * v + 4)
                    pv_stage(v, 1, first, True)
                qk_stage(t, first)
                if not first:
                    wo_stage(v, second)
                s_stage(t, first)
                if not last:
                    pe.wait_ge(d_x, 16 * (t + 2))
                    if not first:
                        pe.wait_ge(s_res, t)
                    else:
                        pe.wait_ge(s_xl, 1)
                    a_stage(t + 1)
                if not first:
                    x1_stage(v, last)

            pe.wait_ge(d_const, 48)
            pe.wait_ge(d_x, 16)
            a_stage(0)
            pe.wait_ge(s_w1l, 2)
            pe.wait_ge(s_init, 3)
            tile_steps(0, first=True)
            tile_steps(1, second=True)
            with pe.Fori(2, T - 1) as t:
                tile_steps(t)
            tile_steps(T - 1, last=True)
            v = T - 1
            pt_stage(v, 0)
            pt_stage(v, 1)
            pe.wait_ge(s_vl, T)
            pe.wait_ge(s_al, v)
            pe.wait_ge(s_pl, 4 * v + 2)
            pv_stage(v, 0, False, False)
            pt_stage(v, 2)
            pt_stage(v, 3)
            pe.wait_ge(s_pl, 4 * v + 4)
            pv_stage(v, 1, False, True)
            wo_stage(v, False)
            x1_stage(v, True)

            pe.wait_ge(s_x1l, T)
            pe.wait_ge(d_ctx, 16)
            CT = banks[0:4]
            for t in range(T):
                if t >= 4:
                    pe.wait_ge(c_xl, t - 3)
                for c in range(EC):
                    mm = pe.transpose(CT[t % 4][:, c * P:(c + 1) * P], ctx_raw[:, t, c * P:(c + 1) * P], ident[:])
                mm.then_inc(c_xT, 1)
            pe.wait_ge(c_xl, T)

            BQ2, BKV2, TR2, BS2, BO2 = banks[0:2], banks[2], banks[3:5], banks[5], banks[6:8]

            def q_proj(u, c, i, first):
                if not first:
                    pe.wait_ge(c_rq, 2 * u + i - 1)
                tok = slice((2 * c + i) * P, (2 * c + i + 1) * P)
                product(BQ2[i][:], lambda a, e: xT[a][:, e, tok], lambda b, e: w2q_s[b][:, e, :], EC
                        ).then_inc(c_q, 1)

            def kv_proj(u, c, i, first):
                if i == 0 and not first:
                    pe.wait_ge(c_rk, u)
                    pe.wait_ge(c_vl, u)
                tok = slice((2 * c + i) * P, (2 * c + i + 1) * P)
                mm = product(BKV2[:, 256 * i:256 * i + 256], lambda a, e: cT[a][:, e, tok],
                             lambda b, e: w2kv_s[b][:, e, :], EC)
                if i == 1:
                    mm.then_inc(c_kv, 1)

            def p_turn(v):
                pe.wait_ge(c_trl, 3 * v + 2)
                pe.wait_ge(c_pn, v + 1)
                for i in range(2):
                    for h in range(2):
                        mm = pe.transpose(TR2[0][:, (2 * i + h) * P:(2 * i + h + 1) * P],
                                          p2[:, (2 * h + i) * P:(2 * h + i + 1) * P], ident[:])
                mm.then_inc(c_pt, 1)

            def pv(v, c, first):
                pe.wait_ge(c_pl, v + 1)
                pe.wait_ge(c_vl, v + 1)
                if not first:
                    pe.wait_ge(c_acc, 2 * v)
                for s in range(2):
                    rows = slice(S * s, S * s + S)
                    for i in range(2):
                        for n, (a, b) in enumerate(PASSES):
                            mm = pe.matmul(BO2[s][:, 256 * i:256 * i + 256], v2[c % 2][a][rows, i, :],
                                           pT2[b][rows, i, :], start=(n == 0), stop=(n == 2))
                    mm.then_inc(c_pv, 1)

            def q_turn(u, i, first):
                if i == 0:
                    if not first:
                        pe.wait_ge(c_trl, 3 * u)
                elif not first:
                    pe.wait_ge(c_pl, u)
                pe.wait_ge(c_qs, 2 * u + i + 1)
                for h in range(HG):
                    mm = pe.transpose(TR2[1 - i][:, h * P:(h + 1) * P], u1q[i][:, h * P:(h + 1) * P], ident[:])
                mm.then_inc(c_tr, 1)

            def k_turn(u):
                pe.wait_ge(c_trl, 3 * u + 1)
                pe.wait_ge(c_ks, u + 1)
                for i in range(2):
                    mm = pe.transpose(TR2[1][:, i * P:(i + 1) * P], u1k[:, i * P:(i + 1) * P], ident[:])
                mm.then_inc(c_tr, 1)

            def out_proj(i, heads):
                for h in heads:
                    for n, (a, b) in enumerate(PASSES):
                        mm = pe.matmul(BO2[i][:], at2[a][:, h, i * P:(i + 1) * P], w2o_s[b][:, h, :],
                                       start=(h == 0 and n == 0), stop=(h == HG - 1 and n == 2))
                if heads[-1] == HG - 1:
                    mm.then_inc(c_wo, 1)

            def scores(u, first):
                pe.wait_ge(c_trl, 3 * u + 3)
                if not first:
                    pe.wait_ge(c_cp, u)
                for h in range(2):
                    for b in range(4):
                        at = (4 * h + b) * S
                        for n, (a, k) in enumerate(PASSES):
                            mm = pe.matmul(BS2[:, at:at + S], qT2[a][:, b, 2 * h:2 * h + 2, :].rearrange("p h q -> p (h q)"),
                                           kT2[k][:, b * S:(b + 1) * S], start=(n == 0), stop=(n == 2))
                mm.then_inc(c_s, 1)

            def slot(u, g, c):
                old, oldest = stages(u)
                v = u - 1
                if oldest:
                    out_proj(1, range(HG))
                pe.wait_ge(c_wql, 4 * g + 4)
                q_proj(u, c, 0, not old)
                q_proj(u, c, 1, not old)
                if old:
                    p_turn(v)
                q_turn(u, 0, not old)
                pe.wait_ge(c_wkl, 2 * g + 2)
                kv_proj(u, c, 0, not old)
                if old:
                    pv(v, (c - 1) % UN, not oldest)
                kv_proj(u, c, 1, not old)
                q_turn(u, 1, not old)
                if old:
                    pe.wait_ge(c_al, 2 * v + 2)
                    pe.wait_ge(c_wol, 4 * (g if c > 0 else g - 1) + 4)
                    out_proj(0, range(HG - 1))
                k_turn(u)
                if old:
                    out_proj(0, range(HG - 1, HG))
                scores(u, not old)

            for u in range(UN + 1):
                slot(u, u // UN, u % UN)
            with pe.Fori(1, G2 - 1) as g:
                for c in range(1, UN + 1):
                    slot(UN * g + c, g + c // UN, c % UN)
            for u in range(U - UN + 1, U):
                slot(u, u // UN, u % UN)

            v = U - 1
            out_proj(1, range(HG))
            WT = (banks[0], banks[1], banks[2], banks[4])
            pe.wait_ge(d_fw, 16)
            pe.wait_ge(c_rq, 2 * U)
            pe.wait_ge(c_rk, U)
            pe.wait_ge(c_vl, U)
            for c in range(EC):
                for j in range(EC):
                    mm = pe.transpose(WT[c][:, j * P:(j + 1) * P], fw_raw[:, j, c * P:(c + 1) * P], ident[:])
                mm.then_inc(f_wT, 1)
            p_turn(v)
            pe.wait_ge(d_fc, 16 * 3)
            pe.wait_ge(f_wl, 1)
            for c in range(EC):
                mm = pe.transpose(banks[0][:, c * NC:(c + 1) * NC], fc_raw[:, c * P:(c + 1) * P], ident[0:NC, 0:NC])
            mm.then_inc(f_wT, 1)
            pv(v, v % UN, False)

            def x3_turn(t):
                pe.wait_ge(f_xn, t + 1)
                if t < 2:
                    pe.wait_ge(f_wl, t + 2)
                else:
                    pe.wait_ge(f_xl, t - 1)
                for c in range(EC):
                    mm = pe.transpose(banks[1 + t % 2][:, c * P:(c + 1) * P], res[:, t, c * P:(c + 1) * P], ident[:])
                mm.then_inc(f_xT, 1)

            def cluster_dots(t):
                pe.wait_ge(f_xl, t + 1)
                product(banks[5][:, t * NC:(t + 1) * NC], lambda a, c: xT[a][:, c, t * P:(t + 1) * P],
                        lambda b, c: fcT[b][:, c, :], EC).then_inc(f_dots, 1)

            DB = (banks[3], banks[4], banks[6], banks[7], banks[1], banks[2])

            def dense(t):
                if t >= len(DB):
                    pe.wait_ge(f_dn, t - len(DB) + 1)
                product(DB[t % len(DB)][:], lambda a, c: xT[a][:, c, t * P:(t + 1) * P],
                        lambda b, c: fwT[b][:, c, :], EC).then_inc(f_dense, 1)

            x3_turn(0)
            x3_turn(1)
            pe.wait_ge(c_al, 2 * v + 2)
            pe.wait_ge(c_wol, 4 * G2)
            out_proj(0, range(HG))
            x3_turn(2)
            out_proj(1, range(HG))
            x3_turn(3)
            pe.wait_ge(f_wl, EC + 1)
            for t in range(2):
                cluster_dots(t)
            for t in range(2, 6):
                x3_turn(t + 2)
                cluster_dots(t)
            dense(0)
            cluster_dots(6)
            cluster_dots(7)
            dense(1)
            pe.wait_ge(c_acc, 2 * U)
            dense(2)
            pe.wait_ge(f_hit, 1)
            pe.wait_ge(s_dinit, 4)
            pe.matmul(banks[0][0:NC, 0:P], any_hit, ones[:], start=True, stop=True).then_inc(f_cnt, 1)
            dense(3)
            pe.wait_ge(f_rs, 1)
            pe.matmul(banks[0][:], cluster_hit[0:NC, :], onehot, start=True, stop=True).then_inc(f_cnt, 1)
            for t in range(4, T):
                dense(t)

        @block.scalar
        def _(act):
            def copy(dst, src, done):
                act.activation(dst, src, ACT.Copy).then_inc(done, 1)

            act.wait_ge(s_xT, 1)
            copy(xt[0], banks[0][:].rearrange("p (c n) -> p c n", c=EC), s_xh)
            act.wait_ge(d_w1, 48)
            copy(w1[0], w1_raw, s_w1h)
            act.wait_ge(d_w1o, 16 * G1)
            copy(w1out[0], w1out_raw, s_w1h)

            def p_high(v, u, first):
                act.wait_ge(s_pt, 4 * v + u + 1)
                if u == 0 and not first:
                    act.wait_ge(s_pv, v)
                copy(pT1[0][:, 4 * (u // 2):4 * (u // 2) + 4, u % 2, :],
                     banks[3 + u % 2][:].rearrange("p (g n) -> p g n", g=4), s_ph)

            def at_high(v, first):
                act.wait_ge(s_pv, v + 1)
                if not first:
                    act.wait_ge(s_wo, v)
                for i, bank in enumerate((banks[7], banks[2])):
                    copy(at1[0][:, :, i, :], bank[:, 0:2 * P].rearrange("p (a q) -> p a q", a=4), s_ah)

            def tile_steps(t, first=False, last=False, tail=False, second=False):
                v = t - 1
                if not tail:
                    act.wait_ge(s_kv, t + 1)
                    if not first:
                        act.wait_ge(s_vl, t)
                    copy(v_raw, banks[2][:, KV1:2 * KV1], s_vr)
                if not first:
                    p_high(v, 0, second)
                    p_high(v, 1, second)
                if not tail:
                    act.wait_ge(s_qs, t + 1)
                    if not first:
                        act.wait_ge(s_qk, 6 * t)
                    copy(stack_q.rearrange("p h (a b d) -> p h a b d", a=2, b=2)[:, :, 0],
                         bcast(t1q.rearrange("p (h d) -> p h d", h=H1), 2, 2), s_qh)
                    act.wait_ge(s_ks, t + 1)
                    copy(stack_k.rearrange("p g (a b d) -> p g a b d", a=4, b=2)[:, :, :, 0],
                         bcast(t1k.rearrange("p (g d) -> p g d", g=G1), 2, 4), s_kh)
                if not first:
                    p_high(v, 2, second)
                    p_high(v, 3, second)
                    at_high(v, second)
                if not tail:
                    copy(vpad[0].rearrange("p (g n) -> p g n", g=G1)[:, :, 0:D1],
                         v_raw.rearrange("p (g d) -> p g d", g=G1), s_vh)
                    n_q = n_k = 0
                    if not first:
                        act.wait_ge(s_s, 4 * t)
                    for j, kind in enumerate("qqkqqk"):
                        act.wait_ge(s_qk, 6 * t + j + 1)
                        src = banks[3 + j % 2][:].rearrange("p (g n) -> p g n", g=4)
                        if kind == "q":
                            copy(qT1[:, :, 4 * n_q:4 * n_q + 4, :].rearrange("p b j q -> p j b q"),
                                 src.rearrange("p g (b q) -> p g b q", b=2), s_qke)
                            n_q += 1
                        else:
                            copy(kT1[:, 4 * n_k:4 * n_k + 4, :], src, s_qke)
                            n_k += 1
                if not first:
                    act.wait_ge(s_x1n, v + 1)
                    copy(res[:, bass.ds(v, 1), :].rearrange("p t n -> p (t n)"), x1n, s_x1c)

                def expo(u):
                    act.wait_ge(s_sub, 4 * t + u + 1)
                    act.activation(p1[u], p1[u], ACT.Exp, scale=SCALE1).then_inc(s_ex, 1)

                if not tail:
                    expo(0)
                    expo(1)
                    if not last:
                        act.wait_ge(s_xT, t + 2)
                        copy(xt[0], banks[0][:].rearrange("p (c n) -> p c n", c=EC), s_xh)
                    expo(2)
                if not first:
                    act.wait_ge(s_x1T, v + 1)
                    copy(xT[0][:, :, bass.ds(v * P, P)], banks[0][:].rearrange("p (c n) -> p c n", c=EC), s_x1h)
                if not tail:
                    expo(3)

            act.wait_ge(s_init, 3)
            act.wait_ge(d_res, 16)
            tile_steps(0, first=True)
            tile_steps(1, second=True)
            with act.Fori(2, T - 1) as t:
                tile_steps(t)
            tile_steps(T - 1, last=True)
            tile_steps(T, tail=True)

            act.wait_ge(s_x1l, T)
            for t in range(T):
                act.wait_ge(c_xT, t + 1)
                copy(cT[0][:, :, t * P:(t + 1) * P], banks[t % 4][:].rearrange("p (c n) -> p c n", c=EC), c_xh)

            def wq_high(g, c):
                act.wait_ge(d_w2q, 16 * (g + 1))
                copy(w2q_s[0][:, c, :], w2q_raw[:, c, :], c_wqh)

            def wkv_high(g, i):
                act.wait_ge(d_w2kv, 32 * (g + 1))
                copy(w2kv_s[0][:, 2 * i:2 * i + 2, :], w2kv_raw[:, 2 * i:2 * i + 2, :], c_wkh)

            def wo_high(g, h):
                act.wait_ge(d_w2o, 16 * (g + 1))
                copy(w2o_s[0][:, h, :], w2o_raw[:, h, :], c_woh)

            def turn_high(u, n):
                act.wait_ge(c_tr, 3 * u + n + 1)
                if n < 2:
                    copy(qT2[0][:, 2 * n:2 * n + 2].rearrange("p b h q -> p h b q"),
                         cut(banks[4 - n][:], h=HG, b=2, q=S), c_trh)
                else:
                    copy(kT2[0], banks[4][:, 0:2 * P], c_trh)

            def at2_high(v, s):
                act.wait_ge(c_pv, 2 * v + s + 1)
                copy(at2[0].rearrange("p h (i s q) -> p s i h q", i=2, s=2)[:, s],
                     banks[6 + s][:].rearrange("p (i h q) -> p i h q", i=2, h=HG), c_ah)

            def slot(u, g, c):
                old, oldest = stages(u)
                v = u - 1
                split = c == UN - 1 and not (isinstance(g, int) and g == G2 - 1)
                if old:
                    act.wait_ge(c_sub, v + 1)
                    act.activation(p2, p2, ACT.Exp, scale=SCALE2).then_inc(c_ex, 1)
                if oldest and c == 1:
                    act.wait_ge(c_wo, 2 * v)
                    for h in range(HG):
                        wo_high(g, h)
                if old:
                    act.wait_ge(c_pt, v + 1)
                    if oldest:
                        act.wait_ge(c_pv, 2 * v)
                    copy(pT2[0], banks[3][:].rearrange("p (i n) -> p i n", i=2), c_ph)
                if old:
                    act.wait_ge(c_s, u)
                turn_high(u, 0)
                if split:
                    act.wait_ge(c_q, 2 * u + 2)
                    wq_high(g + 1, 0)
                    wq_high(g + 1, 1)
                if old:
                    if oldest:
                        act.wait_ge(c_wo, 2 * v)
                    at2_high(v, 0)
                    at2_high(v, 1)
                if split:
                    wq_high(g + 1, 2)
                act.wait_ge(c_kv, u + 1)
                copy(v2[c % 2][0], banks[2][:].rearrange("p (i n) -> p i n", i=2)[:, :, D2:2 * D2], c_vh)
                turn_high(u, 1)
                turn_high(u, 2)
                if split:
                    wq_high(g + 1, 3)
                    wkv_high(g + 1, 0)
                    wkv_high(g + 1, 1)

            for n in range(4):
                wq_high(0, n)
            wkv_high(0, 0)
            wkv_high(0, 1)
            for n in range(4):
                wo_high(0, n)
            for u in range(UN + 1):
                slot(u, u // UN, u % UN)
            with act.Fori(1, G2 - 1) as g:
                for c in range(1, UN + 1):
                    slot(UN * g + c, g + c // UN, c % UN)
            for u in range(U - UN + 1, U):
                slot(u, u // UN, u % UN)

            v = U - 1
            act.wait_ge(c_sub, v + 1)
            act.activation(p2, p2, ACT.Exp, scale=SCALE2).then_inc(c_ex, 1)

            def fw_high(c):
                act.wait_ge(f_wT, c + 1)
                copy(fwT[0][:, c, :], banks[(0, 1, 2, 4)[c]][:], f_wh)

            def x3_high(t):
                act.wait_ge(f_xT, t + 1)
                copy(xT[0][:, :, t * P:(t + 1) * P], banks[1 + t % 2][:].rearrange("p (c n) -> p c n", c=EC), f_xh)

            fw_high(0)
            fw_high(1)
            act.wait_ge(c_pt, v + 1)
            act.wait_ge(c_pv, 2 * v)
            copy(pT2[0], banks[3][:].rearrange("p (i n) -> p i n", i=2), c_ph)
            fw_high(2)
            fw_high(3)
            act.wait_ge(f_wT, EC + 1)
            copy(fcT[0], banks[0][:, 0:EC * NC].rearrange("p (c n) -> p c n", c=EC), f_wh)
            act.wait_ge(c_wo, 2 * v)
            at2_high(v, 0)
            at2_high(v, 1)
            for t in range(T):
                x3_high(t)
            act.wait_ge(f_v, 5)
            act.activation(dots, dots, ACT.Exp, scale=INV_TEMPERATURE).then_inc(f_ex, 1)

        @block.gpsimd
        def _(pool):
            pool.memset(f32(vpad[0]), 0.0).then_inc(s_init, 1)
            pool.memset(f32(vpad[1]), 0.0).then_inc(s_init, 1)
            pool.memset(half[:], -0.5).then_inc(s_init, 1)
            pool.memset(half8, -0.5).then_inc(s_dinit, 1)
            pool.memset(ones[:], 1.0).then_inc(s_dinit, 1)
            for i in range(2):
                pool.memset(sc1[i], NEG1).then_inc(s_dinit, 1)
            pool.wait_ge(d_pos, 16)
            for t in range(T):
                pool.indirect_dma_start(cs[:, t, :], None, c_rope2,
                                        bass.IndirectOffsetOnAxis(ap=pos_i[:, t:t + 1], axis=0)).then_inc(d_cs, 16)

            def rope_sum(t):
                pool.wait_ge(s_rq, t + 1)
                pool.tensor_tensor(t1q, t1q, t2q, ALU.add).then_inc(s_qs, 1)
                pool.wait_ge(s_rk, t + 1)
                pool.tensor_tensor(t1k, t1k, t2k, ALU.add).then_inc(s_ks, 1)

            def sub(t, u, first):
                pool.wait_ge(s_mx, 4 * t + u + 1)
                if not first:
                    pool.wait_ge(s_pt, 4 * t + u - 3)
                pool.tensor_tensor(cut(p1[u], b=8, k=S), cut(sc1[u % 2], b=8, k=S), bcast(mx1[u], 2, S),
                                   ALU.subtract).then_inc(s_sub, 1)

            def norm(t, u):
                pool.wait_ge(s_rc, 4 * t + u + 1)
                pool.tensor_tensor(cut(p1[u], b=8, k=S), cut(p1[u], b=8, k=S), bcast(sm1[u], 2, S),
                                   ALU.mult).then_inc(s_pn, 1)

            def ln(v):
                pool.wait_ge(s_ln, 3 * v + 3)
                pool.tensor_tensor(rstd, mv[:, 1:2], half, ALU.pow).then_inc(s_lp, 1)

            def tile_steps(t, first=False, tail=False):
                if not tail:
                    rope_sum(t)
                if not first:
                    ln(t - 1)
                if not tail:
                    sub(t, 0, first)
                    sub(t, 1, first)
                    norm(t, 0)
                    sub(t, 2, first)
                    norm(t, 1)
                    sub(t, 3, first)
                    norm(t, 2)
                    norm(t, 3)

            pool.wait_ge(s_init, 3)
            tile_steps(0, first=True)
            with pool.Fori(1, T) as t:
                tile_steps(t)
            tile_steps(T, tail=True)

            pool.wait_ge(s_x1l, T)
            for i in range(UN):
                pool.memset(sc2[i], NEG2).then_inc(c_init, 1)

            def sum_q(u, i):
                pool.wait_ge(c_rq, 2 * u + i + 1)
                pool.tensor_tensor(u1q[i], u1q[i], u2q[i], ALU.add).then_inc(c_qs, 1)

            def wq_low(g, c):
                pool.wait_ge(c_wqh, 4 * g + c + 1)
                pool.tensor_tensor(w2q_s[1][:, c, :], w2q_raw[:, c, :], f32(w2q_s[0][:, c, :]),
                                   ALU.subtract).then_inc(c_wql, 1)

            def wkv_low(g, i):
                cs_ = slice(2 * i, 2 * i + 2)
                pool.wait_ge(c_wkh, 2 * g + i + 1)
                pool.tensor_tensor(w2kv_s[1][:, cs_, :], w2kv_raw[:, cs_, :], f32(w2kv_s[0][:, cs_, :]),
                                   ALU.subtract).then_inc(c_wkl, 1)

            def wo_low(g, h):
                pool.wait_ge(c_woh, 4 * g + h + 1)
                pool.tensor_tensor(w2o_s[1][:, h, :], w2o_raw[:, h, :], f32(w2o_s[0][:, h, :]),
                                   ALU.subtract).then_inc(c_wol, 1)

            def softmax_steps(v, c, before):
                pool.wait_ge(c_mx, v + 1)
                if before:
                    pool.wait_ge(c_pt, v)
                pool.tensor_tensor(cut(p2, b=8, k=S), cut(sc2[c], b=8, k=S), bcast(mx2, 2, S),
                                   ALU.subtract).then_inc(c_sub, 1)
                pool.wait_ge(c_rc, v + 1)
                pool.tensor_tensor(cut(p2, b=8, k=S), cut(p2, b=8, k=S), bcast(sm2, 2, S),
                                   ALU.mult).then_inc(c_pn, 1)

            def slot(u, g, c):
                old, oldest = stages(u)
                v = u - 1
                split = c == UN - 1 and not (isinstance(g, int) and g == G2 - 1)
                split_o = oldest and c == 1
                if old:
                    softmax_steps(v, (c - 1) % UN, oldest)
                if split_o:
                    wo_low(g, 0)
                sum_q(u, 0)
                if split_o:
                    wo_low(g, 1)
                sum_q(u, 1)
                if split_o:
                    wo_low(g, 2)
                    wo_low(g, 3)
                if split:
                    for n in range(3):
                        wq_low(g + 1, n)
                pool.wait_ge(c_rk, u + 1)
                pool.tensor_tensor(u1k, u1k, u2k, ALU.add).then_inc(c_ks, 1)
                if split:
                    wq_low(g + 1, 3)
                    wkv_low(g + 1, 0)
                    wkv_low(g + 1, 1)

            for u in range(UN + 1):
                slot(u, u // UN, u % UN)
            with pool.Fori(1, G2 - 1) as g:
                for c in range(1, UN + 1):
                    slot(UN * g + c, g + c // UN, c % UN)
            pool.iota(pos_i[0:NC, 0:1], pattern=[[0, 1]], base=0,
                      channel_multiplier=1).then_inc(f_g, 1)

            def root(t, n):
                pool.wait_ge(f_var, n + 1)
                pool.tensor_tensor(rstd8[:, t:t + 1], var8[:, t:t + 1], half8[:, 0:1], ALU.pow).then_inc(f_pow, 1)

            for u in range(U - UN + 1, U):
                slot(u, u // UN, u % UN)
                if u >= U - 2:
                    root(2 * (u - U + 2), 2 * (u - U + 2))
                    root(2 * (u - U + 2) + 1, 2 * (u - U + 2) + 1)

            softmax_steps(U - 1, (U - 1) % UN, True)
            for t in range(4, T):
                root(t, t)
            for t in range(T + 1):
                if t < T:
                    pool.wait_ge(f_dn, t + 1)
                    pool.wait_ge(f_sel, 1)
                    pool.tensor_tensor(masked[t % 2], masked[t % 2], row_sel, ALU.mult).then_inc(f_m, 1)
                if t >= 1:
                    root(t - 1, T + t - 1)

        @block.vector
        def _(dve):
            def low(dst, src, high, done):
                dve.tensor_tensor(dst, src, f32(high), ALU.subtract).then_inc(done, 1)

            def hold():
                dve.sem_inc(s_gate, 1)

            def x_low(t):
                dve.wait_ge(s_xh, t + 1)
                low(xt[1], banks[0][:].rearrange("p (c n) -> p c n", c=EC), xt[0], s_xl)

            def rope_q(t, first):
                q = banks[1][:].rearrange("p (h d) -> p h d", h=H1)
                t1, t2 = (v.rearrange("p (h d) -> p h d", h=H1) for v in (t1q, t2q))
                dve.wait_ge(s_q, t + 1)
                if not first:
                    dve.wait_ge(s_ql, t)
                dve.tensor_tensor(t1, q, bcast(rope1[:, 0:D1], 1, H1), ALU.mult)
                sin = bcast(rope1[:, D1:D1 + 8], 1, H1)
                dve.scalar_tensor_tensor(t2[:, :, 0:D1:2], q[:, :, 1:D1:2], -1.0, sin, ALU.mult, ALU.mult)
                dve.tensor_tensor(t2[:, :, 1:D1:2], q[:, :, 0:D1:2], sin, ALU.mult).then_inc(s_rq, 1)

            def rope_k(t, first):
                k = banks[2][:, 0:KV1].rearrange("p (h d) -> p h d", h=G1)
                t1, t2 = (v.rearrange("p (h d) -> p h d", h=G1) for v in (t1k, t2k))
                dve.wait_ge(s_kv, t + 1)
                dve.wait_ge(s_vr, t + 1)
                if not first:
                    dve.wait_ge(s_kl, t)
                dve.tensor_tensor(t1, k, bcast(rope1[:, 0:D1], 1, G1), ALU.mult)
                sin = bcast(rope1[:, D1:D1 + 8], 1, G1)
                dve.scalar_tensor_tensor(t2[:, :, 0:D1:2], k[:, :, 1:D1:2], -1.0, sin, ALU.mult, ALU.mult)
                dve.tensor_tensor(t2[:, :, 1:D1:2], k[:, :, 0:D1:2], sin, ALU.mult).then_inc(s_rk, 1)

            def p_low(v, u):
                dve.wait_ge(s_ph, 4 * v + u + 1)
                gs = slice(4 * (u // 2), 4 * (u // 2) + 4)
                low(pT1[1][:, gs, u % 2, :], banks[3 + u % 2][:].rearrange("p (g n) -> p g n", g=4),
                    pT1[0][:, gs, u % 2, :], s_pl)

            def stack_low(t):
                dve.wait_ge(s_qh, t + 1)
                sq = stack_q.rearrange("p h (a b d) -> p h a b d", a=2, b=2)
                low(sq[:, :, 1], bcast(t1q.rearrange("p (h d) -> p h d", h=H1), 2, 2), sq[:, :, 0], s_ql)
                dve.wait_ge(s_kh, t + 1)
                sk = stack_k.rearrange("p g (a b d) -> p g a b d", a=4, b=2)
                low(sk[:, :, :, 1], bcast(t1k.rearrange("p (g d) -> p g d", g=G1), 2, 4), sk[:, :, :, 0], s_kl)

            def at_low(v):
                for i, bank in enumerate((banks[7], banks[2])):
                    dve.wait_ge(s_ah, 2 * v + i + 1)
                    ins = dve.tensor_tensor(at1[1][:, :, i, :], bank[:, 0:2 * P].rearrange("p (a q) -> p a q", a=4),
                                            f32(at1[0][:, :, i, :]), ALU.subtract)
                ins.then_inc(s_al, 1)

            def v_low(t):
                dve.wait_ge(s_vh, t + 1)
                vp = [v.rearrange("p (g n) -> p g n", g=G1)[:, :, 0:D1] for v in vpad]
                low(vp[1], v_raw.rearrange("p (g d) -> p g d", g=G1), vp[0], s_vl)

            def ln(v, first):
                y = res[:, bass.ds(v, 1), :].rearrange("p t n -> p (t n)")
                dve.wait_ge(s_wo, v + 1)
                dve.tensor_tensor(y, banks[0][:], y, ALU.add).then_inc(s_res, 1)
                dve.wait_ge(s_res, v + 1)
                hold()
                dve.bn_stats(st6, y).then_inc(s_ln, 1)
                dve.wait_ge(s_ln, 3 * v + 1)
                hold()
                dve.bn_aggr(mv, st6).then_inc(s_ln, 1)
                dve.wait_ge(s_ln, 3 * v + 2)
                dve.tensor_scalar(mv[:, 1:2], mv[:, 1:2], EPS, None, ALU.add).then_inc(s_ln, 1)
                dve.wait_ge(s_lp, v + 1)
                if not first:
                    dve.wait_ge(s_x1T, v)
                    dve.wait_ge(s_x1c, v)
                dve.tensor_scalar(x1n, y, mv[:, 0:1], rstd, ALU.subtract, ALU.mult).then_inc(s_x1n, 1)

            def masked_max(t, u, first):
                dve.wait_ge(s_s, 4 * t + u + 1)
                if u >= 2 or not first:
                    dve.wait_ge(s_sub, 4 * t + u - 1)
                sc = cut(sc1[u % 2], b=8, k=S)
                hold()
                dve.copy_predicated(sc, bcast(causal[:], 1, 8), cut(banks[5 + u % 2][:], b=8, k=S)).then_inc(s_cp, 1)
                dve.wait_ge(s_cp, 4 * t + u + 1)
                dve.tensor_reduce(mx1[u], sc, AX.X, ALU.max).then_inc(s_mx, 1)

            def total(t, u):
                dve.wait_ge(s_ex, 4 * t + u + 1)
                dve.tensor_reduce(sm1[u], cut(p1[u], b=8, k=S), AX.X, ALU.add).then_inc(s_sum, 1)
                dve.wait_ge(s_sum, 4 * t + u + 1)
                dve.reciprocal(sm1[u], sm1[u]).then_inc(s_rc, 1)

            def tile_steps(t, first=False, last=False, tail=False, second=False):
                v = t - 1
                if not tail:
                    rope_q(t, first)
                    rope_k(t, first)
                if not first:
                    p_low(v, 0)
                    p_low(v, 1)
                if not tail:
                    stack_low(t)
                if not first:
                    p_low(v, 2)
                    p_low(v, 3)
                    at_low(v)
                if not tail:
                    v_low(t)
                if not first:
                    ln(v, second)
                if not tail:
                    masked_max(t, 0, first)
                    masked_max(t, 1, first)
                    total(t, 0)
                    masked_max(t, 2, first)
                    total(t, 1)
                    if not last:
                        x_low(t + 1)
                    masked_max(t, 3, first)
                    total(t, 2)
                if not first:
                    dve.wait_ge(s_x1h, v + 1)
                    low(xT[1][:, :, bass.ds(v * P, P)], banks[0][:].rearrange("p (c n) -> p c n", c=EC),
                        xT[0][:, :, bass.ds(v * P, P)], s_x1l)
                if not tail:
                    total(t, 3)

            x_low(0)
            dve.wait_ge(s_w1h, 1)
            low(w1[1], w1_raw, w1[0], s_w1l)
            dve.wait_ge(s_w1h, 2)
            low(w1out[1], w1out_raw, w1out[0], s_w1l)
            dve.wait_ge(d_const, 48)
            dve.wait_ge(s_dinit, 4)
            dve.wait_ge(s_init, 3)
            dve.wait_ge(d_res, 16)
            tile_steps(0, first=True)
            tile_steps(1, second=True)
            with dve.Fori(2, T - 1) as t:
                tile_steps(t)
            tile_steps(T - 1, last=True)
            tile_steps(T, tail=True)

            for t in range(T):
                dve.wait_ge(c_xh, t + 1)
                low(cT[1][:, :, t * P:(t + 1) * P], banks[t % 4][:].rearrange("p (c n) -> p c n", c=EC),
                    cT[0][:, :, t * P:(t + 1) * P], c_xl)

            def w_low(part, raw_, n, high_done, low_done):
                for c in range(n):
                    cs_ = slice(c * EC // n, (c + 1) * EC // n)
                    dve.wait_ge(high_done, c + 1)
                    low(part[1][:, cs_, :], raw_[:, cs_, :], part[0][:, cs_, :], low_done)

            def rope2_q(u, c, i, first):
                dve.wait_ge(c_q, 2 * u + i + 1)
                if not first:
                    dve.wait_ge(c_tr, 3 * u + i - 2)
                q = banks[i][:].rearrange("p (h f d) -> p h f d", h=HG, f=2)
                t1, t2 = (w[i].rearrange("p (h f d) -> p h f d", h=HG, f=2) for w in (u1q, u2q))
                cos = bcast(bcast(cs[:, 2 * c + i, 0:64], 1, 2), 1, HG)
                sin = bcast(cs[:, 2 * c + i, 64:128], 1, HG)
                dve.tensor_tensor(t1, q, cos, ALU.mult)
                dve.scalar_tensor_tensor(t2[:, :, 0, :], q[:, :, 1, :], -1.0, sin, ALU.mult, ALU.mult)
                dve.tensor_tensor(t2[:, :, 1, :], q[:, :, 0, :], sin, ALU.mult).then_inc(c_rq, 1)

            def rope2_k(u, c, first):
                dve.wait_ge(c_kv, u + 1)
                dve.wait_ge(c_vh, u + 1)
                if not first:
                    dve.wait_ge(c_tr, 3 * u)
                k = banks[2][:].rearrange("p (i n) -> p i n", i=2)[:, :, 0:D2].rearrange("p i (f d) -> p i f d", f=2)
                t1, t2 = (w.rearrange("p (i f d) -> p i f d", i=2, f=2) for w in (u1k, u2k))
                cos = bcast(cs[:, 2 * c:2 * c + 2, 0:64], 2, 2)
                sin = cs[:, 2 * c:2 * c + 2, 64:128]
                dve.tensor_tensor(t1, k, cos, ALU.mult)
                dve.scalar_tensor_tensor(t2[:, :, 0, :], k[:, :, 1, :], -1.0, sin, ALU.mult, ALU.mult)
                dve.tensor_tensor(t2[:, :, 1, :], k[:, :, 0, :], sin, ALU.mult).then_inc(c_rk, 1)

            def turn_low(u, n):
                dve.wait_ge(c_trh, 3 * u + n + 1)
                if n < 2:
                    high, lo_ = (w[:, 2 * n:2 * n + 2].rearrange("p b h q -> p h b q") for w in qT2)
                    low(lo_, cut(banks[4 - n][:], h=HG, b=2, q=S), high, c_trl)
                else:
                    low(kT2[1], banks[4][:, 0:2 * P], kT2[0], c_trl)

            def accumulate(v, c, i):
                dve.wait_ge(c_wo, 2 * v + i + 1)
                y = res[:, 2 * c + i, :]
                dve.tensor_tensor(y, banks[6 + i][:], y, ALU.add).then_inc(c_acc, 1)
                if isinstance(v, int) and v >= U - UN:
                    dve.wait_ge(c_acc, 2 * v + i + 1)
                    stats(2 * c + i, 2 * c + i)

            def stats(t, n):
                hold()
                dve.bn_stats(st6b, res[:, t, :]).then_inc(f_st, 1)
                dve.wait_ge(f_st, 2 * n + 1)
                hold()
                dve.bn_aggr(mv8[:, 2 * t:2 * t + 2], st6b).then_inc(f_st, 1)
                dve.wait_ge(f_st, 2 * n + 2)
                dve.tensor_scalar(var8[:, t:t + 1], mv8[:, 2 * t + 1:2 * t + 2], EPS, None, ALU.add).then_inc(f_var, 1)

            def masked_max2(v, c):
                sc = sc2[c].rearrange("p (h n) -> p h n", h=2)
                dve.wait_ge(c_s, v + 1)
                hold()
                dve.copy_predicated(sc, bcast(mask_i[:, c * 4 * S:(c + 1) * 4 * S], 1, 2),
                                    banks[5][:].rearrange("p (h n) -> p h n", h=2)).then_inc(c_cp, 1)
                dve.wait_ge(c_cp, v + 1)
                dve.tensor_reduce(mx2, cut(sc2[c], b=8, k=S), AX.X, ALU.max).then_inc(c_mx, 1)

            def total2(v):
                dve.wait_ge(c_ex, v + 1)
                dve.tensor_reduce(sm2, cut(p2, b=8, k=S), AX.X, ALU.add).then_inc(c_sum, 1)
                dve.wait_ge(c_sum, v + 1)
                dve.reciprocal(sm2, sm2).then_inc(c_rc, 1)

            def p2_low(v):
                dve.wait_ge(c_ph, v + 1)
                low(pT2[1], banks[3][:].rearrange("p (i n) -> p i n", i=2), pT2[0], c_pl)

            def at2_low(v):
                for s in range(2):
                    dve.wait_ge(c_ah, 2 * v + s + 1)
                    at = [w.rearrange("p h (i s q) -> p s i h q", i=2, s=2)[:, s] for w in at2]
                    low(at[1], banks[6 + s][:].rearrange("p (i h q) -> p i h q", i=2, h=HG), at[0], c_al)

            def slot(u, g, c):
                old, oldest = stages(u)
                v = u - 1
                cv = (c - 1) % UN
                if old:
                    masked_max2(v, cv)
                if oldest:
                    accumulate(u - 2, (c - 2) % UN, 1)
                if old:
                    total2(v)
                rope2_q(u, c, 0, not old)
                rope2_q(u, c, 1, not old)
                if old:
                    p2_low(v)
                turn_low(u, 0)
                if old:
                    at2_low(v)
                rope2_k(u, c, not old)
                low(v2[c % 2][1], banks[2][:].rearrange("p (i n) -> p i n", i=2)[:, :, D2:2 * D2],
                    v2[c % 2][0], c_vl)
                turn_low(u, 1)
                turn_low(u, 2)
                if old:
                    accumulate(v, cv, 0)

            dve.wait_ge(d_cs, 16 * T)
            dve.wait_ge(d_mask, 32)
            dve.wait_ge(c_init, UN)
            w_low(w2q_s, w2q_raw, 4, c_wqh, c_wql)
            w_low(w2kv_s, w2kv_raw, 2, c_wkh, c_wkl)
            w_low(w2o_s, w2o_raw, 4, c_woh, c_wol)
            for u in range(UN + 1):
                slot(u, u // UN, u % UN)
            with dve.Fori(1, G2 - 1) as g:
                for c in range(1, UN + 1):
                    slot(UN * g + c, g + c // UN, c % UN)
            for u in range(U - UN + 1, U):
                slot(u, u // UN, u % UN)

            def norm_tile(t):
                dve.wait_ge(f_pow, t + 1)
                dve.tensor_scalar(res[:, t, :], res[:, t, :], mv8[:, 2 * t:2 * t + 1], rstd8[:, t:t + 1],
                                  ALU.subtract, ALU.mult).then_inc(f_xn, 1)

            def fw_low(c):
                dve.wait_ge(f_wh, c + 1)
                low(fwT[1][:, c, :], banks[(0, 1, 2, 4)[c]][:], fwT[0][:, c, :], f_wl)

            def x3_low(t):
                dve.wait_ge(f_xh, t + 1)
                at = slice(t * P, (t + 1) * P)
                low(xT[1][:, :, at], banks[1 + t % 2][:].rearrange("p (c n) -> p c n", c=EC), xT[0][:, :, at], f_xl)

            v, c = U - 1, UN - 1
            norm_tile(0)
            norm_tile(1)
            masked_max2(v, c)
            accumulate(v - 1, c - 1, 1)
            total2(v)
            fw_low(0)
            fw_low(1)
            p2_low(v)
            norm_tile(2)
            norm_tile(3)
            fw_low(2)
            fw_low(3)
            at2_low(v)
            dve.wait_ge(f_wh, EC + 1)
            low(fcT[1], banks[0][:, 0:EC * NC].rearrange("p (c n) -> p c n", c=EC), fcT[0], f_wl)
            x3_low(0)
            x3_low(1)
            norm_tile(4)
            norm_tile(5)
            accumulate(v, c, 0)
            x3_low(2)
            norm_tile(6)
            accumulate(v, c, 1)
            x3_low(3)

            n = 0

            def step(ins):
                nonlocal n
                n += 1
                ins.then_inc(f_v, 1)
                dve.wait_ge(f_v, n)

            dve.wait_ge(f_g, 1)
            dve.wait_ge(d_fc, 48)
            dve.wait_ge(c_wol, 4 * G2)
            norm_tile(7)
            step(dve.tensor_copy(assign_f, assign_i))
            x3_low(4)
            step(dve.tensor_copy(cid, pos_i[0:NC, 0:1]))
            x3_low(5)
            step(dve.tensor_scalar(onehot, assign_f, cid, None, ALU.is_equal))
            x3_low(6)
            x3_low(7)

            d3 = cut(dots, t=T, k=NC)
            dve.wait_ge(f_dots, T)
            step(dve.tensor_reduce(qsel, cut(banks[5][:], t=T, k=NC), AX.X, ALU.max))
            step(dve.tensor_tensor(d3, cut(banks[5][:], t=T, k=NC), bcast(qsel, 2, NC), ALU.subtract))
            dve.wait_ge(f_ex, 1)
            step(dve.tensor_reduce(tot8, d3, AX.X, ALU.add))
            step(dve.reciprocal(tot8, tot8))
            step(dve.tensor_tensor(d3, d3, bcast(tot8, 2, NC), ALU.mult))
            step(dve.tensor_scalar(hits, dots, THRESHOLD, None, ALU.is_gt))
            dve.tensor_reduce(any_hit, hits.rearrange("p (t k) -> p k t", t=T), AX.X, ALU.max).then_inc(f_hit, 1)
            step(dve.tensor_reduce(qsel, cut(hits, t=T, k=NC), AX.X, ALU.max))
            dve.wait_ge(f_cnt, 1)
            dve.tensor_scalar(cluster_hit[0:NC, :], banks[0][0:NC, 0:P], 0.5, None, ALU.is_gt).then_inc(f_rs, 1)
            dve.wait_ge(f_cnt, 2)
            dve.tensor_copy(row_sel, banks[0][:]).then_inc(f_sel, 1)

            DB = (banks[3], banks[4], banks[6], banks[7], banks[1], banks[2])
            for t in range(T + 2):
                if t < T:
                    dve.wait_ge(f_dense, t + 1)
                    if t >= 2:
                        dve.wait_ge(f_r, t - 1)
                    dve.tensor_tensor(masked[t % 2], DB[t % len(DB)][:], bias_b, ALU.add).then_inc(f_dn, 1)
                if 1 <= t <= T:
                    dve.wait_ge(f_m, t)
                    dve.scalar_tensor_tensor(res[:, t - 1, :], masked[(t - 1) % 2], qsel[:, t - 1:t], res[:, t - 1, :],
                                             ALU.mult, ALU.add).then_inc(f_r, 1)
                    dve.wait_ge(f_r, t)
                    stats(t - 1, T + t - 1)
                if t >= 2:
                    w = t - 2
                    dve.wait_ge(f_pow, T + w + 1)
                    if w >= 2:
                        dve.wait_ge(d_out[w % 2], 16 * (w // 2))
                    dve.tensor_scalar(y_out[w % 2], res[:, w, :], mv8[:, 2 * w:2 * w + 1], rstd8[:, w:w + 1],
                                      ALU.subtract, ALU.mult).then_inc(f_y, 1)


_INS = ["x", "ctx_4096", "pos_BxS2", "mask_BxSxS2_ik0", "L0_attn_Wq", "L0_attn_Wk", "L0_attn_Wv", "L0_attn_Wo",
        "L0_xattn_Wq", "L0_xattn_Wk", "L0_xattn_Wv", "L0_xattn_Wo",
        "L0_ffn_weight", "L0_ffn_bias", "L0_ffn_centroids", "L0_ffn_assignments"]


def _constants():
    import numpy as np

    q, k = np.arange(P)[:, None] % S, np.arange(S)[None, :]
    inv1 = np.float32(1.0) / np.float32(10000.0) ** (np.arange(0, D1, 2, dtype=np.float32) / np.float32(D1))
    ang1 = (np.arange(P) % S).astype(np.float32)[:, None] * inv1[None, :]
    inv2 = np.float32(1.0) / np.float32(10000.0) ** (np.arange(0, D2, 2, dtype=np.float32) / np.float32(D2))
    ang2 = np.arange(512, dtype=np.float32)[:, None] * inv2[None, :]
    return {
        "c_ident": np.eye(P, dtype=np.float32),
        "c_causal": (q >= k).astype(np.int32),
        "c_rope1": np.concatenate([np.repeat(np.cos(ang1), 2, 1), np.sin(ang1)], 1).astype(np.float32),
        "c_rope2": np.concatenate([np.cos(ang2), np.sin(ang2)], 1).astype(np.float32),
    }


def kernel(**inputs):
    import numpy as _np
    import concourse.bacc as _bacc
    from concourse import mybir as _mybir
    from concourse.bass_utils import run_bass_kernel_spmd as _run

    nc = _bacc.Bacc("TRN2", target_bir_lowering=False, num_devices=1)
    arrays, args = {}, []
    flat = {"x": (B * S, E), "ctx_4096": (B * S, E)}
    for name in _INS:
        a = _np.ascontiguousarray(inputs[name])
        if name in flat:
            a = a.reshape(flat[name])
        if name == "pos_BxS2":
            a = _np.ascontiguousarray(a.reshape(T, P).T)
        arrays[f"in_{name}"] = a
    for name, a in _constants().items():
        arrays[f"in_{name}"] = a
    for name, a in arrays.items():
        args.append(nc.dram_tensor(name, a.shape, _mybir.dt.from_np(a.dtype), kind="ExternalInput").ap())
    out = nc.dram_tensor("out_0", (B * S, E), F32, kind="ExternalOutput").ap()
    decoder_layer(nc, *args, out)
    r = _run(nc, [arrays], core_ids=[0])
    return r.results[0]["out_0"].reshape(B, S, E)
```

```python
from contextlib import ExitStack

import concourse.bass as bass
from concourse import mybir

F32 = mybir.dt.float32
F32R = mybir.dt.float32r
I32 = mybir.dt.int32
ALU = mybir.AluOpType
ACT = mybir.ActivationFunctionType
AX = mybir.AxisListType

P = 128
B, S, E = 16, 64, 512
T = B * S // P
EC = E // P
H1, G1, D1 = 32, 8, 16
KV1 = G1 * D1
SCALE1 = 1.0 / D1 ** 0.5
NEG1 = -1e38
H2, G2, D2 = 32, 8, 128
HG = H2 // G2
SCALE2 = 1.0 / D2 ** 0.5
NEG2 = -1e9 * D2 ** 0.5
UN = 4
U = G2 * UN
NC = 64
THRESHOLD, INV_TEMPERATURE = 0.01, 10.0
EPS = 1e-5


def bcast(ap, axis, n):
    v = ap.unsqueeze(axis)
    shape = list(v.shape)
    shape[axis] = n
    return v.broadcast_to(shape)


def decoder_layer(nc, x, ctx_in, pos, mask, w1q, w1k, w1v, w1o, w2q, w2k, w2v, w2o,
                  fw, fbias, fcent, fassign, c_ident, c_causal, c_rope1, c_rope2, out):
    stack = ExitStack()
    with stack:
        def sb(name, n, dt=F32, p=P):
            return stack.enter_context(nc.sbuf_tensor(name, [p, n], dt))

        def sem(name):
            return stack.enter_context(nc.semaphore(name))

        arena_r = sb("arena_r", 8192 + 25088, F32R)
        arena_f = sb("arena_f", 5120 + 4096 + 1024 + 6784)
        ident = sb("ident", P)
        causal = sb("causal", S, I32)
        mask_i = sb("mask_i", B * S, I32)
        pos_i = sb("pos_i", T, I32)
        rope1 = sb("rope1", 24)
        small = sb("small", 256)

        class Carver:
            def __init__(self, arena, at):
                self.arena, self.at = arena, at

            def take(self, n):
                v = self.arena[:, self.at:self.at + n]
                self.at += n
                return v

        def parts(carver, n):
            return [carver.take(n), carver.take(n)]

        def cut(ap, **kw):
            names = list(kw)
            return ap.rearrange(f"p ({' '.join(names)}) -> p {' '.join(names)}", **kw)

        r = Carver(arena_r, 0)
        xT = [cut(v, c=EC, n=B * S) for v in parts(r, EC * B * S)]
        r1, r2, r3 = (Carver(arena_r, r.at) for _ in range(3))
        f = Carver(arena_f, 0)
        raw = f.take(5120)
        res = cut(f.take(T * E), t=T, n=E)
        cs = cut(f.take(T * P), t=T, n=P)
        f1, f2, f3 = (Carver(arena_f, f.at) for _ in range(3))

        w1 = [cut(v, c=EC, n=E + 2 * KV1) for v in parts(r1, EC * (E + 2 * KV1))]
        w1out = [cut(v, c=HG, n=E) for v in parts(r1, HG * E)]
        xt = [cut(v, c=EC, n=P) for v in parts(r1, EC * P)]
        stack_q = cut(r1.take(H1 * 64), h=H1, r=64)
        stack_k = cut(r1.take(G1 * 128), g=G1, r=128)
        qT1 = cut(r1.take(16 * P), b=2, j=16, q=S)
        kT1 = cut(r1.take(G1 * P), g=G1, n=P)
        vpad = [cut(v, b=2, n=640) for v in parts(r1, 2 * 640)]
        pT1 = [cut(v, b=2, j=4, a=2, n=P) for v in parts(r1, G1 * 2 * P)]
        at1 = [cut(v, a=4, b=2, q=S) for v in parts(r1, 4 * P)]
        x_st = f1.take(E)
        t1q, t2q = f1.take(E), f1.take(E)
        t1k, t2k = f1.take(KV1), f1.take(KV1)
        v_raw = f1.take(KV1)
        v_st = cut(f1.take(2 * G1 * D1), b=2, j=4, x=2 * D1)
        sc1 = [f1.take(512), f1.take(512)]
        p1 = [f1.take(512) for _ in range(4)]
        x1n = f1.take(E)
        w1_raw = cut(raw[:, 0:EC * (E + 2 * KV1)], c=EC, n=E + 2 * KV1)
        w1out_raw = cut(raw[:, EC * (E + 2 * KV1):5120], c=HG, n=E)

        r3.at = r2.at
        w2q_s = [cut(v, c=EC, n=HG * D2) for v in parts(r2, EC * HG * D2)]
        w2kv_s = [cut(v, c=EC, n=2 * D2) for v in parts(r2, EC * 2 * D2)]
        w2o_s = [cut(v, h=HG, n=E) for v in parts(r2, HG * E)]
        cT = [cut(v, c=EC, n=B * S) for v in parts(r2, EC * B * S)]
        qT2 = [cut(v, b=4, h=HG, q=S) for v in parts(r2, HG * 2 * P)]
        kT2 = parts(r2, 2 * P)
        v2 = [[cut(v, i=2, n=D2) for v in parts(r2, 2 * D2)] for _ in range(2)]
        pT2 = [cut(v, i=2, n=2 * P) for v in parts(r2, 4 * P)]
        at2 = [cut(v, h=HG, n=2 * P) for v in parts(r2, HG * 2 * P)]
        u1q = [f2.take(512), f2.take(512)]
        u2q = [f2.take(512), f2.take(512)]
        u1k, u2k = f2.take(256), f2.take(256)
        p2 = f2.take(512)
        sc2 = [f2.take(512) for _ in range(UN)]
        f2.at = f1.at
        ctx_st = [f2.take(E), f2.take(E)]
        w2q_raw = cut(raw[:, 0:2048], c=EC, n=512)
        w2kv_raw = cut(raw[:, 2048:3072], c=EC, n=256)
        w2o_raw = cut(raw[:, 3072:5120], h=HG, n=E)

        fwT = [cut(v, c=EC, n=E) for v in parts(r3, EC * E)]
        fcT = [cut(v, c=EC, n=NC) for v in parts(r3, EC * NC)]
        masked = [f3.take(E), f3.take(E)]
        fw_raw = cut(raw[:, 0:2048], c=EC, n=E)
        fc_raw = raw[0:NC, 2048:2560]
        bias_b = raw[:, 2560:3072]
        onehot = raw[0:NC, 3072:3584]
        row_sel = raw[:, 3584:4096]
        dots_T = [m[0:NC, :] for m in masked]
        assign_f = raw[0:NC, 4096:4608]
        dots = raw[:, 4608:5120]
        assign_i = mask_i[0:NC, 0:E]
        hits = mask_i[:, E:2 * E].bitcast(F32)

        mx1 = [small[:, 8 * u:8 * u + 8] for u in range(4)]
        sm1 = [small[:, 32 + 8 * u:40 + 8 * u] for u in range(4)]
        mx2, sm2 = small[:, 64:72], small[:, 72:80]
        st6, mv, rstd, half = small[:, 80:86], small[:, 86:88], small[:, 88:89], small[:, 89:90]
        mv8, rstd8, half8, var8 = small[:, 96:112], small[:, 112:120], small[:, 120:128], small[:, 128:136]
        qsel = small[:, 136:144]
        any_hit = small[:, 144:208]
        cid = small[0:NC, 208:209]
        tot8, nmean = small[:, 224:232], small[:, 232:240]
        st6b = small[:, 216:222]

        banks = [stack.enter_context(nc.psum_tensor(f"bank{i}", [P, 512], F32)) for i in range(8)]
        cluster_hit = sb("cluster_hit", P, F32)
        ones = sb("ones", P)

        d_w1q, d_w1kv = [sem(f"d_w1q{c}") for c in range(EC)], sem("d_w1kv")
        d_ident, d_w1o, d_x, d_const, d_res = sem("d_ident"), sem("d_w1o"), sem("d_x"), sem("d_const"), sem("d_res")
        d_pos, d_cs = sem("d_pos"), sem("d_cs")
        d_mask, d_ctx, d_v = sem("d_mask"), [sem("d_ctx0"), sem("d_ctx1")], sem("d_v")
        d_w2q, d_w2kv, d_w2o = sem("d_w2q"), sem("d_w2kv"), sem("d_w2o")
        d_fw, d_fc, d_out = sem("d_fw"), sem("d_fc"), sem("d_out")
        s_w1h, s_w1l, s_init, s_dinit = sem("s_w1h"), sem("s_w1l"), sem("s_init"), sem("s_dinit")
        s_w1oh, s_w1ol = sem("s_w1oh"), sem("s_w1ol")
        s_gate = sem("s_gate")
        s_xT, s_xh, s_xl = sem("s_xT"), sem("s_xh"), sem("s_xl")
        s_q, s_kv = sem("s_q"), sem("s_kv")
        s_rq, s_rk, s_qs, s_ks = sem("s_rq"), sem("s_rk"), sem("s_qs"), sem("s_ks")
        s_qh, s_ql, s_kh, s_kl = sem("s_qh"), sem("s_ql"), sem("s_kh"), sem("s_kl")
        s_vr, s_vh, s_vl = sem("s_vr"), sem("s_vh"), sem("s_vl")
        s_qk, s_qke = sem("s_qk"), sem("s_qke")
        s_s, s_cp, s_mx, s_sub = sem("s_s"), sem("s_cp"), sem("s_mx"), sem("s_sub")
        s_ex, s_sum, s_rc, s_pn = sem("s_ex"), sem("s_sum"), sem("s_rc"), sem("s_pn")
        s_pt, s_ph, s_pl = sem("s_pt"), sem("s_ph"), sem("s_pl")
        s_pv, s_ah, s_al, s_wo = sem("s_pv"), sem("s_ah"), sem("s_al"), sem("s_wo")
        s_res, s_ln, s_lp, s_x1n = sem("s_res"), sem("s_ln"), sem("s_lp"), sem("s_x1n")
        s_x1c, s_x1T, s_x1h, s_x1l = sem("s_x1c"), sem("s_x1T"), sem("s_x1h"), sem("s_x1l")
        c_init, c_xT, c_xh, c_xl = sem("c_init"), sem("c_xT"), sem("c_xh"), sem("c_xl")
        c_wqh, c_wql, c_wkh, c_wkl = sem("c_wqh"), sem("c_wql"), sem("c_wkh"), sem("c_wkl")
        c_woh, c_wol = sem("c_woh"), sem("c_wol")
        c_q, c_kv, c_rq, c_rk, c_qs, c_ks = (sem(n) for n in ("c_q", "c_kv", "c_rq", "c_rk", "c_qs", "c_ks"))
        c_vh, c_vl, c_tr, c_trh, c_trl = (sem(n) for n in ("c_vh", "c_vl", "c_tr", "c_trh", "c_trl"))
        c_s, c_cp, c_mx, c_sub, c_ex = (sem(n) for n in ("c_s", "c_cp", "c_mx", "c_sub", "c_ex"))
        c_sum, c_rc, c_pn, c_pt, c_ph, c_pl = (sem(n) for n in ("c_sum", "c_rc", "c_pn", "c_pt", "c_ph", "c_pl"))
        c_pv, c_ah, c_al, c_wo, c_acc = (sem(n) for n in ("c_pv", "c_ah", "c_al", "c_wo", "c_acc"))
        f_wT, f_wh, f_wl, f_st, f_var, f_pow, f_xn, f_hit = (
            sem(n) for n in ("f_wT", "f_wh", "f_wl", "f_st", "f_var", "f_pow", "f_xn", "f_hit"))
        f_sel, f_m, f_r, f_nm = sem("f_sel"), sem("f_m"), sem("f_r"), sem("f_nm")
        f_xT, f_xh, f_xl, f_dots, f_dense, f_dn = (
            sem(n) for n in ("f_xT", "f_xh", "f_xl", "f_dots", "f_dense", "f_dn"))
        f_half, f_halfc = sem("f_half"), sem("f_halfc")
        f_v, f_cnt, f_rs, f_ex, f_y, f_g = (sem(n) for n in ("f_v", "f_cnt", "f_rs", "f_ex", "f_y", "f_g"))

        PASSES = ((0, 0), (0, 1), (1, 0))

        def stages(u):
            return u >= 2 if isinstance(u, int) else True

        def tile_stages(i):
            return (i + 1 < T, i >= 1, i >= 2) if isinstance(i, int) else (True,) * 3

        def ctx_bank(t):
            return banks[{0: 5, 1: 6, 3: 6}.get(t, 2)]

        def v_blocks(part):
            return part.rearrange("p b (j x) -> p b j x", x=P + 2 * D1)[:, :, :, 0:2 * D1]

        def f32(ap):
            return ap.bitcast(F32)

        block = stack.enter_context(nc.Block())

        @block.sync
        def _(sp):
            def load_x(t):
                sp.dma_start(x_st, x[bass.ds(t * P, P), :]).then_inc(d_x, 16)

            def next_x(t):
                sp.wait_ge(s_xT, t)
                load_x(t)

            load_x(0)
            sp.dma_start(ident[:], c_ident).then_inc(d_ident, 16)
            for w, at in ((w1k, E), (w1v, E + KV1)):
                sp.dma_start(w1_raw[:, :, at:at + KV1], w.rearrange("(c p) n -> p c n", p=P)).then_inc(d_w1kv, 16)
            sp.dma_start(rope1[:], c_rope1).then_inc(d_const, 16)
            sp.dma_start(causal[:], c_causal).then_inc(d_const, 16)
            w1o_v = w1o.rearrange("(g h d) n -> g d h n", g=G1, h=HG)
            for g in range(G1):
                sp.dma_start(w1out_raw[D1 * g:D1 * g + D1, :, :], w1o_v[g]).then_inc(d_w1o, 16)
            sp.dma_start(pos_i[:], pos).then_inc(d_pos, 16)
            next_x(1)
            sp.dma_start(res, x.rearrange("(t p) n -> p t n", p=P)).then_inc(d_res, 16)
            for i in range(2):
                sp.dma_start(mask_i[S * i:S * i + S, :].rearrange("q (b k) -> q b k", b=B),
                             mask.rearrange("b q k -> q b k")).then_inc(d_mask, 16)

            def stage_v(t, first):
                sp.wait_ge(s_vr, t + 1)
                if not first:
                    sp.wait_ge(s_vl, t)
                for b in range(2):
                    for h in range(2):
                        sp.dma_start(v_st[S * h:S * h + S, b, :, D1 * h:D1 * h + D1],
                                     v_raw[S * b:S * b + S].rearrange("p (j x) -> p j x", x=2 * D1)
                                     [:, :, D1 * h:D1 * h + D1]).then_inc(d_v, 16)

            sp.wait_ge(s_dinit, 5)
            stage_v(0, True)
            next_x(2)
            with sp.Fori(1, T - 2) as t:
                stage_v(t, False)
                next_x(t + 2)
            wq_v = w2q.rearrange("(c p) n -> p c n", p=P)
            wk_v = w2k.rearrange("(c p) n -> p c n", p=P)
            wv_v = w2v.rearrange("(c p) n -> p c n", p=P)

            def load_q(g):
                sp.dma_start(w2q_raw, wq_v[:, :, bass.ds(g * HG * D2, HG * D2)]).then_inc(d_w2q, 16)

            def load_kv(g):
                sp.dma_start(w2kv_raw[:, :, 0:D2], wk_v[:, :, bass.ds(g * D2, D2)]).then_inc(d_w2kv, 16)
                sp.dma_start(w2kv_raw[:, :, D2:2 * D2], wv_v[:, :, bass.ds(g * D2, D2)]).then_inc(d_w2kv, 16)

            def load_o(g):
                sp.dma_start(w2o_raw, w2o[bass.ds(g * HG * D2, HG * D2), :].rearrange("(h p) n -> p h n", p=P)
                             ).then_inc(d_w2o, 16)

            def load_ctx(t):
                sp.dma_start(ctx_st[t % 2], ctx_in[t * P:(t + 1) * P, :]).then_inc(d_ctx[t % 2], 16)

            sp.wait_ge(s_w1l, EC + 1)
            sp.wait_ge(s_w1ol, HG)
            load_q(0)
            load_kv(0)
            load_o(0)
            load_ctx(0)
            load_ctx(1)
            stage_v(T - 2, False)
            stage_v(T - 1, False)
            for t in range(2, T):
                sp.wait_ge(c_xT, t - 1)
                load_ctx(t)
            with sp.Fori(0, G2 - 1) as g:
                sp.wait_ge(c_wql, 4 * g + 4)
                load_q(g + 1)
                sp.wait_ge(c_wkl, 2 * g + 2)
                load_kv(g + 1)
                sp.wait_ge(c_wol, 4 * g + 4)
                load_o(g + 1)

            sp.wait_ge(c_wql, 4 * G2)
            sp.dma_start(fw_raw, fw.rearrange("(c p) n -> p c n", p=P)).then_inc(d_fw, 16)
            sp.wait_ge(c_wkl, 2 * G2)
            sp.dma_start(fc_raw, fcent).then_inc(d_fc, 16)
            sp.dma_start(bias_b, fbias.rearrange("(o n) -> o n", o=1).broadcast_to([P, E])).then_inc(d_fc, 16)
            sp.wait_ge(c_cp, U - 2)
            sp.dma_start(assign_i, fassign.rearrange("(o n) -> o n", o=1).broadcast_to([NC, E])).then_inc(d_fc, 16)

            out_v = out.rearrange("(t p) n -> t p n", p=P)
            for t in range(T):
                sp.wait_ge(f_y, t + 1)
                sp.dma_start(out_v[t], res[:, t, :]).then_inc(d_out, 16)
            sp.wait_ge(d_out, 16 * T)

        @block.tensor
        def _(pe):
            def product(bank, lhs, rhs, chunks):
                for c in range(chunks):
                    for n, (a, b) in enumerate(PASSES):
                        mm = pe.matmul(bank, lhs(a, c), rhs(b, c), start=(c == 0 and n == 0),
                                       stop=(c == chunks - 1 and n == 2))
                return mm

            TX, BQ, BKV, TR, SB, BO = banks[0], banks[1], banks[2], banks[3:5], banks[5:7], banks[7]

            def a_stage(t):
                pe.wait_ge(d_x, 16 * (t + 1))
                for c in range(EC):
                    mm = pe.transpose(BQ[:, c * P:(c + 1) * P], x_st[:, c * P:(c + 1) * P], ident[:])
                mm.then_inc(s_xT, 1)

            def b_stage(t, first):
                pe.wait_ge(s_xl, t + 1)
                for c in range(EC):
                    if first:
                        pe.wait_ge(s_w1l, c + 1)
                    for n, (a, b) in enumerate(PASSES):
                        mm = pe.matmul(BQ[:], xt[a][:, c, :], w1[b][:, c, 0:E], start=(c == 0 and n == 0),
                                       stop=(c == EC - 1 and n == 2))
                mm.then_inc(s_q, 1)

            def kv_stage(t, first):
                if first:
                    pe.wait_ge(s_w1l, EC + 1)
                product(BKV[:, 0:2 * KV1], lambda a, c: xt[a][:, c, :],
                        lambda b, c: w1[b][:, c, E:E + 2 * KV1], EC).then_inc(s_kv, 1)

            def pt_stage(v, u):
                if u < 2:
                    pe.wait_ge(s_qke, 6 * v + 5 + u)
                else:
                    pe.wait_ge(s_pl, 4 * v + u - 1)
                pe.wait_ge(s_pn, 4 * v + u + 1)
                for i in range(4):
                    mm = pe.transpose(TR[u % 2][:, i * P:(i + 1) * P], p1[u][:, i * P:(i + 1) * P], ident[:])
                mm.then_inc(s_pt, 1)

            def pv_stage(v, half_, first):
                if half_ == 0:
                    pe.wait_ge(s_vl, v + 1)
                    if not first:
                        pe.wait_ge(s_al, v)
                pe.wait_ge(s_pl, 4 * v + 2 * half_ + 2)
                for j in range(2 * half_, 2 * half_ + 2):
                    for n, (a, k) in enumerate(PASSES):
                        for b in range(2):
                            mm = pe.matmul(BO[:, 2 * P * b:2 * P * (b + 1)], vpad[a][:, b, j * P:(j + 1) * P],
                                           pT1[k][:, b, j, :, :].rearrange("p a n -> p (a n)"),
                                           start=(j == 0 and n == 0 and b == 0), stop=(j == 3 and n == 2),
                                           skip_group_check=True)
                if half_ == 1:
                    mm.then_inc(s_pv, 1)

            QK = (TX, TR[0], TR[1])

            def qk_stage(t, first):
                pe.wait_ge(s_ql, t + 1)
                if tile_stages(t)[2]:
                    pe.wait_ge(s_res, t - 1)
                for j, (kind, n) in enumerate((("q", 0), ("q", 1), ("k", 0), ("q", 2), ("q", 3), ("k", 1))):
                    if j == 2:
                        pe.wait_ge(s_kl, t + 1)
                    if j >= 3:
                        pe.wait_ge(s_qke, 6 * t + j - 2)
                    elif j > 0 and not first:
                        pe.wait_ge(s_pl, 4 * t - 2 + j)
                    for i in range(4):
                        m = 4 * n + i
                        src = f32(stack_q[:, 2 * m:2 * m + 2, :].rearrange("p h r -> p (h r)")) \
                            if kind == "q" else f32(stack_k[:, m, :])
                        mm = pe.transpose(QK[j % 3][:, i * P:(i + 1) * P], src, ident[:])
                    mm.then_inc(s_qk, 1)

            def wo_stage(v, t, first):
                pe.wait_ge(s_al, v + 1)
                if first:
                    pe.wait_ge(s_w1ol, HG)
                if t is None:
                    pe.wait_ge(s_res, v)
                else:
                    pe.wait_ge(s_qke, 6 * t + 4)
                product(TX[:], lambda a, c: at1[a][:, c, :, :].rearrange("p b q -> p (b q)"),
                        lambda b, c: w1out[b][:, 2 * (c % 2) + c // 2, :], 4).then_inc(s_wo, 1)

            def s_stage(t, units, first):
                for u in units:
                    if u % 2 == 0:
                        pe.wait_ge(s_qke, 6 * t + 3 + 3 * (u // 2))
                    if u >= 2 or not first:
                        pe.wait_ge(s_cp, 4 * t + u - 1)
                    rows = slice(S * (u % 2), S * (u % 2) + S)
                    for i in range(4):
                        g = 4 * (u // 2) + i
                        for b in range(2):
                            mm = pe.matmul(SB[u % 2][:, (4 * b + i) * S:(4 * b + i + 1) * S],
                                           qT1[rows, b, 2 * g:2 * g + 2, :].rearrange("p j q -> p (j q)"),
                                           kT1[rows, g, b * S:(b + 1) * S], start=True, stop=True)
                    mm.then_inc(s_s, 1)

            def x1_stage(w, i, bank=BKV):
                pe.wait_ge(s_x1n, w + 1)
                if i is not None:
                    pe.wait_ge(s_rk, i + 1)
                    pe.wait_ge(s_vr, i + 1)
                for c in range(EC):
                    mm = pe.transpose(bank[:, c * P:(c + 1) * P], x1n[:, c * P:(c + 1) * P], ident[:])
                mm.then_inc(s_x1T, 1)

            def tile_steps(i):
                following, old, oldest = tile_stages(i)
                v, w = i - 1, i - 2
                start = not old
                b_stage(i, start)
                if old:
                    pt_stage(v, 0)
                    pt_stage(v, 1)
                if old:
                    pe.wait_ge(s_cp, 4 * i)
                kv_stage(i, start)
                if old:
                    pt_stage(v, 2)
                    pt_stage(v, 3)
                if following:
                    pe.wait_ge(s_rq, i + 1)
                    a_stage(i + 1)
                qk_stage(i, start)
                s_stage(i, (0, 1), start)
                if old:
                    pv_stage(v, 0, not oldest)
                    pv_stage(v, 1, not oldest)
                if oldest:
                    x1_stage(w, i)
                s_stage(i, (2, 3), start)
                if old:
                    wo_stage(v, i, not oldest)

            BQ2, BKV2, TR2, BS2, BO2 = banks[0:2], banks[2], banks[3:5], banks[5], banks[6:8]

            def q_proj(u, c, i, first):
                if not first:
                    pe.wait_ge(c_rq, 2 * u + i - 1)
                tok = slice((2 * c + i) * P, (2 * c + i + 1) * P)
                product(BQ2[i][:], lambda a, e: xT[a][:, e, tok], lambda b, e: w2q_s[b][:, e, :], EC
                        ).then_inc(c_q, 1)

            def kv_proj(u, c, i):
                if isinstance(u, int) and u < UN:
                    pe.wait_ge(c_xl, 2 * c + 2)
                elif i == 0:
                    pe.wait_ge(c_rk, u)
                    pe.wait_ge(c_vl, u)
                tok = slice((2 * c + i) * P, (2 * c + i + 1) * P)
                mm = product(BKV2[:, 256 * i:256 * i + 256], lambda a, e: cT[a][:, e, tok],
                             lambda b, e: w2kv_s[b][:, e, :], EC)
                if i == 1:
                    mm.then_inc(c_kv, 1)

            def ctx_turn(t):
                pe.wait_ge(d_ctx[t % 2], 16 * (t // 2) + 16)
                if t > 3 and t % 2:
                    pe.wait_ge(c_xl, t)
                elif t > 1 and t % 2 == 0:
                    pe.wait_ge(c_rk, t // 2)
                    pe.wait_ge(c_vl, t // 2)
                elif t == 3:
                    pe.wait_ge(c_xl, 2)
                for c in range(EC):
                    mm = pe.transpose(ctx_bank(t)[:, c * P:(c + 1) * P], ctx_st[t % 2][:, c * P:(c + 1) * P], ident[:])
                mm.then_inc(c_xT, 1)

            def p_turn(v):
                pe.wait_ge(c_trl, 3 * v + 2)
                pe.wait_ge(c_pn, v + 1)
                for i in range(2):
                    for h in range(2):
                        mm = pe.transpose(TR2[0][:, (2 * i + h) * P:(2 * i + h + 1) * P],
                                          p2[:, (2 * h + i) * P:(2 * h + i + 1) * P], ident[:])
                mm.then_inc(c_pt, 1)

            def pv(v, c, first):
                pe.wait_ge(c_pl, v + 1)
                pe.wait_ge(c_vl, v + 1)
                if not first:
                    pe.wait_ge(c_acc, 2 * v)
                for s in range(2):
                    rows = slice(S * s, S * s + S)
                    for i in range(2):
                        for n, (a, b) in enumerate(PASSES):
                            mm = pe.matmul(BO2[s][:, 256 * i:256 * i + 256], v2[c % 2][a][rows, i, :],
                                           pT2[b][rows, i, :], start=(n == 0), stop=(n == 2))
                    mm.then_inc(c_pv, 1)

            def q_turn(u, i, first):
                if i == 0:
                    if not first:
                        pe.wait_ge(c_trl, 3 * u)
                elif not first:
                    pe.wait_ge(c_pl, u)
                pe.wait_ge(c_qs, 2 * u + i + 1)
                for h in range(HG):
                    mm = pe.transpose(TR2[1 - i][:, h * P:(h + 1) * P], u1q[i][:, h * P:(h + 1) * P], ident[:])
                mm.then_inc(c_tr, 1)

            def k_turn(u):
                pe.wait_ge(c_trl, 3 * u + 1)
                pe.wait_ge(c_ks, u + 1)
                for i in range(2):
                    mm = pe.transpose(TR2[1][:, i * P:(i + 1) * P], u1k[:, i * P:(i + 1) * P], ident[:])
                mm.then_inc(c_tr, 1)

            def out_proj(i, heads):
                for h in heads:
                    for n, (a, b) in enumerate(PASSES):
                        mm = pe.matmul(BO2[i][:], at2[a][:, h, i * P:(i + 1) * P], w2o_s[b][:, h, :],
                                       start=(h == 0 and n == 0), stop=(h == HG - 1 and n == 2))
                if heads[-1] == HG - 1:
                    mm.then_inc(c_wo, 1)

            def scores(u, first):
                pe.wait_ge(c_trl, 3 * u + 3)
                if not first:
                    pe.wait_ge(c_cp, u)
                for h in range(2):
                    for b in range(4):
                        at = (4 * h + b) * S
                        for n, (a, k) in enumerate(PASSES):
                            mm = pe.matmul(BS2[:, at:at + S], qT2[a][:, b, 2 * h:2 * h + 2, :].rearrange("p h q -> p (h q)"),
                                           kT2[k][:, b * S:(b + 1) * S], start=(n == 0), stop=(n == 2))
                mm.then_inc(c_s, 1)

            def slot(u, g, c):
                oldest = stages(u)
                v = u - 1
                if oldest:
                    out_proj(1, range(HG))
                turn = isinstance(u, int) and u < UN
                pe.wait_ge(c_wql, 4 * g + 4)
                if turn:
                    ctx_turn(2 * c)
                begun = isinstance(u, int) and u == 1
                if not begun:
                    q_proj(u, c, 0, False)
                if turn:
                    ctx_turn(2 * c + 1)
                q_proj(u, c, 1, False)
                if begun:
                    kv_proj(u, c, 0)
                p_turn(v)
                q_turn(u, 0, False)
                pe.wait_ge(c_wkl, 2 * g + 2)
                if begun:
                    pe.wait_ge(s_x1l, T)
                else:
                    kv_proj(u, c, 0)
                pv(v, (c - 1) % UN, not oldest)
                kv_proj(u, c, 1)
                q_turn(u, 1, False)
                pe.wait_ge(c_al, 2 * v + 2)
                pe.wait_ge(c_wol, 4 * (g if c > 0 else g - 1) + 4)
                out_proj(0, range(HG // 2))
                k_turn(u)
                out_proj(0, range(HG // 2, HG))
                scores(u, False)

            pe.wait_ge(d_ident, 16)
            a_stage(0)
            pe.wait_ge(s_init, 3)
            tile_steps(0)
            tile_steps(1)
            with pe.Fori(2, T - 1) as t:
                tile_steps(t)
            tile_steps(T - 1)

            v = T - 1
            pt_stage(v, 0)
            pt_stage(v, 1)
            pe.wait_ge(s_xl, T)
            pe.wait_ge(s_rq, T)
            pe.wait_ge(s_res, v)
            pe.wait_ge(c_wql, 4)
            q_proj(0, 0, 0, True)
            q_proj(0, 0, 1, True)
            pt_stage(v, 2)
            pt_stage(v, 3)
            pv_stage(v, 0, False)
            pv_stage(v, 1, False)
            pe.wait_ge(s_cp, 4 * T)
            ctx_turn(0)
            ctx_turn(1)
            pe.wait_ge(s_pl, 4 * T)
            q_turn(0, 0, True)
            q_turn(0, 1, True)
            pe.wait_ge(c_rq, 1)
            wo_stage(v, None, False)
            pe.wait_ge(c_wkl, 2)
            pe.wait_ge(s_rk, T)
            pe.wait_ge(s_vr, T)
            kv_proj(0, 0, 0)
            kv_proj(0, 0, 1)
            x1_stage(v - 1, None, banks[7])
            pe.wait_ge(s_res, T)
            q_proj(1, 1, 0, False)
            k_turn(0)
            scores(0, True)
            pe.wait_ge(s_x1l, v)
            x1_stage(v, None, banks[7])

            for u in range(1, UN + 1):
                slot(u, u // UN, u % UN)
            with pe.Fori(1, G2 - 1) as g:
                for c in range(1, UN + 1):
                    slot(UN * g + c, g + c // UN, c % UN)
            for u in range(U - UN + 1, U):
                slot(u, u // UN, u % UN)

            v = U - 1
            out_proj(1, range(HG))
            WT = (banks[0], banks[1], banks[2], banks[4])
            pe.wait_ge(d_fw, 16)
            pe.wait_ge(c_rq, 2 * U)
            pe.wait_ge(c_rk, U)
            pe.wait_ge(c_vl, U)
            for c in range(EC):
                for j in range(EC):
                    mm = pe.transpose(WT[c][:, j * P:(j + 1) * P], fw_raw[:, j, c * P:(c + 1) * P], ident[:])
                mm.then_inc(f_wT, 1)
            pe.wait_ge(d_fc, 16 * 3)
            pe.wait_ge(f_wl, 1)
            for c in range(EC):
                mm = pe.transpose(banks[0][:, c * NC:(c + 1) * NC], fc_raw[:, c * P:(c + 1) * P], ident[0:NC, 0:NC])
            mm.then_inc(f_wT, 1)
            p_turn(v)

            def x3_turn(t):
                pe.wait_ge(f_xn, t + 1)
                if t < 2:
                    pe.wait_ge(f_wl, t + 2)
                else:
                    pe.wait_ge(f_xl, t - 1)
                for c in range(EC):
                    mm = pe.transpose(banks[1 + t % 2][:, c * P:(c + 1) * P], res[:, t, c * P:(c + 1) * P], ident[:])
                mm.then_inc(f_xT, 1)

            def cluster_dots(half):
                pe.wait_ge(f_wl, EC + 1)
                pe.wait_ge(f_xl, 4 * half + 4)
                product(banks[4 * half][0:NC, :], lambda a, c: fcT[a][:, c, :],
                        lambda b, c: xT[b][:, c, 4 * half * P:(4 * half + 4) * P], EC).then_inc(f_half, 1)

            def dots_turn(half):
                pe.wait_ge(f_halfc, half + 1)
                for t in range(4 * half, 4 * half + 4):
                    mm = pe.transpose(banks[5][:, t * NC:(t + 1) * NC], dots_T[half][:, (t % 4) * P:(t % 4 + 1) * P],
                                      ident[0:NC, 0:NC])
                mm.then_inc(f_dots, 1)

            DB = (banks[3], banks[4], banks[6], banks[7], banks[1], banks[2])

            def dense(t):
                if t >= len(DB):
                    pe.wait_ge(f_dn, t - len(DB) + 1)
                product(DB[t % len(DB)][:], lambda a, c: xT[a][:, c, t * P:(t + 1) * P],
                        lambda b, c: fwT[b][:, c, :], EC).then_inc(f_dense, 1)

            x3_turn(0)
            x3_turn(1)
            pv(v, v % UN, False)
            pe.wait_ge(c_al, 2 * v + 2)
            pe.wait_ge(c_wol, 4 * G2)
            out_proj(0, range(HG))
            x3_turn(2)
            out_proj(1, range(HG))
            x3_turn(3)
            x3_turn(4)
            pe.wait_ge(f_wl, EC + 1)
            pe.wait_ge(c_pl, U)
            dense(0)
            x3_turn(5)
            x3_turn(6)
            x3_turn(7)
            cluster_dots(0)
            cluster_dots(1)
            dots_turn(0)
            dots_turn(1)
            dense(1)
            pe.wait_ge(c_acc, 2 * U)
            dense(2)
            pe.wait_ge(f_hit, 1)
            pe.wait_ge(s_dinit, 5)
            pe.matmul(banks[0][0:NC, 0:P], any_hit, ones[:], start=True, stop=True).then_inc(f_cnt, 1)
            pe.wait_ge(f_rs, 1)
            pe.matmul(banks[0][:], cluster_hit[0:NC, :], onehot, start=True, stop=True).then_inc(f_cnt, 1)
            for t in range(3, T):
                dense(t)

        @block.scalar
        def _(act):
            def copy(dst, src, done):
                act.activation(dst, src, ACT.Copy).then_inc(done, 1)

            def x_high(t):
                act.wait_ge(s_xT, t + 1)
                copy(xt[0], banks[1][:].rearrange("p (c n) -> p c n", c=EC), s_xh)

            for c in range(EC):
                act.dma_start(w1_raw[:, c, 0:E], w1q[c * P:(c + 1) * P, :]).then_inc(d_w1q[c], 16)
            x_high(0)
            for c in range(EC):
                act.wait_ge(d_w1q[c], 16)
                copy(w1[0][:, c, 0:E], w1_raw[:, c, 0:E], s_w1h)
            act.wait_ge(d_w1kv, 32)
            copy(w1[0][:, :, E:], w1_raw[:, :, E:], s_w1h)
            act.wait_ge(d_w1o, 16 * G1)
            for h in range(HG):
                copy(w1out[0][:, h, :], w1out_raw[:, h, :], s_w1oh)

            def p_high(v, u, first):
                act.wait_ge(s_pt, 4 * v + u + 1)
                if u == 0 and not first:
                    act.wait_ge(s_pv, v)
                copy(pT1[0][:, :, 2 * (u // 2):2 * (u // 2) + 2, u % 2, :],
                     banks[3 + u % 2][:].rearrange("p (b j n) -> p b j n", b=2, j=2), s_ph)

            def at_high(v, first):
                act.wait_ge(s_pv, v + 1)
                if not first:
                    act.wait_ge(s_wo, v)
                copy(at1[0], banks[7][:].rearrange("p (b a q) -> p a b q", b=2, a=4), s_ah)

            def expo(v, u):
                act.wait_ge(s_sub, 4 * v + u + 1)
                act.activation(p1[u], p1[u], ACT.Exp, scale=SCALE1).then_inc(s_ex, 1)

            def tile_steps(i):
                following, old, oldest = tile_stages(i)
                v, w = i - 1, i - 2
                if old:
                    p_high(v, 0, not oldest)
                    p_high(v, 1, not oldest)
                act.wait_ge(s_qs, i + 1)
                if old:
                    act.wait_ge(s_qk, 6 * i)
                copy(stack_q.rearrange("p h (a b d) -> p h a b d", a=2, b=2)[:, :, 0],
                     bcast(t1q.rearrange("p (h d) -> p h d", h=H1), 2, 2), s_qh)
                if old:
                    p_high(v, 2, not oldest)
                act.wait_ge(s_ks, i + 1)
                copy(stack_k.rearrange("p g (a b d) -> p g a b d", a=4, b=2)[:, :, :, 0],
                     bcast(t1k.rearrange("p (g d) -> p g d", g=G1), 2, 4), s_kh)
                if old:
                    p_high(v, 3, not oldest)
                act.wait_ge(s_rk, i + 1)
                if old:
                    act.wait_ge(s_vl, i)
                copy(v_raw, banks[2][:, KV1:2 * KV1], s_vr)
                if not following:
                    wq_high(0, 0)
                    wq_high(0, 1)
                n_q = n_k = 0
                if old:
                    act.wait_ge(s_s, 4 * i)
                for j, kind in enumerate("qqkqqk"):
                    act.wait_ge(s_qk, 6 * i + j + 1)
                    if j == 3 and following:
                        x_high(i + 1)
                    src = banks[(0, 3, 4)[j % 3]][:].rearrange("p (g n) -> p g n", g=4)
                    if kind == "q":
                        copy(qT1[:, :, 4 * n_q:4 * n_q + 4, :].rearrange("p b j q -> p j b q"),
                             src.rearrange("p g (b q) -> p g b q", b=2), s_qke)
                        n_q += 1
                    else:
                        copy(kT1[:, 4 * n_k:4 * n_k + 4, :], src, s_qke)
                        n_k += 1
                if not following:
                    wq_high(0, 2)
                    wq_high(0, 3)
                if old:
                    at_high(v, not oldest)
                expo(i, 0)
                expo(i, 1)
                act.wait_ge(d_v, 64 * (i + 1))
                if old:
                    act.wait_ge(s_pv, i)
                copy(v_blocks(vpad[0]), v_st, s_vh)
                if oldest:
                    act.wait_ge(s_x1n, w + 1)
                    copy(res[:, bass.ds(w, 1), :].rearrange("p t n -> p (t n)"), x1n, s_x1c)
                    x1_high(w)
                if not following:
                    wkv_high(0, 0)
                    wkv_high(0, 1)
                expo(i, 2)
                expo(i, 3)

            def x1_high(w, bank=banks[2]):
                act.wait_ge(s_x1T, w + 1)
                copy(xT[0][:, :, bass.ds(w * P, P)], bank[:].rearrange("p (c n) -> p c n", c=EC), s_x1h)

            def wq_high(g, c):
                act.wait_ge(d_w2q, 16 * (g + 1))
                copy(w2q_s[0][:, c, :], w2q_raw[:, c, :], c_wqh)

            def wkv_high(g, i):
                act.wait_ge(d_w2kv, 32 * (g + 1))
                copy(w2kv_s[0][:, 2 * i:2 * i + 2, :], w2kv_raw[:, 2 * i:2 * i + 2, :], c_wkh)

            def wo_high(g, h):
                act.wait_ge(d_w2o, 16 * (g + 1))
                copy(w2o_s[0][:, h, :], w2o_raw[:, h, :], c_woh)

            def ctx_high(t):
                act.wait_ge(c_xT, t + 1)
                copy(cT[0][:, :, t * P:(t + 1) * P], ctx_bank(t)[:].rearrange("p (c n) -> p c n", c=EC), c_xh)

            def turn_high(u, n):
                act.wait_ge(c_tr, 3 * u + n + 1)
                if n < 2:
                    copy(qT2[0][:, 2 * n:2 * n + 2].rearrange("p b h q -> p h b q"),
                         cut(banks[4 - n][:], h=HG, b=2, q=S), c_trh)
                else:
                    copy(kT2[0], banks[4][:, 0:2 * P], c_trh)

            def at2_high(v, s):
                act.wait_ge(c_pv, 2 * v + s + 1)
                copy(at2[0].rearrange("p h (i s q) -> p s i h q", i=2, s=2)[:, s],
                     banks[6 + s][:].rearrange("p (i h q) -> p i h q", i=2, h=HG), c_ah)

            def slot(u, g, c):
                oldest = stages(u)
                v = u - 1
                split = c == UN - 1 and not (isinstance(g, int) and g == G2 - 1)
                turn = isinstance(u, int) and u < UN
                if turn and u == 1:
                    ctx_high(2 * c)
                    ctx_high(2 * c + 1)
                act.wait_ge(c_sub, v + 1)
                act.activation(p2, p2, ACT.Exp, scale=SCALE2).then_inc(c_ex, 1)
                if turn and u > 1:
                    ctx_high(2 * c)
                    ctx_high(2 * c + 1)
                if c == 1:
                    if oldest:
                        act.wait_ge(c_wo, 2 * v)
                    else:
                        act.wait_ge(s_wo, T)
                    for h in range(HG):
                        wo_high(g, h)
                act.wait_ge(c_pt, v + 1)
                if oldest:
                    act.wait_ge(c_pv, 2 * v)
                copy(pT2[0], banks[3][:].rearrange("p (i n) -> p i n", i=2), c_ph)
                act.wait_ge(c_s, u)
                turn_high(u, 0)
                if split:
                    act.wait_ge(c_q, 2 * u + 2)
                    wq_high(g + 1, 0)
                    wq_high(g + 1, 1)
                if oldest:
                    act.wait_ge(c_wo, 2 * v)
                at2_high(v, 0)
                at2_high(v, 1)
                if split:
                    wq_high(g + 1, 2)
                turn_high(u, 1)
                act.wait_ge(c_rk, u + 1)
                copy(v2[c % 2][0], banks[2][:].rearrange("p (i n) -> p i n", i=2)[:, :, D2:2 * D2], c_vh)
                turn_high(u, 2)
                if split:
                    wq_high(g + 1, 3)
                    wkv_high(g + 1, 0)
                    wkv_high(g + 1, 1)

            act.wait_ge(s_init, 3)
            tile_steps(0)
            act.wait_ge(d_res, 16)
            tile_steps(1)
            with act.Fori(2, T - 1) as t:
                tile_steps(t)
            tile_steps(T - 1)

            v = T - 1
            for u in range(4):
                p_high(v, u, False)
            at_high(v, False)
            ctx_high(0)
            ctx_high(1)
            turn_high(0, 0)
            turn_high(0, 1)
            act.wait_ge(s_x1n, v)
            copy(res[:, v - 1, :], x1n, s_x1c)
            act.wait_ge(c_rk, 1)
            copy(v2[0][0], banks[2][:].rearrange("p (i n) -> p i n", i=2)[:, :, D2:2 * D2], c_vh)
            x1_high(v - 1, banks[7])
            turn_high(0, 2)
            act.wait_ge(s_x1n, T)
            copy(res[:, v, :], x1n, s_x1c)
            x1_high(v, banks[7])

            for u in range(1, UN + 1):
                slot(u, u // UN, u % UN)
            with act.Fori(1, G2 - 1) as g:
                for c in range(1, UN + 1):
                    slot(UN * g + c, g + c // UN, c % UN)
            for u in range(U - UN + 1, U):
                slot(u, u // UN, u % UN)

            v = U - 1
            act.wait_ge(c_sub, v + 1)
            act.activation(p2, p2, ACT.Exp, scale=SCALE2).then_inc(c_ex, 1)

            def fw_high(c):
                act.wait_ge(f_wT, c + 1)
                copy(fwT[0][:, c, :], banks[(0, 1, 2, 4)[c]][:], f_wh)

            def x3_high(t):
                act.wait_ge(f_xT, t + 1)
                copy(xT[0][:, :, t * P:(t + 1) * P], banks[1 + t % 2][:].rearrange("p (c n) -> p c n", c=EC), f_xh)

            def dots_copy(half):
                act.wait_ge(f_half, half + 1)
                copy(dots_T[half], banks[4 * half][0:NC, :], f_halfc)

            for c in range(EC):
                fw_high(c)
            act.wait_ge(c_pt, v + 1)
            act.wait_ge(c_pv, 2 * v)
            copy(pT2[0], banks[3][:].rearrange("p (i n) -> p i n", i=2), c_ph)
            act.wait_ge(f_wT, EC + 1)
            copy(fcT[0], banks[0][:, 0:EC * NC].rearrange("p (c n) -> p c n", c=EC), f_wh)
            act.wait_ge(c_wo, 2 * v)
            at2_high(v, 0)
            at2_high(v, 1)
            for t in range(T):
                x3_high(t)
            dots_copy(0)
            dots_copy(1)
            act.wait_ge(f_v, 5)
            act.activation(dots, dots, ACT.Exp, scale=INV_TEMPERATURE).then_inc(f_ex, 1)
            for t in range(T):
                act.wait_ge(f_nm, t + 1)
                act.activation(res[:, t, :], res[:, t, :], ACT.Identity, bias=nmean[:, t:t + 1],
                               scale=rstd8[:, t:t + 1]).then_inc(f_y, 1)

        @block.gpsimd
        def _(pool):
            pool.memset(f32(vpad[0]), 0.0).then_inc(s_init, 1)
            pool.memset(f32(vpad[1]), 0.0).then_inc(s_init, 1)
            pool.memset(half[:], -0.5).then_inc(s_init, 1)
            pool.memset(half8, -0.5).then_inc(s_dinit, 1)
            pool.memset(ones[:], 1.0).then_inc(s_dinit, 1)
            pool.memset(v_st, 0.0).then_inc(s_dinit, 1)
            for i in range(2):
                pool.memset(sc1[i], NEG1).then_inc(s_dinit, 1)

            def gather_rope(t):
                pool.indirect_dma_start(cs[:, t, :], None, c_rope2,
                                        bass.IndirectOffsetOnAxis(ap=pos_i[:, t:t + 1], axis=0)).then_inc(d_cs, 16)

            def sub(v, u, first):
                pool.wait_ge(s_mx, 4 * v + u + 1)
                if not first:
                    pool.wait_ge(s_pt, 4 * v + u - 3)
                pool.tensor_tensor(cut(p1[u], b=8, k=S), cut(sc1[u % 2], b=8, k=S), bcast(mx1[u], 2, S),
                                   ALU.subtract).then_inc(s_sub, 1)

            def norm(v, u):
                pool.wait_ge(s_rc, 4 * v + u + 1)
                pool.tensor_tensor(cut(p1[u], b=8, k=S), cut(p1[u], b=8, k=S), bcast(sm1[u], 2, S),
                                   ALU.mult).then_inc(s_pn, 1)

            def root1(w):
                pool.wait_ge(s_ln, 3 * w + 3)
                pool.tensor_tensor(rstd, mv[:, 1:2], half, ALU.pow).then_inc(s_lp, 1)

            def tile_steps(i):
                following, old, oldest = tile_stages(i)
                v, w = i - 1, i - 2
                if old:
                    norm(v, 2)
                pool.wait_ge(s_rq, i + 1)
                pool.tensor_tensor(t1q, t1q, t2q, ALU.add).then_inc(s_qs, 1)
                if old:
                    norm(v, 3)
                pool.wait_ge(s_rk, i + 1)
                pool.tensor_tensor(t1k, t1k, t2k, ALU.add).then_inc(s_ks, 1)
                pool.wait_ge(s_kh, i + 1)
                sk = stack_k.rearrange("p g (a b d) -> p g a b d", a=4, b=2)
                pool.tensor_tensor(sk[:, :, :, 1], bcast(t1k.rearrange("p (g d) -> p g d", g=G1), 2, 4),
                                   f32(sk[:, :, :, 0]), ALU.subtract).then_inc(s_kl, 1)
                if isinstance(i, int) and i < 2:
                    pool.wait_ge(d_pos, 16)
                    for t in range(T // 2 * i, T // 2 * (i + 1)):
                        gather_rope(t)
                if not following:
                    wq_low(0, 0)
                    wq_low(0, 1)
                if oldest:
                    root1(w)
                sub(i, 0, not old)
                sub(i, 1, not old)
                norm(i, 0)
                pool.wait_ge(s_vh, i + 1)
                pool.tensor_tensor(v_blocks(vpad[1]), v_st, f32(v_blocks(vpad[0])),
                                   ALU.subtract).then_inc(s_vl, 1)
                sub(i, 2, not old)
                norm(i, 1)
                sub(i, 3, not old)

            def sum_q(u, i):
                pool.wait_ge(c_rq, 2 * u + i + 1)
                pool.tensor_tensor(u1q[i], u1q[i], u2q[i], ALU.add).then_inc(c_qs, 1)

            def sum_k(u):
                pool.wait_ge(c_rk, u + 1)
                pool.tensor_tensor(u1k, u1k, u2k, ALU.add).then_inc(c_ks, 1)

            def wq_low(g, c):
                pool.wait_ge(c_wqh, 4 * g + c + 1)
                pool.tensor_tensor(w2q_s[1][:, c, :], w2q_raw[:, c, :], f32(w2q_s[0][:, c, :]),
                                   ALU.subtract).then_inc(c_wql, 1)

            def wkv_low(g, i):
                cs_ = slice(2 * i, 2 * i + 2)
                pool.wait_ge(c_wkh, 2 * g + i + 1)
                pool.tensor_tensor(w2kv_s[1][:, cs_, :], w2kv_raw[:, cs_, :], f32(w2kv_s[0][:, cs_, :]),
                                   ALU.subtract).then_inc(c_wkl, 1)

            def wo_low(g, h):
                pool.wait_ge(c_woh, 4 * g + h + 1)
                pool.tensor_tensor(w2o_s[1][:, h, :], w2o_raw[:, h, :], f32(w2o_s[0][:, h, :]),
                                   ALU.subtract).then_inc(c_wol, 1)

            def softmax_steps(v, c, before):
                pool.wait_ge(c_mx, v + 1)
                if before:
                    pool.wait_ge(c_pt, v)
                pool.tensor_tensor(cut(p2, b=8, k=S), cut(sc2[c], b=8, k=S), bcast(mx2, 2, S),
                                   ALU.subtract).then_inc(c_sub, 1)
                pool.wait_ge(c_rc, v + 1)
                pool.tensor_tensor(cut(p2, b=8, k=S), cut(p2, b=8, k=S), bcast(sm2, 2, S),
                                   ALU.mult).then_inc(c_pn, 1)

            def slot(u, g, c):
                oldest = stages(u)
                v = u - 1
                split = c == UN - 1 and not (isinstance(g, int) and g == G2 - 1)
                split_o = c == 1
                softmax_steps(v, (c - 1) % UN, oldest)
                if split_o:
                    wo_low(g, 0)
                sum_q(u, 0)
                if split_o:
                    wo_low(g, 1)
                sum_q(u, 1)
                if split_o:
                    wo_low(g, 2)
                    wo_low(g, 3)
                if split:
                    wq_low(g + 1, 0)
                    wq_low(g + 1, 1)
                sum_k(u)
                if split:
                    wq_low(g + 1, 2)
                    wq_low(g + 1, 3)
                    wkv_low(g + 1, 0)
                    wkv_low(g + 1, 1)

            pool.wait_ge(s_init, 3)
            tile_steps(0)
            tile_steps(1)
            with pool.Fori(2, T - 1) as t:
                tile_steps(t)
            tile_steps(T - 1)

            v = T - 1
            norm(v, 2)
            norm(v, 3)
            sum_q(0, 0)
            sum_q(0, 1)
            root1(v - 1)
            wkv_low(0, 0)
            wkv_low(0, 1)
            pool.wait_ge(s_pt, 4 * T)
            for i in range(UN):
                pool.memset(sc2[i], NEG2).then_inc(c_init, 1)
            sum_k(0)
            root1(v)

            for u in range(1, UN + 1):
                slot(u, u // UN, u % UN)
            with pool.Fori(1, G2 - 1) as g:
                for c in range(1, UN + 1):
                    slot(UN * g + c, g + c // UN, c % UN)
            pool.iota(pos_i[0:NC, 0:1], pattern=[[0, 1]], base=0,
                      channel_multiplier=1).then_inc(f_g, 1)

            def root(t, n):
                pool.wait_ge(f_var, n + 1)
                pool.tensor_tensor(rstd8[:, t:t + 1], var8[:, t:t + 1], half8[:, 0:1], ALU.pow).then_inc(f_pow, 1)

            for u in range(U - UN + 1, U):
                slot(u, u // UN, u % UN)
                if u >= U - 2:
                    root(2 * (u - U + 2), 2 * (u - U + 2))
                    root(2 * (u - U + 2) + 1, 2 * (u - U + 2) + 1)

            softmax_steps(U - 1, (U - 1) % UN, True)
            for t in range(4, T):
                root(t, t)
            for t in range(T + 2):
                if t < T:
                    pool.wait_ge(f_dn, t + 1)
                    pool.wait_ge(f_sel, 1)
                    pool.tensor_tensor(masked[t % 2], masked[t % 2], row_sel, ALU.mult).then_inc(f_m, 1)
                if t >= 2:
                    root(t - 2, T + t - 2)

        @block.vector
        def _(dve):
            def low(dst, src, high, done):
                dve.tensor_tensor(dst, src, f32(high), ALU.subtract).then_inc(done, 1)

            def hold():
                dve.sem_inc(s_gate, 1)

            def x_low(t):
                dve.wait_ge(s_xh, t + 1)
                low(xt[1], banks[1][:].rearrange("p (c n) -> p c n", c=EC), xt[0], s_xl)

            def rope_q(t, first):
                q = banks[1][:].rearrange("p (h d) -> p h d", h=H1)
                t1, t2 = (v.rearrange("p (h d) -> p h d", h=H1) for v in (t1q, t2q))
                dve.wait_ge(s_q, t + 1)
                if not first:
                    dve.wait_ge(s_ql, t)
                dve.tensor_tensor(t1, q, bcast(rope1[:, 0:D1], 1, H1), ALU.mult)
                sin = bcast(rope1[:, D1:D1 + 8], 1, H1)
                dve.scalar_tensor_tensor(t2[:, :, 0:D1:2], q[:, :, 1:D1:2], -1.0, sin, ALU.mult, ALU.mult)
                dve.tensor_tensor(t2[:, :, 1:D1:2], q[:, :, 0:D1:2], sin, ALU.mult).then_inc(s_rq, 1)

            def rope_k(t, first):
                k = banks[2][:, 0:KV1].rearrange("p (h d) -> p h d", h=G1)
                t1, t2 = (v.rearrange("p (h d) -> p h d", h=G1) for v in (t1k, t2k))
                dve.wait_ge(s_kv, t + 1)
                if not first:
                    dve.wait_ge(s_kl, t)
                dve.tensor_tensor(t1, k, bcast(rope1[:, 0:D1], 1, G1), ALU.mult)
                sin = bcast(rope1[:, D1:D1 + 8], 1, G1)
                dve.scalar_tensor_tensor(t2[:, :, 0:D1:2], k[:, :, 1:D1:2], -1.0, sin, ALU.mult, ALU.mult)
                dve.tensor_tensor(t2[:, :, 1:D1:2], k[:, :, 0:D1:2], sin, ALU.mult).then_inc(s_rk, 1)

            def p_low(v, u):
                dve.wait_ge(s_ph, 4 * v + u + 1)
                js = slice(2 * (u // 2), 2 * (u // 2) + 2)
                low(pT1[1][:, :, js, u % 2, :], banks[3 + u % 2][:].rearrange("p (b j n) -> p b j n", b=2, j=2),
                    pT1[0][:, :, js, u % 2, :], s_pl)

            def q_low(t):
                dve.wait_ge(s_qh, t + 1)
                sq = stack_q.rearrange("p h (a b d) -> p h a b d", a=2, b=2)
                low(sq[:, :, 1], bcast(t1q.rearrange("p (h d) -> p h d", h=H1), 2, 2), sq[:, :, 0], s_ql)

            def at_low(v):
                dve.wait_ge(s_ah, v + 1)
                low(at1[1], banks[7][:].rearrange("p (b a q) -> p a b q", b=2, a=4), at1[0], s_al)

            def residual(v):
                return res[:, bass.ds(v, 1), :].rearrange("p t n -> p (t n)")

            def add1(v):
                dve.wait_ge(s_wo, v + 1)
                dve.tensor_tensor(residual(v), banks[0][:], residual(v), ALU.add).then_inc(s_res, 1)

            def stats1(w):
                dve.wait_ge(s_res, w + 1)
                hold()
                dve.bn_stats(st6, residual(w)).then_inc(s_ln, 1)

            def moments1(w):
                dve.wait_ge(s_ln, 3 * w + 1)
                hold()
                dve.bn_aggr(mv, st6).then_inc(s_ln, 1)
                dve.wait_ge(s_ln, 3 * w + 2)
                dve.tensor_scalar(mv[:, 1:2], mv[:, 1:2], EPS, None, ALU.add).then_inc(s_ln, 1)

            def norm1(w):
                dve.wait_ge(s_lp, w + 1)
                dve.tensor_scalar(x1n, residual(w), mv[:, 0:1], rstd, ALU.subtract, ALU.mult).then_inc(s_x1n, 1)

            def x1_low(w, bank=banks[2]):
                dve.wait_ge(s_x1h, w + 1)
                low(xT[1][:, :, bass.ds(w * P, P)], bank[:].rearrange("p (c n) -> p c n", c=EC),
                    xT[0][:, :, bass.ds(w * P, P)], s_x1l)

            def masked_max(v, u, first):
                dve.wait_ge(s_s, 4 * v + u + 1)
                if u >= 2 or not first:
                    dve.wait_ge(s_sub, 4 * v + u - 1)
                sc = cut(sc1[u % 2], b=8, k=S)
                hold()
                dve.copy_predicated(sc, bcast(causal[:], 1, 8), cut(banks[5 + u % 2][:], b=8, k=S)).then_inc(s_cp, 1)
                dve.wait_ge(s_cp, 4 * v + u + 1)
                dve.tensor_reduce(mx1[u], sc, AX.X, ALU.max).then_inc(s_mx, 1)

            def total(v, u):
                dve.wait_ge(s_ex, 4 * v + u + 1)
                dve.tensor_reduce(sm1[u], cut(p1[u], b=8, k=S), AX.X, ALU.add).then_inc(s_sum, 1)
                dve.wait_ge(s_sum, 4 * v + u + 1)
                dve.reciprocal(sm1[u], sm1[u]).then_inc(s_rc, 1)

            def tile_steps(i):
                following, old, oldest = tile_stages(i)
                v, w = i - 1, i - 2
                if old:
                    total(v, 2)
                rope_q(i, not old)
                if old:
                    total(v, 3)
                    p_low(v, 0)
                    p_low(v, 1)
                rope_k(i, not old)
                if not old:
                    for h in range(HG):
                        dve.wait_ge(s_w1oh, h + 1)
                        low(w1out[1][:, h, :], w1out_raw[:, h, :], w1out[0][:, h, :], s_w1ol)
                if oldest:
                    add1(w)
                q_low(i)
                if old:
                    p_low(v, 2)
                    p_low(v, 3)
                if oldest:
                    stats1(w)
                if following:
                    x_low(i + 1)
                if oldest:
                    moments1(w)
                masked_max(i, 0, not old)
                if oldest:
                    norm1(w)
                masked_max(i, 1, not old)
                if not following:
                    w2q_low(2)
                if old:
                    at_low(v)
                total(i, 0)
                masked_max(i, 2, not old)
                total(i, 1)
                if oldest:
                    x1_low(w)
                if not following:
                    w2q_low(3)
                    add1(v)
                masked_max(i, 3, not old)

            x_low(0)
            for c in range(EC):
                dve.wait_ge(s_w1h, c + 1)
                low(w1[1][:, c, 0:E], w1_raw[:, c, 0:E], w1[0][:, c, 0:E], s_w1l)
            dve.wait_ge(s_w1h, EC + 1)
            low(w1[1][:, :, E:], w1_raw[:, :, E:], w1[0][:, :, E:], s_w1l)
            dve.wait_ge(d_const, 32)
            dve.wait_ge(s_dinit, 5)
            dve.wait_ge(s_init, 3)
            def ctx_low(t):
                dve.wait_ge(c_xh, t + 1)
                low(cT[1][:, :, t * P:(t + 1) * P], ctx_bank(t)[:].rearrange("p (c n) -> p c n", c=EC),
                    cT[0][:, :, t * P:(t + 1) * P], c_xl)

            def rope2_q(u, c, i, first):
                dve.wait_ge(c_q, 2 * u + i + 1)
                if not first:
                    dve.wait_ge(c_tr, 3 * u + i - 2)
                q = banks[i][:].rearrange("p (h f d) -> p h f d", h=HG, f=2)
                t1, t2 = (w[i].rearrange("p (h f d) -> p h f d", h=HG, f=2) for w in (u1q, u2q))
                cos = bcast(bcast(cs[:, 2 * c + i, 0:64], 1, 2), 1, HG)
                sin = bcast(cs[:, 2 * c + i, 64:128], 1, HG)
                dve.tensor_tensor(t1, q, cos, ALU.mult)
                dve.scalar_tensor_tensor(t2[:, :, 0, :], q[:, :, 1, :], -1.0, sin, ALU.mult, ALU.mult)
                dve.tensor_tensor(t2[:, :, 1, :], q[:, :, 0, :], sin, ALU.mult).then_inc(c_rq, 1)

            def rope2_k(u, c, first):
                dve.wait_ge(c_kv, u + 1)
                if not first:
                    dve.wait_ge(c_tr, 3 * u)
                k = banks[2][:].rearrange("p (i n) -> p i n", i=2)[:, :, 0:D2].rearrange("p i (f d) -> p i f d", f=2)
                t1, t2 = (w.rearrange("p (i f d) -> p i f d", i=2, f=2) for w in (u1k, u2k))
                cos = bcast(cs[:, 2 * c:2 * c + 2, 0:64], 2, 2)
                sin = cs[:, 2 * c:2 * c + 2, 64:128]
                dve.tensor_tensor(t1, k, cos, ALU.mult)
                dve.scalar_tensor_tensor(t2[:, :, 0, :], k[:, :, 1, :], -1.0, sin, ALU.mult, ALU.mult)
                dve.tensor_tensor(t2[:, :, 1, :], k[:, :, 0, :], sin, ALU.mult).then_inc(c_rk, 1)

            def turn_low(u, n):
                dve.wait_ge(c_trh, 3 * u + n + 1)
                if n < 2:
                    high, lo_ = (w[:, 2 * n:2 * n + 2].rearrange("p b h q -> p h b q") for w in qT2)
                    low(lo_, cut(banks[4 - n][:], h=HG, b=2, q=S), high, c_trl)
                else:
                    low(kT2[1], banks[4][:, 0:2 * P], kT2[0], c_trl)

            def add_out(v, c, i):
                dve.wait_ge(c_wo, 2 * v + i + 1)
                y = res[:, 2 * c + i, :]
                dve.tensor_tensor(y, banks[6 + i][:], y, ALU.add).then_inc(c_acc, 1)

            def accumulate(v, c, i):
                add_out(v, c, i)
                if isinstance(v, int) and v >= U - UN:
                    dve.wait_ge(c_acc, 2 * v + i + 1)
                    stats(2 * c + i, 2 * c + i)

            def stats(t, n):
                bn_tile(t, n)
                aggregate(t, n)

            def bn_tile(t, n):
                if n >= T:
                    dve.wait_ge(f_r, t + 1)
                hold()
                dve.bn_stats(st6b, res[:, t, :]).then_inc(f_st, 1)

            def aggregate(t, n):
                dve.wait_ge(f_st, 2 * n + 1)
                hold()
                dve.bn_aggr(mv8[:, 2 * t:2 * t + 2], st6b).then_inc(f_st, 1)
                dve.wait_ge(f_st, 2 * n + 2)
                dve.tensor_scalar(var8[:, t:t + 1], mv8[:, 2 * t + 1:2 * t + 2], EPS, None, ALU.add).then_inc(f_var, 1)

            def masked_max2(v, c):
                sc = sc2[c].rearrange("p (h n) -> p h n", h=2)
                dve.wait_ge(c_s, v + 1)
                hold()
                dve.copy_predicated(sc, bcast(mask_i[:, c * 4 * S:(c + 1) * 4 * S], 1, 2),
                                    banks[5][:].rearrange("p (h n) -> p h n", h=2)).then_inc(c_cp, 1)
                dve.wait_ge(c_cp, v + 1)
                dve.tensor_reduce(mx2, cut(sc2[c], b=8, k=S), AX.X, ALU.max).then_inc(c_mx, 1)

            def total2(v):
                dve.wait_ge(c_ex, v + 1)
                dve.tensor_reduce(sm2, cut(p2, b=8, k=S), AX.X, ALU.add).then_inc(c_sum, 1)
                dve.wait_ge(c_sum, v + 1)
                dve.reciprocal(sm2, sm2).then_inc(c_rc, 1)

            def p2_low(v):
                dve.wait_ge(c_ph, v + 1)
                low(pT2[1], banks[3][:].rearrange("p (i n) -> p i n", i=2), pT2[0], c_pl)

            def at2_low(v):
                for s in range(2):
                    dve.wait_ge(c_ah, 2 * v + s + 1)
                    at = [w.rearrange("p h (i s q) -> p s i h q", i=2, s=2)[:, s] for w in at2]
                    low(at[1], banks[6 + s][:].rearrange("p (i h q) -> p i h q", i=2, h=HG), at[0], c_al)

            def slot(u, g, c):
                oldest = stages(u)
                v = u - 1
                cv = (c - 1) % UN
                if not (isinstance(u, int) and u == 1):
                    masked_max2(v, cv)
                if oldest:
                    accumulate(u - 2, (c - 2) % UN, 1)
                turn = isinstance(u, int) and u < UN
                if turn and u > 1:
                    ctx_low(2 * c)
                total2(v)
                if not (isinstance(u, int) and u == 1):
                    rope2_q(u, c, 0, False)
                if turn:
                    ctx_low(2 * c + 1)
                rope2_q(u, c, 1, False)
                p2_low(v)
                turn_low(u, 0)
                at2_low(v)
                rope2_k(u, c, False)
                turn_low(u, 1)
                values_low(u, c)
                turn_low(u, 2)
                accumulate(v, cv, 0)

            def values_low(u, c):
                dve.wait_ge(c_vh, u + 1)
                low(v2[c % 2][1], banks[2][:].rearrange("p (i n) -> p i n", i=2)[:, :, D2:2 * D2], v2[c % 2][0], c_vl)

            def w2q_low(c):
                dve.wait_ge(c_wqh, c + 1)
                low(w2q_s[1][:, c, :], w2q_raw[:, c, :], w2q_s[0][:, c, :], c_wql)

            tile_steps(0)
            dve.wait_ge(d_res, 16)
            tile_steps(1)
            with dve.Fori(2, T - 1) as t:
                tile_steps(t)
            tile_steps(T - 1)

            v = T - 1
            dve.wait_ge(d_cs, 16 * T)
            total(v, 2)
            p_low(v, 0)
            total(v, 3)
            p_low(v, 1)
            dve.wait_ge(s_kl, T)
            dve.wait_ge(s_vl, T)
            rope2_q(0, 0, 0, True)
            p_low(v, 2)
            p_low(v, 3)
            rope2_q(0, 0, 1, True)
            stats1(v - 1)
            moments1(v - 1)
            at_low(v)
            ctx_low(0)
            ctx_low(1)
            norm1(v - 1)
            turn_low(0, 0)
            turn_low(0, 1)
            add1(v)
            stats1(v)
            rope2_k(0, 0, True)
            moments1(v)
            values_low(0, 0)
            x1_low(v - 1, banks[7])
            turn_low(0, 2)
            norm1(v)

            dve.wait_ge(d_mask, 32)
            dve.wait_ge(c_init, UN)
            rope2_q(1, 1, 0, False)
            masked_max2(0, 0)
            ctx_low(2)
            x1_low(v, banks[7])
            for u in range(1, UN + 1):
                slot(u, u // UN, u % UN)
            with dve.Fori(1, G2 - 1) as g:
                for c in range(1, UN + 1):
                    slot(UN * g + c, g + c // UN, c % UN)
            for u in range(U - UN + 1, U):
                slot(u, u // UN, u % UN)

            def norm_tile(t):
                dve.wait_ge(f_pow, t + 1)
                dve.tensor_scalar(res[:, t, :], res[:, t, :], mv8[:, 2 * t:2 * t + 1], rstd8[:, t:t + 1],
                                  ALU.subtract, ALU.mult).then_inc(f_xn, 1)

            def fw_low(c):
                dve.wait_ge(f_wh, c + 1)
                low(fwT[1][:, c, :], banks[(0, 1, 2, 4)[c]][:], fwT[0][:, c, :], f_wl)

            def x3_low(t):
                dve.wait_ge(f_xh, t + 1)
                at = slice(t * P, (t + 1) * P)
                low(xT[1][:, :, at], banks[1 + t % 2][:].rearrange("p (c n) -> p c n", c=EC), xT[0][:, :, at], f_xl)

            v, c = U - 1, UN - 1
            norm_tile(0)
            norm_tile(1)
            masked_max2(v, c)
            add_out(v - 1, c - 1, 1)
            total2(v)
            fw_low(0)
            fw_low(1)
            fw_low(2)
            norm_tile(2)
            p2_low(v)
            fw_low(3)
            dve.wait_ge(c_acc, 2 * v)
            stats(2 * c - 1, 2 * c - 1)
            at2_low(v)
            norm_tile(3)
            dve.wait_ge(f_wh, EC + 1)
            low(fcT[1], banks[0][:, 0:EC * NC].rearrange("p (c n) -> p c n", c=EC), fcT[0], f_wl)
            x3_low(0)
            x3_low(1)
            norm_tile(4)
            norm_tile(5)
            accumulate(v, c, 0)
            x3_low(2)
            norm_tile(6)
            accumulate(v, c, 1)
            x3_low(3)

            n = 0

            def step(ins):
                nonlocal n
                n += 1
                ins.then_inc(f_v, 1)
                dve.wait_ge(f_v, n)

            dve.wait_ge(f_g, 1)
            dve.wait_ge(d_fc, 48)
            dve.wait_ge(c_wol, 4 * G2)
            norm_tile(7)
            step(dve.tensor_copy(assign_f, assign_i))
            x3_low(4)
            step(dve.tensor_copy(cid, pos_i[0:NC, 0:1]))
            x3_low(5)
            step(dve.tensor_scalar(onehot, assign_f, cid, None, ALU.is_equal))
            x3_low(6)
            x3_low(7)

            d3 = cut(dots, t=T, k=NC)
            dve.wait_ge(f_dots, 2)
            step(dve.tensor_reduce(qsel, cut(banks[5][:], t=T, k=NC), AX.X, ALU.max))
            step(dve.tensor_tensor(d3, cut(banks[5][:], t=T, k=NC), bcast(qsel, 2, NC), ALU.subtract))
            dve.wait_ge(f_ex, 1)
            step(dve.tensor_reduce(tot8, d3, AX.X, ALU.add))
            step(dve.reciprocal(tot8, tot8))
            step(dve.tensor_tensor(d3, d3, bcast(tot8, 2, NC), ALU.mult))
            step(dve.tensor_scalar(hits, dots, THRESHOLD, None, ALU.is_gt))
            dve.tensor_reduce(any_hit, hits.rearrange("p (t k) -> p k t", t=T), AX.X, ALU.max).then_inc(f_hit, 1)
            step(dve.tensor_reduce(qsel, cut(hits, t=T, k=NC), AX.X, ALU.max))
            DB = (banks[3], banks[4], banks[6], banks[7], banks[1], banks[2])

            def biased(t):
                dve.wait_ge(f_dense, t + 1)
                dve.tensor_tensor(masked[t % 2], DB[t % len(DB)][:], bias_b, ALU.add).then_inc(f_dn, 1)

            def finish(t):
                dve.wait_ge(f_pow, T + t + 1)
                dve.tensor_scalar(nmean[:, t:t + 1], mv8[:, 2 * t:2 * t + 1], rstd8[:, t:t + 1], -1.0,
                                  ALU.mult, ALU.mult).then_inc(f_nm, 1)

            dve.wait_ge(f_cnt, 1)
            dve.tensor_scalar(cluster_hit[0:NC, :], banks[0][0:NC, 0:P], 0.5, None, ALU.is_gt).then_inc(f_rs, 1)
            biased(0)
            dve.wait_ge(f_cnt, 2)
            dve.tensor_copy(row_sel, banks[0][:]).then_inc(f_sel, 1)
            for t in range(T):
                if t + 1 < T:
                    if t >= 1:
                        dve.wait_ge(f_r, t)
                    biased(t + 1)
                if t >= 1:
                    bn_tile(t - 1, T + t - 1)
                dve.wait_ge(f_m, t + 1)
                dve.scalar_tensor_tensor(res[:, t, :], masked[t % 2], qsel[:, t:t + 1], res[:, t, :],
                                         ALU.mult, ALU.add).then_inc(f_r, 1)
                if t >= 1:
                    aggregate(t - 1, T + t - 1)
                if t >= 2:
                    finish(t - 2)
            bn_tile(T - 1, 2 * T - 1)
            finish(T - 2)
            aggregate(T - 1, 2 * T - 1)
            finish(T - 1)


_INS = ["x", "ctx_4096", "pos_BxS2", "mask_BxSxS2_ik0", "L0_attn_Wq", "L0_attn_Wk", "L0_attn_Wv", "L0_attn_Wo",
        "L0_xattn_Wq", "L0_xattn_Wk", "L0_xattn_Wv", "L0_xattn_Wo",
        "L0_ffn_weight", "L0_ffn_bias", "L0_ffn_centroids", "L0_ffn_assignments"]


def _constants():
    import numpy as np

    q, k = np.arange(P)[:, None] % S, np.arange(S)[None, :]
    inv1 = np.float32(1.0) / np.float32(10000.0) ** (np.arange(0, D1, 2, dtype=np.float32) / np.float32(D1))
    ang1 = (np.arange(P) % S).astype(np.float32)[:, None] * inv1[None, :]
    inv2 = np.float32(1.0) / np.float32(10000.0) ** (np.arange(0, D2, 2, dtype=np.float32) / np.float32(D2))
    ang2 = np.arange(512, dtype=np.float32)[:, None] * inv2[None, :]
    return {
        "c_ident": np.eye(P, dtype=np.float32),
        "c_causal": (q >= k).astype(np.int32),
        "c_rope1": np.concatenate([np.repeat(np.cos(ang1), 2, 1), np.sin(ang1)], 1).astype(np.float32),
        "c_rope2": np.concatenate([np.cos(ang2), np.sin(ang2)], 1).astype(np.float32),
    }


def kernel(**inputs):
    import numpy as _np
    import concourse.bacc as _bacc
    from concourse import mybir as _mybir
    from concourse.bass_utils import run_bass_kernel_spmd as _run

    nc = _bacc.Bacc("TRN2", target_bir_lowering=False, num_devices=1)
    arrays, args = {}, []
    flat = {"x": (B * S, E), "ctx_4096": (B * S, E)}
    for name in _INS:
        a = _np.ascontiguousarray(inputs[name])
        if name in flat:
            a = a.reshape(flat[name])
        if name == "pos_BxS2":
            a = _np.ascontiguousarray(a.reshape(T, P).T)
        arrays[f"in_{name}"] = a
    for name, a in _constants().items():
        arrays[f"in_{name}"] = a
    for name, a in arrays.items():
        args.append(nc.dram_tensor(name, a.shape, _mybir.dt.from_np(a.dtype), kind="ExternalInput").ap())
    out = nc.dram_tensor("out_0", (B * S, E), F32, kind="ExternalOutput").ap()
    decoder_layer(nc, *args, out)
    r = _run(nc, [arrays], core_ids=[0])
    return r.results[0]["out_0"].reshape(B, S, E)
```
